# Optimizing a Trainium2 kernel written in Bass

```python
import numpy as np
import jax
import jax.numpy as jnp

def _softmax(x, axis=-1):
    return jax.nn.softmax(x, axis=axis)

def _gelu(x):
    return jax.nn.gelu(x, approximate=True)

def _silu(x):
    return jax.nn.silu(x)

def _sigmoid(x):
    return jax.nn.sigmoid(x)

def _layernorm(x, axis=-1, eps=1e-05):
    m = jnp.mean(x, axis=axis, keepdims=True)
    v = jnp.var(x, axis=axis, keepdims=True)
    return (x - m) / jnp.sqrt(v + eps)

def _scatter_add(tgt, idx, src, axis=0):
    return tgt.at[idx].add(src)

def _segment_sum(src, seg, n):
    return jax.ops.segment_sum(src, seg, n)
kernel_name = 'mk_seq_postln_d2_jaxref_r8_bdb617'

def setup_inputs(seed: int=0):
    np.random.seed(seed)
    _w = jnp.asarray

    def _L0_attn_setup():
        import jax, jax.numpy as jnp
        import numpy as np
        B_SZ, L, D_MODEL = (2, 256, 128)
        EXPAND, N_STATE, K = (2, 16, 4)
        D_INNER = D_MODEL * EXPAND

        def _layernorm(x, g, b, eps=1e-05):
            mu = jnp.mean(x, axis=-1, keepdims=True)
            var = jnp.var(x, axis=-1, keepdims=True)
            return (x - mu) * jax.lax.rsqrt(var + eps) * g + b

        def _selective_scan(x, delta, A, B_mat, C_mat, D_vec):
            dA = jnp.exp(delta[..., None] * A)
            Bx = jnp.einsum('bld,nd->bln', x, B_mat) * delta[..., None]

            def step(h, inp):
                dA_t, Bx_t = inp
                h = dA_t * h + Bx_t
                return (h, h)
            h0 = jnp.zeros((x.shape[0], A.shape[0]), x.dtype)
            _, hs = jax.lax.scan(step, h0, (jnp.swapaxes(dA, 0, 1), jnp.swapaxes(Bx, 0, 1)))
            hs = jnp.swapaxes(hs, 0, 1)
            return jnp.einsum('bln,dn->bld', hs, C_mat) + D_vec * x
        key = jax.random.key(seed)
        ks = jax.random.split(key, 12)
        s = lambda k, shape, scale=0.02: jax.random.normal(k, shape, jnp.float32) * scale
        return {'x': jax.random.normal(ks[0], (B_SZ, L, D_MODEL), jnp.float32), 'ln_gamma': jnp.ones((D_MODEL,), jnp.float32), 'ln_beta': jnp.zeros((D_MODEL,), jnp.float32), 'W_in': s(ks[1], (D_MODEL, 2 * D_INNER)), 'conv_w': s(ks[2], (D_INNER, 1, K), 0.1), 'conv_b': jnp.zeros((D_INNER,), jnp.float32), 'A_log': jax.random.normal(ks[3], (N_STATE,), jnp.float32), 'B_mat': s(ks[4], (N_STATE, D_INNER), 0.05), 'C_mat': s(ks[5], (D_INNER, N_STATE), 0.05), 'D_vec': s(ks[6], (D_INNER,), 0.1), 'Wd': s(ks[7], (D_INNER, D_INNER)), 'bd': jnp.zeros((D_INNER,), jnp.float32), 'W_out': s(ks[8], (D_INNER, D_MODEL))}
    _L0_attn_in = _L0_attn_setup()

    def _L0_ffn_setup():
        import jax, jax.numpy as jnp
        import numpy as np
        B, S, H, E = (4, 256, 128, 8)
        key = jax.random.key(seed)
        k1, k2, k3 = jax.random.split(key, 3)
        scale_w = 1.0 / np.sqrt(H)
        return {'x': jax.random.normal(k1, (B, S, H), dtype=jnp.float32), 'router_w': jax.random.normal(k2, (H, E), dtype=jnp.float32) * scale_w, 'router_b': jnp.zeros((E,), dtype=jnp.float32), 'expert_w': jax.random.normal(k3, (E, H, H), dtype=jnp.float32) * scale_w, 'expert_b': jnp.zeros((E, H), dtype=jnp.float32)}
    _L0_ffn_in = _L0_ffn_setup()

    def _L1_attn_setup():
        import jax, jax.numpy as jnp
        import numpy as np
        B, T, E, H = (2, 256, 128, 16)
        HD = E // H

        def _xavier(key, shape):
            limit = float(np.sqrt(6.0 / (shape[0] + shape[1])))
            return jax.random.uniform(key, shape, dtype=jnp.float32, minval=-limit, maxval=limit)
        key = jax.random.key(seed)
        kx, kq, kk, kv = jax.random.split(key, 4)
        return {'x': jax.random.normal(kx, (B, T, E), dtype=jnp.float32), 'w_Q': _xavier(kq, (E, E)), 'w_K': _xavier(kk, (E, E)), 'w_V': _xavier(kv, (E, E))}
    _L1_attn_in = _L1_attn_setup()

    def _L1_ffn_setup():
        import jax, jax.numpy as jnp
        import numpy as np
        NUM_NOD = 6
        MAX_PREV = 5
        NUM_EDGE = 20
        D = 128
        H = 8
        LN_EPS = 1e-06

        def _layernorm(x, g, b):
            mu = jnp.mean(x, axis=-1, keepdims=True)
            var = jnp.mean(jnp.square(x - mu), axis=-1, keepdims=True)
            return (x - mu) * jax.lax.rsqrt(var + LN_EPS) * g + b

        def _mha(q, k, v, wq, wk, wv, wo):
            B, S, d = q.shape
            dh = d // H
            qh = (q @ wq).reshape(B, S, H, dh)
            kh = (k @ wk).reshape(B, S, H, dh)
            vh = (v @ wv).reshape(B, S, H, dh)
            scores = jnp.einsum('bqhd,bkhd->bhqk', qh, kh) / jnp.sqrt(jnp.asarray(dh, q.dtype))
            attn = jax.nn.softmax(scores, axis=-1)
            ctx = jnp.einsum('bhqk,bkhd->bqhd', attn, vh).reshape(B, S, d)
            return ctx @ wo
        key = jax.random.key(seed)
        ks = jax.random.split(key, 12)
        B, S = (8, 128)
        scale = 1.0 / np.sqrt(D)
        return {'inputs': jax.random.normal(ks[0], (B, S, D), jnp.float32), 'ew': jax.random.uniform(ks[1], (NUM_NOD, 3), jnp.float32), 'act_w': jax.random.uniform(ks[2], (NUM_NOD,), jnp.float32), 'We': jax.random.normal(ks[3], (NUM_EDGE, D, D), jnp.float32) * scale, 'be': jnp.zeros((NUM_EDGE, D), jnp.float32), 'Wq': jax.random.normal(ks[4], (NUM_NOD, D, D), jnp.float32) * scale, 'Wk': jax.random.normal(ks[5], (NUM_NOD, D, D), jnp.float32) * scale, 'Wv': jax.random.normal(ks[6], (NUM_NOD, D, D), jnp.float32) * scale, 'Wo': jax.random.normal(ks[7], (NUM_NOD, D, D), jnp.float32) * scale, 'ln_g': jnp.ones((D,), jnp.float32), 'ln_b': jnp.zeros((D,), jnp.float32)}
    _L1_ffn_in = _L1_ffn_setup()
    _d = {'L0_attn_x': _L0_attn_in['x'], 'L0_attn_ln_gamma': _L0_attn_in['ln_gamma'], 'L0_attn_ln_beta': _L0_attn_in['ln_beta'], 'L0_attn_W_in': _L0_attn_in['W_in'], 'L0_attn_conv_w': _L0_attn_in['conv_w'], 'L0_attn_conv_b': _L0_attn_in['conv_b'], 'L0_attn_A_log': _L0_attn_in['A_log'], 'L0_attn_B_mat': _L0_attn_in['B_mat'], 'L0_attn_C_mat': _L0_attn_in['C_mat'], 'L0_attn_D_vec': _L0_attn_in['D_vec'], 'L0_attn_Wd': _L0_attn_in['Wd'], 'L0_attn_bd': _L0_attn_in['bd'], 'L0_attn_W_out': _L0_attn_in['W_out'], 'L0_ffn_router_w': _L0_ffn_in['router_w'], 'L0_ffn_router_b': _L0_ffn_in['router_b'], 'L0_ffn_expert_w': _L0_ffn_in['expert_w'], 'L0_ffn_expert_b': _L0_ffn_in['expert_b'], 'L1_attn_w_Q': _L1_attn_in['w_Q'], 'L1_attn_w_K': _L1_attn_in['w_K'], 'L1_attn_w_V': _L1_attn_in['w_V'], 'L1_ffn_ew': _L1_ffn_in['ew'], 'L1_ffn_act_w': _L1_ffn_in['act_w'], 'L1_ffn_We': _L1_ffn_in['We'], 'L1_ffn_be': _L1_ffn_in['be'], 'L1_ffn_Wq': _L1_ffn_in['Wq'], 'L1_ffn_Wk': _L1_ffn_in['Wk'], 'L1_ffn_Wv': _L1_ffn_in['Wv'], 'L1_ffn_Wo': _L1_ffn_in['Wo'], 'L1_ffn_ln_g': _L1_ffn_in['ln_g'], 'L1_ffn_ln_b': _L1_ffn_in['ln_b']}
    _x0 = _d['L0_attn_x']
    _d['L0_attn_x'] = jax.random.normal(jax.random.fold_in(jax.random.key(seed), 1), (8, 512, 128), dtype=_x0.dtype)
    del _x0
    return _d

def reference(L0_attn_x, L0_attn_ln_gamma, L0_attn_ln_beta, L0_attn_W_in, L0_attn_conv_w, L0_attn_conv_b, L0_attn_A_log, L0_attn_B_mat, L0_attn_C_mat, L0_attn_D_vec, L0_attn_Wd, L0_attn_bd, L0_attn_W_out, L0_ffn_router_w, L0_ffn_router_b, L0_ffn_expert_w, L0_ffn_expert_b, L1_attn_w_Q, L1_attn_w_K, L1_attn_w_V, L1_ffn_ew, L1_ffn_act_w, L1_ffn_We, L1_ffn_be, L1_ffn_Wq, L1_ffn_Wk, L1_ffn_Wv, L1_ffn_Wo, L1_ffn_ln_g, L1_ffn_ln_b):

    def _L0_attn_ref(x, ln_gamma, ln_beta, W_in, conv_w, conv_b, A_log, B_mat, C_mat, D_vec, Wd, bd, W_out):
        import jax, jax.numpy as jnp
        import numpy as np
        B_SZ, L, D_MODEL = (2, 256, 128)
        EXPAND, N_STATE, K = (2, 16, 4)
        D_INNER = D_MODEL * EXPAND

        def _layernorm(x, g, b, eps=1e-05):
            mu = jnp.mean(x, axis=-1, keepdims=True)
            var = jnp.var(x, axis=-1, keepdims=True)
            return (x - mu) * jax.lax.rsqrt(var + eps) * g + b

        def _selective_scan(x, delta, A, B_mat, C_mat, D_vec):
            dA = jnp.exp(delta[..., None] * A)
            Bx = jnp.einsum('bld,nd->bln', x, B_mat) * delta[..., None]

            def step(h, inp):
                dA_t, Bx_t = inp
                h = dA_t * h + Bx_t
                return (h, h)
            h0 = jnp.zeros((x.shape[0], A.shape[0]), x.dtype)
            _, hs = jax.lax.scan(step, h0, (jnp.swapaxes(dA, 0, 1), jnp.swapaxes(Bx, 0, 1)))
            hs = jnp.swapaxes(hs, 0, 1)
            return jnp.einsum('bln,dn->bld', hs, C_mat) + D_vec * x
        residual = x
        h = _layernorm(x, ln_gamma, ln_beta)
        xg = h @ W_in
        xs, gate = jnp.split(xg, 2, axis=-1)
        xc = jnp.swapaxes(xs, 1, 2)
        xc = jax.lax.conv_general_dilated(xc, conv_w, window_strides=(1,), padding=((K - 1, 0),), dimension_numbers=('NCH', 'OIH', 'NCH'), feature_group_count=D_INNER)
        xc = xc + conv_b[None, :, None]
        xs = jnp.swapaxes(xc, 1, 2)
        xs = jax.nn.silu(xs)
        delta = jnp.mean(jax.nn.softplus(xs @ Wd + bd), axis=-1)
        A = -jnp.exp(A_log)
        y = _selective_scan(xs, delta, A, B_mat, C_mat, D_vec)
        y = y * jax.nn.silu(gate)
        y = y @ W_out
        return residual + y

    def _L0_ffn_ref(x, router_w, router_b, expert_w, expert_b):
        import jax, jax.numpy as jnp
        import numpy as np
        B, S, H, E = (4, 256, 128, 8)
        b, s, h = x.shape
        xt = x.reshape(b * s, h)
        logits = xt @ router_w + router_b
        probs = jax.nn.softmax(logits, axis=-1)
        gate = jnp.max(probs, axis=-1)
        idx = jnp.argmax(probs, axis=-1)
        out_all = jnp.einsum('th,ehd->ted', xt, expert_w) + expert_b[None, :, :]
        e_out = jnp.take_along_axis(out_all, idx[:, None, None], axis=1)[:, 0, :]
        y = gate[:, None] * e_out
        return y.reshape(b, s, h)

    def _L1_attn_ref(x, w_Q, w_K, w_V):
        import jax, jax.numpy as jnp
        import numpy as np
        B, T, E, H = (2, 256, 128, 16)
        HD = E // H

        def _xavier(key, shape):
            limit = float(np.sqrt(6.0 / (shape[0] + shape[1])))
            return jax.random.uniform(key, shape, dtype=jnp.float32, minval=-limit, maxval=limit)
        Bs, Ts, Es = x.shape
        q = (x @ w_Q).reshape(Bs, Ts, H, HD).transpose(0, 2, 1, 3)
        k = (x @ w_K).reshape(Bs, Ts, H, HD).transpose(0, 2, 1, 3)
        v = (x @ w_V).reshape(Bs, Ts, H, HD).transpose(0, 2, 1, 3)
        scores = jnp.einsum('bhtd,bhsd->bhts', q, k) / jnp.sqrt(jnp.asarray(HD, x.dtype))
        probs = jax.nn.softmax(scores, axis=-1)
        attn = jnp.einsum('bhts,bhsd->bhtd', probs, v)
        return attn.transpose(0, 2, 1, 3).reshape(Bs, Ts, H * HD)

    def _L1_ffn_ref(inputs, ew, act_w, We, be, Wq, Wk, Wv, Wo, ln_g, ln_b):
        import jax, jax.numpy as jnp
        import numpy as np
        NUM_NOD = 6
        MAX_PREV = 5
        NUM_EDGE = 20
        D = 128
        H = 8
        LN_EPS = 1e-06

        def _layernorm(x, g, b):
            mu = jnp.mean(x, axis=-1, keepdims=True)
            var = jnp.mean(jnp.square(x - mu), axis=-1, keepdims=True)
            return (x - mu) * jax.lax.rsqrt(var + LN_EPS) * g + b

        def _mha(q, k, v, wq, wk, wv, wo):
            B, S, d = q.shape
            dh = d // H
            qh = (q @ wq).reshape(B, S, H, dh)
            kh = (k @ wk).reshape(B, S, H, dh)
            vh = (v @ wv).reshape(B, S, H, dh)
            scores = jnp.einsum('bqhd,bkhd->bhqk', qh, kh) / jnp.sqrt(jnp.asarray(dh, q.dtype))
            attn = jax.nn.softmax(scores, axis=-1)
            ctx = jnp.einsum('bhqk,bkhd->bqhd', attn, vh).reshape(B, S, d)
            return ctx @ wo
        nodes = {-1: inputs}
        lind = 0
        for c in range(NUM_NOD):
            nsrc = min(c + 1, MAX_PREV)
            snode = c - nsrc
            eq, ek, ev = (lind + nsrc - 1, lind, lind + nsrc // 2)
            in_q, in_k, in_v = (c - 1, snode, snode + nsrc // 2)
            q = ew[c, 0] * (nodes[in_q] @ We[eq] + be[eq])
            k = ew[c, 1] * (nodes[in_k] @ We[ek] + be[ek])
            v = ew[c, 2] * (nodes[in_v] @ We[ev] + be[ev])
            o = _mha(q, k, v, Wq[c], Wk[c], Wv[c], Wo[c])
            nodes[c] = act_w[c] * o + q
            lind += nsrc
        out = nodes[NUM_NOD - 1]
        return _layernorm(out, ln_g, ln_b)
    x = L0_attn_x
    x = _layernorm(x + _L0_attn_ref(x, L0_attn_ln_gamma, L0_attn_ln_beta, L0_attn_W_in, L0_attn_conv_w, L0_attn_conv_b, L0_attn_A_log, L0_attn_B_mat, L0_attn_C_mat, L0_attn_D_vec, L0_attn_Wd, L0_attn_bd, L0_attn_W_out), axis=-1)
    x = _layernorm(x + _L0_ffn_ref(x, L0_ffn_router_w, L0_ffn_router_b, L0_ffn_expert_w, L0_ffn_expert_b), axis=-1)
    x = _layernorm(x + _L1_attn_ref(x, L1_attn_w_Q, L1_attn_w_K, L1_attn_w_V), axis=-1)
    x = _layernorm(x + _L1_ffn_ref(x, L1_ffn_ew, L1_ffn_act_w, L1_ffn_We, L1_ffn_be, L1_ffn_Wq, L1_ffn_Wk, L1_ffn_Wv, L1_ffn_Wo, L1_ffn_ln_g, L1_ffn_ln_b), axis=-1)
    return x

_drawn_inputs = setup_inputs


def setup_inputs(seed=0):
    import zlib

    import numpy as np

    out = dict(_drawn_inputs(seed))
    spreads = {'L0_attn_ln_gamma': (1.0, 0.6),
     'L0_attn_ln_beta': (0.0, 0.8),
     'L0_attn_conv_b': (0.0, 0.8),
     'L0_attn_bd': (0.0, 2.0),
     'L0_ffn_router_b': (0.0, 0.1),
     'L0_ffn_expert_b': (0.0, 0.291),
     'L1_ffn_be': (0.0, 0.1),
     'L1_ffn_ln_g': (1.0, 0.2),
     'L1_ffn_ln_b': (0.0, 0.1)}
    factors = {'L0_attn_W_in': 8.0,
     'L0_attn_conv_w': 8.0,
     'L0_attn_A_log': 8.0,
     'L0_attn_B_mat': 8.0,
     'L0_attn_C_mat': 8.0,
     'L0_attn_D_vec': 175.028,
     'L0_attn_Wd': 8.0,
     'L0_attn_W_out': 8.0,
     'L1_ffn_Wq': 200.0,
     'L1_ffn_Wk': 200.0}
    for name, (base, spread) in spreads.items():
        noise = np.random.default_rng([zlib.crc32(name.encode()), seed]).standard_normal(out[name].shape)
        drawn = base * np.exp(spread * noise) if base else spread * noise
        out[name] = jnp.asarray(drawn.astype(out[name].dtype))
    for name, factor in factors.items():
        out[name] = (out[name] * factor).astype(out[name].dtype)
    return out
```

```python
from contextlib import ExitStack

import concourse.bass as bass
from concourse import mybir

F32 = mybir.dt.float32
BF16 = mybir.dt.bfloat16
ACT = mybir.ActivationFunctionType
ALU = mybir.AluOpType
AX = mybir.AxisListType

P = 128
NB = 8
L = 512
D = 128
NT = L // P
DI = 256
NH = DI // P
NS = 16
KC = 4
NE = 8
NODES = 6
HU = 8
GH = 4
COL = 32
RING = 4
EPS_LN = 1e-5
EPS_NODE = 1e-6

TERMS_16 = [(0, 0), (0, 1), (0, 2), (1, 0), (1, 1), (2, 0)]
TERMS_8 = [(a, b) for a in range(3) for b in range(3)]
ROWS_TOP = 128

PK = ["WeQ", "WqP", "WeKT", "WkP", "WeVT", "Wv", "Wo"]
PKC = len(PK) * P + 3 + 4
WA = 3 * P + 2
WB = 2 * P


def need(e, sem, value):
    if isinstance(value, int) and value <= 0:
        return
    e.wait_ge(sem, value)


def build(nc, a):
    f = lambda name, shape: nc.dram_tensor(name, shape, F32).ap()
    wA_d, wB_d, wO_d = f("wA_d", (NODES, P, WA)), f("wB_d", (NODES, P, WB)), f("wO_d", (NODES, P, P))
    dB_d = f("dB_d", (NB, NS, 2, L))
    hs_d = f("hs_d", (NB, NS, L))
    x2T_d, x2_d, x3_d = f("x2T_d", (NB, P, L)), f("x2_d", (NB, P, NT * D)), f("x3_d", (NB, P, NT * D))
    nodes_d = f("nodes_d", ((NODES + 1) * NB, P, L))

    with ExitStack() as ctx:
        def sb(name, shape, dt=F32):
            return ctx.enter_context(nc.sbuf_tensor(name, shape, dt))

        def sem(name):
            return ctx.enter_context(nc.semaphore(name))

        bank_x = ctx.enter_context(nc.psum_tensor("bank_x", [P, 2, 1024], F32))
        bank_s = ctx.enter_context(nc.psum_tensor("bank_s", [P, 2, 512], F32))
        bank_o = ctx.enter_context(nc.psum_tensor("bank_o", [P, 512], F32))
        bank_m = ctx.enter_context(nc.psum_tensor("bank_m", [P, 512], F32))

        ident = sb("ident", [P, P])
        identb = sb("identb", [P, P], BF16)
        half = sb("half", [P, NT])
        eps_ln, eps_node = sb("eps_ln", [P, NT]), sb("eps_node", [P, NT])
        cv = sb("cv", [P, NH, KC + 4])
        cvh = sb("cvh", [P, NH, KC + 1])
        gb = sb("gb", [P, 2])
        alog = sb("alog", [P, 1])
        aneg = sb("aneg", [P, 2])
        w_in = sb("w_in", [P, 2 * DI])
        wd = sb("wd", [P, NH, DI])
        w_out = sb("w_out", [P, NH, D])
        woh = sb("woh", [P, NH, D])
        bmt = sb("bmt", [P, NH, NS])
        cmt = sb("cmt", [NS, DI])
        mean_w = sb("mean_w", [P, NS])
        rw = sb("rw", [P, NE])
        rb = sb("rb", [P, NE])
        rank = sb("rank", [P, NE])
        xw = sb("xw", [P, NE * D])
        xb = sb("xb", [NE, D])
        wc = sb("wc", [P, 3, P])
        lngb = sb("lngb", [P, 2, D])

        big = sb("big", [P, 30 * 1024])
        xs_all = big[:, 0:8192].rearrange("p (h n) -> p h n", h=NH)
        sg_all = big[:, 8192:16384].rearrange("p (h n) -> p h n", h=NH)
        qst = big[:, 0:8192].bitcast(BF16).rearrange("p (u h n) -> p u h n", u=RING, h=HU)
        kst = big[:, 8192:16384].bitcast(BF16).rearrange("p (u h n) -> p u h n", u=RING, h=HU)
        PT = big[:, 16384:24576].rearrange("p (k h c n) -> p k h c n", k=2, h=GH, c=2)
        wk = big[:, 16384:30720]

        at = sb("at", [P, 15 * 1024])
        o = [0]

        def cut(n):
            o[0] += n
            return at[:, o[0] - n:o[0]]

        st_qk = [cut(WA + 2 * L) for _ in range(2)]
        st_v = [cut(WB + L) for _ in range(2)]
        st_o = [cut(P) for _ in range(2)]
        q_sb = [cut(L) for _ in range(RING)]
        qf, kf = cut(L), cut(L)
        qp = cut(3 * L // 2).bitcast(BF16).rearrange("p (t n) -> p t n", t=3)
        kp_ = cut(3 * L // 2).bitcast(BF16).rearrange("p (t n) -> p t n", t=3)
        ot_sb = cut(L)
        assert o[0] <= 15 * 1024, o
        atb = big[:, 24576:30720]
        o2 = [0]

        def cut2(n):
            o2[0] += n
            return atb[:, o2[0] - n:o2[0]]

        vaug = [cut2(NT * HU * COL).rearrange("p (c h m) -> p c h m", c=NT, h=HU) for _ in range(2)]
        ctx_sb = cut2(L)
        ctxT = cut2(L)
        no_sb = cut2(L)
        x2s = cut2(L)
        x3s = cut2(L)
        nm = cut2(32).rearrange("p (g n) -> p g n", g=2)
        mr = cut2(16)
        mp = cut2(24).bitcast(BF16)
        mT = cut2(64).bitcast(BF16)
        rec = cut2(16).rearrange("p (t h) -> p t h", t=NT)
        stt = cut2(NT * 6).rearrange("p (t s) -> p t s", t=NT)
        mv = cut2(NT * 2).rearrange("p (t s) -> p t s", t=NT)
        rs = cut2(NT)
        rs0 = cut2(NT)
        assert o2[0] <= 6144, o2

        w0 = [0]

        def cutw(n):
            w0[0] += n
            assert w0[0] <= 14336
            return wk[:, w0[0] - n:w0[0]]

        xt = cutw(L).rearrange("p (t d) -> p t d", t=NT)
        hn = cutw(L)
        hT = cutw(L)
        cbuf = cutw(NH * (L + KC)).rearrange("p (h n) -> p h n", h=NH)
        tg = cutw(NH * L).rearrange("p (h n) -> p h n", h=NH)
        yh = cutw(NH * L).rearrange("p (h n) -> p h n", h=NH)
        ab = cutw(NH * L).rearrange("p (h n) -> p h n", h=NH)
        rl = cutw(NH * L).rearrange("p (h n) -> p h n", h=NH)
        dbx = cutw(2 * L)[0:NS, :].rearrange("p (t n) -> p t n", t=2)
        db = cutw(2 * L).rearrange("p (t n) -> p t n", t=2)
        hs = cutw(L)
        hsb = cutw(L)[0:NS, :]
        x2w, x2Tw, ybs = cutw(L), cutw(L), cutw(L)
        lg = cutw(NT * NE).rearrange("p (t e) -> p t e", t=NT)
        lge = cutw(NT * NE).rearrange("p (t e) -> p t e", t=NT)
        lgm = cutw(NT * NE).rearrange("p (t e) -> p t e", t=NT)
        mx = cutw(NT)
        nmx = cutw(NT)
        sm = cutw(NT)
        fm = cutw(NT)
        mgT = cutw(L)[0:NE, :]
        sta = cutw(NT * 6).rearrange("p (t s) -> p t s", t=NT)
        mva = cutw(NT * 2).rearrange("p (t s) -> p t s", t=NT)
        rsa, rsb = cutw(NT), cutw(NT)
        pk_sb = at[:, 0:PKC]
        po_sb = at[:, 1024:1024 + WA + WB + P]
        bvr = at[:, 2048:2048 + P]
        wv = {n: pk_sb[:, i * P:(i + 1) * P] for i, n in enumerate(PK)}
        vec = pk_sb[:, len(PK) * P:PKC]

        bx0, bx1 = bank_x[:, 0, :], bank_x[:, 1, :]
        sec = lambda t, h: t[:, h * 512:(h + 1) * 512]

        s_w = sem("weights_in")
        s_id = sem("identity_ready")
        s_c = sem("constants_ready")
        N_W = 17

        block = ctx.enter_context(nc.Block())
        S = {}
        credit = []

        def now(e, name, b, n=1, k=None):
            e.wait_ge(S[name], n * b + (n if k is None else k) + 1)

        def before(e, name, b, n=1):
            e.wait_ge(S[name], n * b + 1)

        def names(prefix, *ns):
            for n in ns:
                S[prefix + n] = sem(prefix + n)
                if prefix in ("p_", "a_", "b_", "f_"):
                    credit.append(S[prefix + n])

        v_link, g_link = sem("vector_link"), sem("gpsimd_link")
        credit += [v_link, g_link]
        passed = sem("wait_passed")
        names("p_", "bc", "ev", "in", "mm", "out")
        names("a_", "ab", "dB_out", "g_ev", "hT_ev", "hT_ps", "hn", "ln", "mb_ev", "mb_ps", "mv", "rs", "sp", "tg", "th", "win_ps", "x", "xs", "xs_ev", "yh", "z_ps", "z_ev")
        names("r_", "A", "bx", "dA", "hs", "in", "out")
        names("b_", "c_ps", "e_ev", "e_ps", "ex", "hs", "lg", "lg_ps", "mg", "mgT_ev", "mgT_ps", "mv", "out", "outT", "rs", "x", "x1", "x2", "x2T_ev", "x2T_ps", "xT_ev", "xT_ps", "y", "yb_ev", "yb_ps", "yo_ps")
        names("f_", "mv", "n_in", "out", "rs", "tT_ps", "x3_in", "y", "z")
        for p in ("c_", "d_"):
            names(p, "qk0", "qk1", "v0", "v1", "kh_ps", "qh_ps", "v_ps", "ot_ps", "mT_ps", "kf_ev", "qf_ev", "v_ev", "ot_ev", "mT_ev", "pv_ev", "spk", "spq", "stk0", "stk1", "stk2", "stk3", "m_dma", "s_ps", "red", "nm_ok", "st_ps", "ex", "pv_ps", "store", "link", "pool", "x2link")
        names("c_", "x3T_ps", "x3T_ev", "x2in", "x3", "x3out", "mv", "rs", "ones", "xlink", "plink")
        names("d_", "o0", "o1", "qT_ps", "wo_ps", "cT_ps", "q_ev", "wo_ev", "cT_ev")

        class Cfg:
            pass

        cc, cd = Cfg(), Cfg()
        cc.p, cc.U, cc.hd, cc.terms, cc.moe = "c_", 2 * NB, 8, TERMS_8, False
        cd.p, cd.U, cd.hd, cd.terms, cd.moe = "d_", NODES * NB, 16, TERMS_16, True
        for c in (cc, cd):
            c.R = len(c.terms) * c.hd
            c.R3 = c.R + 3
            c.np_ = HU * c.hd
            c.node = c.moe
            c.s = lambda n, c=c: S[c.p + n]
            c.scale = float(c.hd) ** -0.5

        def units(e, c, body):
            for u in range(RING):
                body(0, u)
            with e.Fori(1, c.U // RING - 1) as it:
                for r in range(RING):
                    body(it, r)
            for r in range(RING):
                body(c.U // RING - 1, r)

        def inside(c, q, r):
            return not isinstance(q, int) or 0 <= RING * q + r < c.U

        @block.sync
        def _(sp):
            for dst, src in ((cv[:, :, :], a["cv"]), (gb[:, :], a["gb"]), (alog[:, :], a["alog"]),
                             (w_in[:, :], a["w_in"]), (wd[:, :, :], a["wd"]), (w_out[:, :, :], a["w_out"]),
                             (bmt[:, :, :], a["bmt"]), (cmt[:, :], a["cmt"]), (rw[:, :], a["rw"]),
                             (rb[:, :], a["rb"]), (xw[:, :], a["xw"]), (xb[:, :], a["xb"]),
                             (wc[:, 0, :], a["wcq"]), (wc[:, 1, :], a["wck"]), (wc[:, 2, :], a["wcv"]),
                             (lngb[:, 0, :], a["lng"]), (lngb[:, 1, :], a["lnb"])):
                sp.dma_start(dst, src).then_inc(s_w, 16)

            def row(t, i):
                return t[bass.ds(i, 1)].rearrange("o p n -> (o p) n")

            def when(*waits):
                for x, v in waits:
                    need(sp, x, v)
                    if not isinstance(v, int):
                        sp.sem_inc(passed, 1)

            with sp.Fori(0, NODES) as c:
                when((S["p_ev"], c + 1))
                sp.dma_start(pk_sb, row(a["pk"], c)).then_inc(S["p_in"], 16)
                when((S["p_ev"], c + 2))
                sp.dma_start(row(wA_d, c), po_sb[:, 0:WA]).then_inc(S["p_out"], 16)
                sp.dma_start(row(wB_d, c), po_sb[:, WA:WA + WB]).then_inc(S["p_out"], 16)
                sp.dma_start(row(wO_d, c), po_sb[:, WA + WB:WA + WB + P]).then_inc(S["p_out"], 16)
            sp.wait_ge(S["p_out"], 48 * NODES + 1)

            def tokens(t, i):
                return t[bass.ds(i, 1)].rearrange("o (t p) d -> p (o t) d", p=P)

            with sp.Fori(0, NB) as b:
                when((S["a_hn"], b + 1))
                sp.dma_start(xt, tokens(a["x"], b)).then_inc(S["a_x"], 16)
                when((S["a_mb_ev"], b + 2))
                sp.dma_start(dB_d[bass.ds(b, 1)].rearrange("o n t l -> (o n) t l"), dbx).then_inc(S["a_dB_out"], 16)
            sp.wait_ge(S["a_dB_out"], 16 * NB + 1)
            sp.dma_start(db, dB_d.rearrange("b n t l -> (b n) t l")).then_inc(S["r_in"], 16)
            sp.wait_ge(S["r_hs"], 1)
            sp.dma_start(hs_d.rearrange("b n l -> (b n) l"), hs).then_inc(S["r_out"], 16)
            sp.wait_ge(S["r_out"], 16)
            with sp.Fori(0, NB) as b:
                when((S["b_mv"], 2 * b + 1), (S["b_c_ps"], b + 1))
                sp.dma_start(xt, tokens(a["x"], b)).then_inc(S["b_x"], 16)
                sp.dma_start(hsb, row(hs_d, b)).then_inc(S["b_hs"], 16)
                when((S["b_x2"], b + 2))
                sp.dma_start(row(x2_d, b), x2w).then_inc(S["b_out"], 16)
                when((S["b_x2T_ev"], b + 2))
                sp.dma_start(row(x2T_d, b), x2Tw).then_inc(S["b_outT"], 16)
            sp.wait_ge(S["b_out"], 16 * NB + 1)
            sp.wait_ge(S["b_outT"], 16 * NB + 1)
            sp.wait_ge(S["c_ones"], 3)

            for c in (cc, cd):
                s = c.s

                def index(q, r, c=c):
                    return RING * q + r

                def load_qk(q, r, c=c, s=s):
                    if not inside(c, q, r):
                        return
                    u = RING * q + r
                    t = st_qk[r % 2]
                    when((s("qh_ps"), u - 1), *[(s("store"), 16 * (u - NB + 3))] * c.node)
                    if c.node:
                        sp.dma_start(t[:, 0:WA], row(wA_d, u // NB)).then_inc(s(f"qk{r % 2}"), 16)
                        sp.dma_start(t[:, WA:WA + L], row(nodes_d, u)).then_inc(s(f"qk{r % 2}"), 16)
                        sp.dma_start(t[:, WA + L:WA + 2 * L], row(nodes_d, (u // 40) * NB + u % NB)).then_inc(s(f"qk{r % 2}"), 16)
                    else:
                        sp.dma_start(t[:, WA:WA + L], row(x2T_d, u // 2)).then_inc(s(f"qk{r % 2}"), 16)

                def load_v(q, r, c=c, s=s):
                    if not inside(c, q, r):
                        return
                    u = RING * q + r
                    t = st_v[r % 2]
                    when((s("v_ev"), u - 1), *[(s("store"), 16 * (u - NB + 3))] * c.node)
                    if c.node:
                        sp.dma_start(t[:, 0:WB], row(wB_d, u // NB)).then_inc(s(f"v{r % 2}"), 16)
                        sp.dma_start(t[:, WB:WB + L], row(nodes_d, ((u // NB + 1) // 2) * NB + u % NB)).then_inc(s(f"v{r % 2}"), 16)
                    else:
                        sp.dma_start(t[:, WB:WB + L], row(x2T_d, u // 2)).then_inc(s(f"v{r % 2}"), 16)

                def load_o(q, r, c=c, s=s):
                    if not c.node or not inside(c, q, r):
                        return
                    u = RING * q + r
                    when((s("wo_ps"), u - 1))
                    sp.dma_start(st_o[r % 2], row(wO_d, u // NB)).then_inc(s(f"o{r % 2}"), 16)

                def stack(q, r, c=c, s=s):
                    if not inside(c, q, r):
                        return
                    u = RING * q + r
                    when((s("spk"), u + 1), (s("spq"), u + 1), (s("ex"), 16 * (u - RING + 1)))
                    for i, (pq, pk) in enumerate(c.terms):
                        rows = slice(i * c.hd, (i + 1) * c.hd)
                        sp.dma_start(kst[rows, r % RING, :, :], kp_[0:c.np_, pk, :]).then_inc(s(f"stk{r % RING}"), 16)
                        sp.dma_start(qst[rows, r % RING, :, :], qp[0:c.np_, pq, :]).then_inc(s(f"stk{r % RING}"), 16)

                def store(q, r, c=c, s=s):
                    if not inside(c, q, r):
                        return
                    u = RING * q + r
                    if c.node:
                        when((s("store"), 16 * u), (s("wo_ev"), u + 1))
                        sp.dma_start(row(nodes_d, u + NB), no_sb).then_inc(s("store"), 16)
                    elif r % 2:
                        b1 = 2 * q + r // 2 + 1
                        when((s("x3T_ev"), b1))
                        sp.dma_start(row(nodes_d, u // 2), no_sb).then_inc(s("store"), 16)
                        sp.dma_start(row(x3_d, u // 2), x3s).then_inc(s("x3out"), 16)

                def load_x2(q, r, c=c, s=s):
                    if c.node or r % 2 == 0 or not inside(c, q, r):
                        return
                    when((s("x3"), 2 * q + r // 2))
                    sp.dma_start(x2s, row(x2_d, 2 * q + r // 2)).then_inc(s("x2in"), 16)

                load_qk(0, 0)
                load_qk(0, 1)
                load_v(0, 0)
                stack(0, 0)
                load_qk(0, 2)
                stack(0, 1)
                load_v(0, 1)
                load_o(0, 0)

                def body(q, r, c=c):
                    load_qk(q, r + 3)
                    load_v(q, r + 2)
                    load_o(q, r + 1)
                    load_x2(q, r)
                    stack(q, r + 2)
                    store(q, r - 1)
                units(sp, c, body)
                store(c.U // RING, -1)
                sp.wait_ge(s("store"), 16 * (c.U if c.node else NB))
                if not c.node:
                    sp.wait_ge(s("x3out"), 16 * NB)

            with sp.Fori(0, NB) as b:
                when((S["f_y"], b + 1))
                sp.dma_start(no_sb, row(nodes_d, b + NODES * NB)).then_inc(S["f_n_in"], 16)
                sp.dma_start(x2s, row(x3_d, b)).then_inc(S["f_x3_in"], 16)
                when((S["f_y"], b + 2))
                sp.dma_start(tokens(a["out"], b), x3s.rearrange("p (t d) -> p t d", t=NT)).then_inc(S["f_out"], 16)
            sp.wait_ge(S["f_out"], 16 * NB + 1)

        @block.gpsimd
        def _(pool):
            for x in credit + [S["b_e_ev"]]:
                pool.sem_inc(x, 1)
            pool.memset(ident[:, :], 0.0).then_inc(s_id, 1)
            pool.memset(identb[:, :], 0.0).then_inc(s_id, 1)
            pool.memset(half[:, :], -0.5).then_inc(s_c, 1)
            pool.memset(eps_ln[:, :], EPS_LN).then_inc(s_c, 1)
            pool.memset(eps_node[:, :], EPS_NODE).then_inc(s_c, 1)
            pool.memset(mean_w[:, :], 1.0 / DI).then_inc(s_c, 1)
            pool.memset(cbuf[:, :, 0:KC], 0.0).then_inc(s_c, 1)
            for e_ in range(NE):
                pool.memset(rank[:, e_:e_ + 1], float(NE - e_)).then_inc(s_c, 1)
            pool.wait_ge(s_id, 2)
            for m in (ident, identb):
                pool.affine_select(out=m[:, :], in_=m[:, :], compare_op=ALU.not_equal, fill=1.0, base=0,
                                   pattern=[[-1, P]], channel_multiplier=1).then_inc(s_id, 1)
            pool.wait_ge(s_c, 5 + NE)

            def rstd(mv_, t0, t1, eps, ready, link, done):
                pool.wait_ge(*ready)
                pool.tensor_tensor(t0, mv_[:, :, 1], eps, ALU.add).then_inc(link[0], 1)
                pool.wait_ge(*link)
                pool.tensor_tensor(t1, t0, half[:, :], ALU.pow).then_inc(done, 1)

            with pool.Fori(0, NB) as b:
                rstd(mva, rsb, rsa, eps_ln[:, :], (S["a_mv"], b + 2), (g_link, b + 2), S["a_rs"])
            with pool.Fori(0, NB) as b:
                rstd(mva, rsb, rsa, eps_ln[:, :], (S["b_mv"], 2 * b + 2), (g_link, NB + 2 * b + 2), S["b_rs"])
                rstd(mva, rsb, rsa, eps_ln[:, :], (S["b_mv"], 2 * b + 3), (g_link, NB + 2 * b + 3), S["b_rs"])

            for c in (cc, cd):
                s = c.s
                if not c.node:
                    pool.wait_ge(S["b_x2T_ev"], NB + 1)
                    pool.wait_ge(S["b_out"], 16 * NB + 1)
                    pool.wait_ge(S["b_outT"], 16 * NB + 1)
                    pool.memset(kst[64:P, :, :, :], 1.0).then_inc(s("ones"), 1)
                    for j in range(2):
                        pool.wait_ge(s("ones"), j + 1)
                        pool.memset(vaug[j], 1.0).then_inc(s("ones"), 1)
                    pool.wait_ge(s("ones"), 3)

                def split(q, r, c=c, s=s):
                    if not inside(c, q, r):
                        return
                    u = RING * q + r
                    base = 6 * u
                    n = c.np_
                    for i, (src, dst, ready, done) in enumerate(((kf, kp_, "kf_ev", "spk"), (qf, qp, "qf_ev", "spq"))):
                        need(pool, s(ready), u + 1)
                        if i == 0:
                            need(pool, s(f"stk{(r - 1) % RING}"), 16 * 2 * len(c.terms) * (q + (r - 1) // RING + 1))
                        pool.sem_inc(passed, 1)
                        pool.tensor_copy(dst[0:n, 0, :], src[0:n, :]).then_inc(s("pool"), 1)
                        need(pool, s("pool"), base + 3 * i + 1)
                        pool.tensor_tensor(src[0:n, :], src[0:n, :], dst[0:n, 0, :], ALU.subtract).then_inc(s("pool"), 1)
                        need(pool, s("pool"), base + 3 * i + 2)
                        pool.sem_inc(passed, 1)
                        pool.tensor_copy(dst[0:n, 1, :], src[0:n, :]).then_inc(s("pool"), 1)
                        need(pool, s("pool"), base + 3 * i + 3)
                        pool.tensor_tensor(dst[0:n, 2, :], src[0:n, :], dst[0:n, 1, :], ALU.subtract).then_inc(s(done), 1)

                split(0, 0)
                split(0, 1)

                def body(q, r, c=c, s=s):
                    split(q, r + 2)
                    if not c.node and r % 2 == 0 and inside(c, q, r - 1):
                        b1 = 2 * q + r // 2
                        rstd(mv, rs0, rs, eps_ln[:, :], (s("mv"), b1), (s("plink"), b1), s("rs"))
                units(pool, c, body)
                if not c.node:
                    rstd(mv, rs0, rs, eps_ln[:, :], (s("mv"), NB), (s("plink"), NB), s("rs"))

            with pool.Fori(0, NB) as b:
                rstd(mv, rs0, rs, eps_node[:, :], (S["f_mv"], 2 * b + 2), (g_link, 3 * NB + 2 * b + 2), S["f_rs"])
                rstd(mv, rs0, rs, eps_ln[:, :], (S["f_mv"], 2 * b + 3), (g_link, 3 * NB + 2 * b + 3), S["f_rs"])

        @block.scalar
        def _(act):
            act.wait_ge(s_w, 16 * N_W)
            act.activation(aneg[:, 0:1], alog[:, :], ACT.Exp).then_inc(S["r_A"], 1)
            act.wait_ge(S["r_A"], 1)
            act.activation(aneg[:, 1:2], aneg[:, 0:1], ACT.Copy, scale=-1.0).then_inc(S["r_A"], 1)

            with act.Fori(0, NB) as b:
                now(act, "a_hT_ps", b)
                before(act, "a_win_ps", b)
                act.activation(hT, bank_m[:, :], ACT.Identity, bias=gb[:, 1:2], scale=gb[:, 0:1]).then_inc(S["a_hT_ev"], 1)
                now(act, "a_win_ps", b)
                before(act, "a_yh", b)
                act.activation(cbuf[:, :, KC:KC + L], bx0.rearrange("p (h n) -> p h n", h=NH), ACT.Copy).then_inc(S["a_xs_ev"], 1)
                before(act, "a_g_ev", b)
                act.activation(tg, bx1.rearrange("p (h n) -> p h n", h=NH), ACT.Tanh, scale=0.5).then_inc(S["a_tg"], 1)
                now(act, "a_yh", b)
                before(act, "a_sp", b)
                act.activation(ab, yh, ACT.Tanh).then_inc(S["a_th"], 1)
                now(act, "a_z_ev", b, NH)
                now(act, "a_xs", b)
                act.activation(ab, rl, ACT.Abs).then_inc(S["a_ab"], 1)
                now(act, "a_ab", b, 2, 1)
                act.activation(ab, ab, ACT.Exp, scale=-1.0).then_inc(S["a_ab"], 1)
                now(act, "a_ab", b, 2)
                act.activation(ab, ab, ACT.Ln, bias=1.0).then_inc(S["a_ln"], 1)
                now(act, "a_mb_ps", b)
                before(act, "a_dB_out", b, 16)
                act.activation(dbx[:, 0, :], bank_o[0:NS, :], ACT.Copy)
                act.activation(dbx[:, 1, :], bank_m[0:NS, :], ACT.Copy).then_inc(S["a_mb_ev"], 1)
            act.wait_ge(S["r_in"], 16)
            act.wait_ge(S["r_A"], 2)
            act.activation(hn, db[:, 0, :], ACT.Exp, scale=aneg[:, 1:2]).then_inc(S["r_dA"], 1)

            with act.Fori(0, NB) as b:
                now(act, "b_xT_ps", b)
                before(act, "b_e_ps", b, NT)
                act.activation(hT, bank_m[:, :], ACT.Copy).then_inc(S["b_xT_ev"], 1)
                now(act, "b_lg", b)
                for t in range(NT):
                    act.activation(lge[:, t, :], lg[:, t, :], ACT.Exp, bias=nmx[:, t:t + 1],
                                   accum_out=sm[:, t:t + 1]).then_inc(S["b_ex"], 1)
                now(act, "b_mgT_ps", b)
                act.activation(mgT, bank_m[0:NE, :], ACT.Copy).then_inc(S["b_mgT_ev"], 1)
                now(act, "b_yb_ps", b)
                act.activation(ybs, bank_o[:, :], ACT.Copy).then_inc(S["b_yb_ev"], 1)
                now(act, "b_x2T_ps", b)
                before(act, "b_outT", b, 16)
                act.activation(x2Tw, bank_m[:, :], ACT.Copy).then_inc(S["b_x2T_ev"], 1)

            for c in (cc, cd):
                s = c.s

                def ev_proj(q, r, which, c=c, s=s):
                    if not inside(c, q, r):
                        return
                    u = RING * q + r
                    n = c.np_
                    t = st_qk[r % 2]
                    if which == "qT":
                        need(act, s("qT_ps"), u + 1)
                        need(act, s("wo_ev"), u - RING + 1)
                        act.activation(q_sb[r % RING], bank_m[:, :], ACT.Identity, bias=t[:, 3 * P:3 * P + 1]).then_inc(s("q_ev"), 1)
                    elif which == "kh":
                        need(act, s("kh_ps"), u + 1)
                        need(act, s("spk"), u)
                        if c.node:
                            act.activation(kf[0:n, :], bank_m[0:n, :], ACT.Identity, bias=t[:, 3 * P + 1:3 * P + 2]).then_inc(s("kf_ev"), 1)
                        else:
                            act.activation(kf[0:n, :], bank_m[0:n, :], ACT.Copy).then_inc(s("kf_ev"), 1)
                    else:
                        need(act, s("qh_ps"), u + 1)
                        need(act, s("spq"), u)
                        act.activation(qf[0:n, :], bank_m[0:n, :], ACT.Copy).then_inc(s("qf_ev"), 1)

                def ev_m(g, c=c, s=s):
                    q, r, k = g
                    if not inside(c, q, r):
                        return
                    G = 2 * (RING * q + r) + k
                    need(act, s("mT_ps"), G + 1)
                    need(act, s("m_dma"), 16 * G)
                    act.activation(mT[0:48, :], bank_m[0:48, 0:P], ACT.Copy).then_inc(s("mT_ev"), 1)
                    need(act, s("mT_ev"), G + 1)
                    act.dma_start(qst[c.R:c.R3, r % RING, GH * k:GH * k + GH, :], mT[0:48, :]).then_inc(s("m_dma"), 16)

                def ev_pv(q, r, k, c=c, s=s):
                    if not inside(c, q, r):
                        return
                    G = 2 * (RING * q + r) + k
                    need(act, s("pv_ps"), 2 * G + 2)
                    need(act, s("ot_ps"), G)
                    act.activation(ot_sb, bank_o[:, :], ACT.Copy).then_inc(s("pv_ev"), 1)

                def ev_cT(q, r, c=c, s=s):
                    if not c.node or not inside(c, q, r):
                        return
                    u = RING * q + r
                    need(act, s("cT_ps"), u + 1)
                    need(act, s("wo_ps"), u)
                    act.activation(ctxT, bank_m[:, :], ACT.Copy).then_inc(s("cT_ev"), 1)

                def ev_x3T(q, r, c=c, s=s):
                    if c.node or r % 2 == 0 or not inside(c, q, r):
                        return
                    b = 2 * q + r // 2
                    need(act, s("x3T_ps"), b + 1)
                    need(act, s("store"), 16 * b)
                    act.activation(no_sb, bank_m[:, :], ACT.Copy).then_inc(s("x3T_ev"), 1)

                def exp(q, r, k, i, c=c, s=s):
                    G = 2 * (RING * q + r) + k
                    kp, h = i // GH, i % GH
                    need(act, s("st_ps"), 8 * G + i + 1)
                    if h == 0:
                        need(act, s("pv_ps"), 2 * (G - 1) + kp + 1)
                    act.activation(PT[:, kp, h, :, :], bank_x[:, i % 2, :].rearrange("p (c n) -> p c n", c=2),
                                   ACT.Exp, scale=c.scale).then_inc(s("ex"), 1)

                def start(q, r, c=c):
                    if c.node:
                        ev_proj(q, r, "qT")
                    ev_proj(q, r, "kh")
                    ev_proj(q, r, "qh")

                start(0, 0)
                start(0, 1)
                ev_m((0, 0, 0))

                def body(q, r, c=c):
                    for i in range(8):
                        exp(q, r, 0, i)
                        if i == 0 and c.node:
                            ev_proj(q, r + 2, "qT")
                        if i == 1:
                            ev_proj(q, r + 2, "kh")
                        if i == 2:
                            ev_pv(q, r - 1, 1)
                            ev_proj(q, r + 2, "qh")
                        if i == 5:
                            ev_m((q, r, 1))
                        if i == 6:
                            ev_cT(q, r - 1)
                    for i in range(8):
                        exp(q, r, 1, i)
                        if i == 0:
                            ev_x3T(q, r - 1)
                        if i == 2:
                            ev_pv(q, r, 0)
                        if i == 5:
                            ev_m((q, r + 1, 0))
                units(act, c, body)
                G = 2 * c.U - 1
                act.wait_ge(s("pv_ps"), 2 * G + 2)
                act.wait_ge(s("ot_ps"), G)
                act.activation(ot_sb, bank_o[:, :], ACT.Copy).then_inc(s("pv_ev"), 1)
                if c.node:
                    act.wait_ge(s("cT_ps"), c.U)
                    act.wait_ge(s("wo_ps"), c.U - 1)
                    act.activation(ctxT, bank_m[:, :], ACT.Copy).then_inc(s("cT_ev"), 1)
                else:
                    act.wait_ge(s("x3T_ps"), NB)
                    act.wait_ge(s("store"), 16 * (NB - 1))
                    act.activation(no_sb, bank_m[:, :], ACT.Copy).then_inc(s("x3T_ev"), 1)

        @block.tensor
        def _(pe):
            pe.wait_ge(s_id, 4)
            pe.wait_ge(s_w, 16 * N_W)
            with pe.Fori(0, NODES) as c:
                now(pe, "p_bc", c)
                pe.matmul(bank_m[:, 0:P], wv["WeKT"], wv["WkP"], start=True, stop=True)
                pe.matmul(bank_o[:, 0:P], wv["WeVT"], wv["Wv"], start=True, stop=True)
                pe.matmul(bank_s[:, 0, 0:P], bvr, wv["Wv"], start=True, stop=True)
                pe.matmul(bank_s[:, 1, 0:1], wv["WkP"], vec[:, 1:2], start=True, stop=True).then_inc(S["p_mm"], 1)

            pe.wait_ge(S["p_ev"], NODES + 1)
            with pe.Fori(0, NB) as b:
                now(pe, "a_hn", b)
                before(pe, "a_mb_ev", b)
                for t in range(NT):
                    mm = pe.transpose(bank_m[:, t * P:(t + 1) * P], hn[:, t * P:(t + 1) * P], ident[:, :])
                mm.then_inc(S["a_hT_ps"], 1)
                now(pe, "a_hT_ev", b)
                before(pe, "a_g_ev", b)
                for j in range(2 * NH):
                    mm = pe.matmul(sec(bank_x[:, j // NH, :], j % NH), w_in[:, j * P:(j + 1) * P], hT, start=True, stop=True)
                mm.then_inc(S["a_win_ps"], 1)
                now(pe, "a_xs", b)
                before(pe, "a_sp", b)
                for h in range(NH):
                    for k in range(NH):
                        mm = pe.matmul(bank_s[:, h, :], wd[:, k, h * P:(h + 1) * P], yh[:, k, :],
                                       start=(k == 0), stop=(k == NH - 1))
                mm.then_inc(S["a_z_ps"], 1)
                now(pe, "a_sp", b)
                for k in range(NH):
                    pe.matmul(bank_o[0:NS, :], mean_w[:, :], rl[:, k, :], start=(k == 0), stop=(k == NH - 1))
                for k in range(NH):
                    mm = pe.matmul(bank_m[0:NS, :], bmt[:, k, :], yh[:, k, :], start=(k == 0), stop=(k == NH - 1))
                mm.then_inc(S["a_mb_ps"], 1)

            with pe.Fori(0, NB) as b:
                now(pe, "b_hs", b, 16)
                before(pe, "b_x2T_ev", b)
                for h in range(NH):
                    mm = pe.matmul(bank_s[:, h, :], cmt[:, h * P:(h + 1) * P], hsb, start=True, stop=True)
                mm.then_inc(S["b_c_ps"], 1)
                now(pe, "b_y", b)
                for t in range(NT):
                    for k in range(NH):
                        mm = pe.matmul(bank_o[:, t * P:(t + 1) * P], yh[:, k, t * P:(t + 1) * P], woh[:, k, :],
                                       start=(k == 0), stop=(k == NH - 1))
                mm.then_inc(S["b_yo_ps"], 1)
                now(pe, "b_x1", b)
                for t in range(NT):
                    mm = pe.transpose(bank_m[:, t * P:(t + 1) * P], hn[:, t * P:(t + 1) * P], ident[:, :])
                mm.then_inc(S["b_xT_ps"], 1)
                now(pe, "b_xT_ev", b)
                for t in range(NT):
                    mm = pe.matmul(bank_s[:, 0, t * NE:(t + 1) * NE], hT[:, t * P:(t + 1) * P], rw[:, :], start=True, stop=True)
                mm.then_inc(S["b_lg_ps"], 1)
                for t in range(NT):
                    pe.wait_ge(S["b_e_ev"], NT * b + t + 1)
                    for j in range(2):
                        mm = pe.matmul(sec(bank_x[:, t % 2, :], j), hT[:, t * P:(t + 1) * P], xw[:, j * 512:(j + 1) * 512],
                                       start=True, stop=True)
                    mm.then_inc(S["b_e_ps"], 1)
                    if t == 1:
                        now(pe, "b_mg", b)
                        for tt in range(NT):
                            mm = pe.transpose(bank_m[0:NE, tt * P:(tt + 1) * P], lgm[:, tt, :], ident[:, :])
                        mm.then_inc(S["b_mgT_ps"], 1)
                        now(pe, "b_mgT_ev", b)
                        for tt in range(NT):
                            mm = pe.matmul(bank_o[:, tt * P:(tt + 1) * P], mgT[:, tt * P:(tt + 1) * P], xb[:, :], start=True, stop=True)
                        mm.then_inc(S["b_yb_ps"], 1)
                now(pe, "b_x2", b)
                for t in range(NT):
                    mm = pe.transpose(bank_m[:, t * P:(t + 1) * P], x2w[:, t * P:(t + 1) * P], ident[:, :])
                mm.then_inc(S["b_x2T_ps"], 1)

            for c in (cc, cd):
                s = c.s
                last = [None]

                def misc(sem_, value, last=last):
                    if last[0] is not None:
                        need(pe, *last[0])
                    last[0] = (sem_, value)

                def proj(q, r, which, c=c, s=s):
                    if not inside(c, q, r):
                        return
                    u = RING * q + r
                    t = st_qk[r % 2]
                    nd = 3 if c.node else 1
                    n = c.np_
                    if which == "qT" or (which == "kh" and not c.node):
                        need(pe, s(f"qk{r % 2}"), 16 * nd * (2 * q + r // 2 + 1))
                    if which == "qT":
                        misc(s("q_ev"), u + 1)
                        pe.matmul(bank_m[:, :], t[:, 0:P], t[:, WA:WA + L], start=True, stop=True).then_inc(s("qT_ps"), 1)
                    elif which == "kh":
                        misc(s("kf_ev"), u + 1)
                        lhs, rhs = (t[:, 2 * P:3 * P], t[:, WA + L:WA + 2 * L]) if c.node else (wc[:, 1, (r % 2) * 64:(r % 2) * 64 + 64], t[:, WA:WA + L])
                        pe.matmul(bank_m[0:n, :], lhs, rhs, start=True, stop=True).then_inc(s("kh_ps"), 1)
                    else:
                        misc(s("qf_ev"), u + 1)
                        if c.node:
                            need(pe, s("q_ev"), u + 1)
                        lhs, rhs = (t[:, P:2 * P], q_sb[r % RING]) if c.node else (wc[:, 0, (r % 2) * 64:(r % 2) * 64 + 64], t[:, WA:WA + L])
                        pe.matmul(bank_m[0:n, :], lhs, rhs, start=True, stop=True).then_inc(s("qh_ps"), 1)

                def value(q, r, c=c, s=s):
                    if not inside(c, q, r):
                        return
                    u = RING * q + r
                    t = st_v[r % 2]
                    nd = 2 if c.node else 1
                    n = c.np_
                    need(pe, s(f"v{r % 2}"), 16 * nd * (2 * q + r // 2 + 1))
                    misc(s("v_ev"), u + 1)
                    w = t[:, 0:P] if c.node else wc[:, 2, (r % 2) * 64:(r % 2) * 64 + 64]
                    for k in range(NT):
                        mm = pe.matmul(bank_m[:, k * n:(k + 1) * n], t[:, WB + k * P:WB + (k + 1) * P], w, start=True, stop=True)
                    mm.then_inc(s("v_ps"), 1)

                def scores(q, r, k, n, c=c, s=s):
                    if not inside(c, q, r):
                        return
                    N = 16 * (2 * (RING * q + r) + k) + n
                    slot = r % RING
                    if k == 0 and n == 0:
                        need(pe, s(f"stk{slot}"), 16 * 2 * len(c.terms) * (q + r // RING + 1))
                    need(pe, s("red"), N - 1)
                    h, t = GH * k + n // NT, n % NT
                    pe.matmul(bank_s[:, n % 2, :], qst[0:c.R, slot, h, t * P:(t + 1) * P], kst[0:c.R, slot, h, :],
                              start=True, stop=True).then_inc(s("s_ps"), 1)

                def maxima(q, r, k, c=c, s=s):
                    if not inside(c, q, r):
                        return
                    G = 2 * (RING * q + r) + k
                    need(pe, s("nm_ok"), G + 1)
                    misc(s("mT_ev"), G + 1)
                    pe.matmul(bank_m[0:48, 0:P], mp[:, 0:48], identb[:, :], start=True, stop=True).then_inc(s("mT_ps"), 1)

                def scoresT(q, r, k, i, c=c, s=s):
                    G = 2 * (RING * q + r) + k
                    t = 8 * G + i
                    kp, h = i // GH, GH * k + i % GH
                    if i == 0:
                        need(pe, s("m_dma"), 16 * (G + 1))
                    need(pe, s("ex"), t - 1)
                    for j in range(2):
                        kc = 2 * kp + j
                        mm = pe.matmul(sec(bank_x[:, i % 2, :], j), kst[0:c.R3, r % RING, h, kc * P:(kc + 1) * P],
                                       qst[0:c.R3, r % RING, h, :], start=True, stop=True)
                    mm.then_inc(s("st_ps"), 1)

                def output(q, r, k, kp, c=c, s=s):
                    if not inside(c, q, r):
                        return
                    u = RING * q + r
                    G = 2 * u + k
                    need(pe, s("ex"), 8 * G + 4 * kp + 4)
                    if kp == 0:
                        need(pe, s("pv_ev"), G)
                        need(pe, s("v_ev"), u + 1)
                    for j in range(2):
                        for h in range(GH):
                            mm = pe.matmul(bank_o[COL * h:COL * (h + 1), :], vaug[r % 2][:, 2 * kp + j, GH * k + h, :],
                                           PT[:, kp, h, j, :], start=(kp == 0 and j == 0), stop=(kp == 1 and j == 1))
                    mm.then_inc(s("pv_ps"), 1)

                def turn(q, r, k, c=c, s=s):
                    if not inside(c, q, r):
                        return
                    G = 2 * (RING * q + r) + k
                    need(pe, s("pv_ev"), G + 1)
                    misc(s("ot_ev"), G + 1)
                    for t in range(NT):
                        mm = pe.transpose(bank_m[:, t * P:(t + 1) * P], ot_sb[:, t * P:(t + 1) * P], ident[:, :])
                    mm.then_inc(s("ot_ps"), 1)

                def turn_ctx(q, r, c=c, s=s):
                    if not c.node or not inside(c, q, r):
                        return
                    u = RING * q + r
                    need(pe, s("ot_ev"), 2 * u + 2)
                    misc(s("cT_ev"), u + 1)
                    for t in range(NT):
                        mm = pe.transpose(bank_m[:, t * P:(t + 1) * P], ctx_sb[:, t * P:(t + 1) * P], ident[:, :])
                    mm.then_inc(s("cT_ps"), 1)

                def out_proj(q, r, c=c, s=s):
                    if not c.node or not inside(c, q, r):
                        return
                    u = RING * q + r
                    need(pe, s(f"o{r % 2}"), 16 * (2 * q + r // 2 + 1))
                    misc(s("wo_ev"), u + 1)
                    pe.matmul(bank_m[:, :], st_o[r % 2], ctxT, start=True, stop=True).then_inc(s("wo_ps"), 1)

                def turn_x3(q, r, c=c, s=s):
                    if c.node or r % 2 == 0 or not inside(c, q, r):
                        return
                    b = 2 * q + r // 2
                    need(pe, s("x3"), b + 1)
                    misc(s("x3T_ev"), b + 1)
                    for t in range(NT):
                        mm = pe.transpose(bank_m[:, t * P:(t + 1) * P], x3s[:, t * P:(t + 1) * P], ident[:, :])
                    mm.then_inc(s("x3T_ps"), 1)

                def start(q, r, c=c):
                    if c.node:
                        proj(q, r, "qT")
                    proj(q, r, "kh")
                    proj(q, r, "qh")

                if not c.node:
                    pe.wait_ge(s("ones"), 3)
                    need(pe, S["b_x2T_ev"], NB + 1)
                start(0, 0)
                start(0, 1)
                value(0, 0)
                for n in range(16):
                    scores(0, 0, 0, n)
                maxima(0, 0, 0)
                for n in range(8):
                    scores(0, 0, 1, n)

                def lead(q, r, k, i):
                    k1, r1 = (1, r) if k == 0 else (0, r + 1)
                    for j in range(2):
                        if i < 4:
                            scores(q, r1, k1, 8 + 2 * i + j)
                        else:
                            scores(q, r + 1, k, 2 * (i - 4) + j)

                def body(q, r, c=c):
                    for i in range(8):
                        scoresT(q, r, 0, i)
                        lead(q, r, 0, i)
                        if i == 0 and c.node:
                            proj(q, r + 2, "qT")
                        if i == 1:
                            output(q, r - 1, 1, 1)
                            proj(q, r + 2, "kh")
                        if i == 2:
                            proj(q, r + 2, "qh")
                        if i == 3:
                            turn(q, r - 1, 1)
                        if i == 5:
                            output(q, r, 0, 0)
                            maxima(q, r, 1)
                        if i == 6:
                            turn_ctx(q, r - 1)
                    for i in range(8):
                        scoresT(q, r, 1, i)
                        lead(q, r, 1, i)
                        if i == 0:
                            out_proj(q, r - 1)
                            turn_x3(q, r - 1)
                        if i == 1:
                            output(q, r, 0, 1)
                            value(q, r + 1)
                        if i == 3:
                            turn(q, r, 0)
                        if i == 5:
                            output(q, r, 1, 0)
                            maxima(q, r + 1, 0)

                def units_pe(c=c):
                    for u in range(RING):
                        body(0, u)
                    keep = last[0]
                    with pe.Fori(1, c.U // RING - 1) as it:
                        last[0] = (s("mT_ev"), 2 * RING * it + 1)
                        for r in range(RING):
                            body(it, r)
                    qe = c.U // RING - 1
                    last[0] = (s("mT_ev"), 2 * RING * qe + 1)
                    for r in range(RING):
                        body(qe, r)
                units_pe()
                qe, re = c.U // RING - 1, RING - 1
                output(qe, re, 1, 1)
                turn(qe, re, 1)
                turn_ctx(qe, re)
                if c.node:
                    need(pe, s("cT_ev"), c.U)
                out_proj(qe, re)
                turn_x3(qe, re)

            with pe.Fori(0, NB) as b:
                now(pe, "f_n_in", b, 16)
                before(pe, "f_y", b)
                for t in range(NT):
                    mm = pe.transpose(bank_m[:, t * P:(t + 1) * P], no_sb[:, t * P:(t + 1) * P], ident[:, :])
                mm.then_inc(S["f_tT_ps"], 1)

        @block.vector
        def _(dve):
            dve.wait_ge(s_w, 16 * N_W)
            dve.wait_ge(s_c, 5 + NE)
            dve.tensor_scalar(cvh[:, :, :], cv[:, :, 0:KC + 1], 0.5, None, ALU.mult).then_inc(s_c, 1)
            dve.tensor_scalar(woh[:, :, :], w_out[:, :, :], 0.5, None, ALU.mult).then_inc(s_c, 1)

            with dve.Fori(0, NODES) as c:
                now(dve, "p_in", c, 16)
                dve.tensor_copy(bvr, vec[:, 2:3].broadcast_to([P, P])).then_inc(S["p_bc"], 1)
                now(dve, "p_mm", c)
                before(dve, "p_out", c, 48)
                dve.tensor_scalar(po_sb[:, 0:P], wv["WeQ"], vec[:, 3:4], None, ALU.mult)
                dve.tensor_copy(po_sb[:, P:2 * P], wv["WqP"])
                dve.tensor_scalar(po_sb[:, 2 * P:3 * P], bank_m[:, 0:P], vec[:, 4:5], None, ALU.mult)
                dve.tensor_scalar(po_sb[:, 3 * P:3 * P + 1], vec[:, 0:1], vec[:, 3:4], None, ALU.mult)
                dve.tensor_scalar(po_sb[:, 3 * P + 1:WA], bank_s[:, 1, 0:1], vec[:, 4:5], None, ALU.mult)
                dve.tensor_scalar(po_sb[:, WA:WA + P], bank_o[:, 0:P], vec[:, 5:6], None, ALU.mult)
                dve.tensor_scalar(po_sb[:, WA + P:WA + WB], bank_s[:, 0, 0:P], vec[:, 5:6], None, ALU.mult)
                dve.tensor_scalar(po_sb[:, WA + WB:WA + WB + P], wv["Wo"], vec[:, 6:7], None, ALU.mult).then_inc(S["p_ev"], 1)

            def stats(src, st_, mv_, link, base, done):
                for t in range(NT):
                    dve.bn_stats(st_[:, t, :], src[:, t * D:(t + 1) * D]).then_inc(link, 1)
                need(dve, link, base + NT)
                dve.sem_inc(passed, 1)
                for t in range(NT):
                    i = dve.bn_aggr(mv_[:, t, :], st_[:, t, :])
                i.then_inc(done, 1)

            def normalise(dst, src, mv_, rs_, done):
                for t in range(NT):
                    i = dve.tensor_scalar(dst[:, t * D:(t + 1) * D], src[:, t * D:(t + 1) * D], mv_[:, t, 0:1], rs_[:, t:t + 1],
                                          ALU.subtract, ALU.mult)
                i.then_inc(done, 1)

            K = NT + NH + NH * (KC - 2) + 1 + 1
            xtf = xt.rearrange("p t d -> p (t d)")
            dve.wait_ge(s_c, 5 + NE + 2)
            with dve.Fori(0, NB) as b:
                n = K * b + 1
                now(dve, "a_x", b, 16)
                stats(xtf, sta, mva, v_link, n, S["a_mv"])
                n = n + NT
                now(dve, "a_rs", b)
                before(dve, "a_hT_ps", b)
                normalise(hn, xtf, mva, rsa, S["a_hn"])
                now(dve, "a_xs_ev", b)
                before(dve, "a_mb_ps", b)
                for h in range(NH):
                    dve.tensor_scalar(yh[:, h, :], cbuf[:, h, KC:KC + L], cvh[:, h, KC - 1:KC], cvh[:, h, KC:KC + 1],
                                      ALU.mult, ALU.add).then_inc(v_link, 1)
                for j in range(1, KC):
                    for h in range(NH):
                        n = n + 1
                        dve.wait_ge(v_link, n)
                        i = dve.scalar_tensor_tensor(yh[:, h, :], cbuf[:, h, KC - j:KC - j + L],
                                                     cvh[:, h, KC - 1 - j:KC - j], yh[:, h, :], ALU.mult, ALU.add)
                        i.then_inc(S["a_yh"] if (j, h) == (KC - 1, NH - 1) else v_link, 1)
                n = n + 1
                now(dve, "a_tg", b)
                dve.scalar_tensor_tensor(sg_all[:, :, bass.ds(b * L, L)], tg, 1.0,
                                         bx1.rearrange("p (h n) -> p h n", h=NH), ALU.add, ALU.mult).then_inc(S["a_g_ev"], 1)
                now(dve, "a_th", b)
                dve.wait_ge(v_link, n)
                now(dve, "a_yh", b)
                dve.scalar_tensor_tensor(yh, ab, 1.0, yh, ALU.add, ALU.mult).then_inc(S["a_xs"], 1)
                now(dve, "a_xs", b)
                dve.tensor_copy(xs_all[:, :, bass.ds(b * L, L)], yh).then_inc(v_link, 1)
                n = n + 1
                now(dve, "a_z_ps", b)
                before(dve, "a_mb_ps", b)
                for h in range(NH):
                    dve.tensor_scalar(rl[:, h, :], bank_s[:, h, :], cv[:, h, KC + 2:KC + 3], None, ALU.add).then_inc(S["a_z_ev"], 1)
                now(dve, "a_ln", b)
                dve.scalar_tensor_tensor(rl, rl, 0.0, ab, ALU.max, ALU.add).then_inc(S["a_sp"], 1)

            dve.wait_ge(S["r_in"], 16)
            dve.tensor_tensor(hT, db[:, 1, :], db[:, 0, :], ALU.mult).then_inc(S["r_bx"], 1)
            dve.wait_ge(S["r_dA"], 1)
            dve.wait_ge(S["r_bx"], 1)
            dve.tensor_tensor_scan(hs, hn, hT, 0.0, ALU.mult, ALU.add).then_inc(S["r_hs"], 1)

            KB = NH + 1 + NT + 1 + 1 + 2 + 1 + 2 + NT * (NE - 1) + 1 + NT
            with dve.Fori(0, NB) as b:
                first = K * NB + KB * b + 1
                n = 0

                def link(ins):
                    nonlocal n
                    n += 1
                    ins.then_inc(v_link, 1)
                    dve.wait_ge(v_link, first + n)

                now(dve, "b_c_ps", b)
                for h in range(NH):
                    link(dve.scalar_tensor_tensor(yh[:, h, :], xs_all[:, h, bass.ds(b * L, L)], cv[:, h, KC + 1:KC + 2], bank_s[:, h, :],
                                                  ALU.mult, ALU.add))
                dve.tensor_tensor(yh, yh, sg_all[:, :, bass.ds(b * L, L)], ALU.mult).then_inc(S["b_y"], 1)
                now(dve, "b_x", b, 16)
                now(dve, "b_yo_ps", b)
                link(dve.scalar_tensor_tensor(tg[:, 0, :], xtf, 2.0, bank_o[:, :], ALU.mult, ALU.add))
                stats(tg[:, 0, :], sta, mva, v_link, first + n, S["b_mv"])
                n += NT
                now(dve, "b_rs", b, 2, 1)
                before(dve, "b_xT_ps", b)
                normalise(hn, tg[:, 0, :], mva, rsa, S["b_x1"])
                now(dve, "b_lg_ps", b)
                link(dve.tensor_tensor(lg, bank_s[:, 0, 0:NT * NE].rearrange("p (t e) -> p t e", t=NT),
                                       rb[:, :].unsqueeze(1).broadcast_to([P, NT, NE]), ALU.add))
                link(dve.tensor_reduce(mx, lg, AX.X, ALU.max))
                dve.tensor_scalar(nmx, mx, -1.0, None, ALU.mult).then_inc(S["b_lg"], 1)
                before(dve, "b_mgT_ps", b)
                link(dve.tensor_tensor(lgm, lg, mx.unsqueeze(2).broadcast_to([P, NT, NE]), ALU.is_equal))
                link(dve.tensor_tensor(lgm, lgm, rank[:, :].unsqueeze(1).broadcast_to([P, NT, NE]), ALU.mult))
                link(dve.tensor_reduce(fm, lgm, AX.X, ALU.max))
                link(dve.tensor_tensor(lgm, lgm, fm.unsqueeze(2).broadcast_to([P, NT, NE]), ALU.is_equal))
                now(dve, "b_ex", b, NT)
                link(dve.reciprocal(mx, sm))
                dve.tensor_tensor(lgm, lgm, mx.unsqueeze(2).broadcast_to([P, NT, NE]), ALU.mult).then_inc(S["b_mg"], 1)
                now(dve, "b_mg", b)
                now(dve, "b_x1", b)
                for t in range(NT):
                    now(dve, "b_e_ps", b, NT, t + 1)
                    dst = tg[:, 1, t * D:(t + 1) * D]
                    for e_ in range(NE):
                        in1 = hn[:, t * D:(t + 1) * D] if e_ == 0 else dst
                        i = dve.scalar_tensor_tensor(dst, bank_x[:, t % 2, e_ * D:(e_ + 1) * D], lgm[:, t, e_:e_ + 1], in1,
                                                     ALU.mult, ALU.add)
                        if e_ < NE - 1:
                            link(i)
                        else:
                            i.then_inc(S["b_e_ev"], 1)
                now(dve, "b_yb_ev", b)
                dve.wait_ge(S["b_e_ev"], NT * b + NT + 2)
                link(dve.tensor_tensor(tg[:, 1, :], tg[:, 1, :], ybs, ALU.add))
                stats(tg[:, 1, :], sta, mva, v_link, first + n, S["b_mv"])
                n += NT
                now(dve, "b_rs", b, 2)
                before(dve, "b_x2T_ps", b)
                before(dve, "b_out", b, 16)
                normalise(x2w, tg[:, 1, :], mva, rsa, S["b_x2"])
                assert KB == n, (KB, n)

            for c in (cc, cd):
                s = c.s
                hd = c.hd
                cx = ctx_sb.rearrange("p (t m) -> p t m", t=NT)

                def reduce(q, r, k, n, c=c, s=s):
                    if not inside(c, q, r):
                        return
                    G = 2 * (RING * q + r) + k
                    N = 16 * G + n
                    need(dve, s("s_ps"), N + 1)
                    dve.tensor_reduce(nm[:, k, n:n + 1], bank_s[:, n % 2, :], AX.X, ALU.max, negate=True).then_inc(s("red"), 1)

                def parts(q, r, k, c=c, s=s):
                    if not inside(c, q, r):
                        return
                    G = 2 * (RING * q + r) + k
                    base = 3 * G
                    need(dve, s("red"), 16 * G + 16)
                    need(dve, s("mT_ps"), G)
                    dve.tensor_copy(mp[:, 0:16], nm[:, k, :]).then_inc(s("link"), 1)
                    need(dve, s("link"), base + 1)
                    dve.tensor_tensor(mr, nm[:, k, :], mp[:, 0:16], ALU.subtract).then_inc(s("link"), 1)
                    need(dve, s("link"), base + 2)
                    dve.tensor_copy(mp[:, 16:32], mr).then_inc(s("link"), 1)
                    need(dve, s("link"), base + 3)
                    dve.tensor_tensor(mp[:, 32:48], mr, mp[:, 16:32], ALU.subtract).then_inc(s("nm_ok"), 1)

                def divide(q, r, k, c=c, s=s):
                    if not inside(c, q, r):
                        return
                    u = RING * q + r
                    G = 2 * u + k
                    need(dve, s("ot_ps"), G + 1)
                    o4 = bank_m[:, :].rearrange("p (t h m) -> p t h m", t=NT, h=GH)
                    dve.reciprocal(rec, o4[:, :, :, hd]).then_inc(s("x2link"), 1)
                    need(dve, s("x2link"), G + 1)
                    if c.node:
                        w = NT * hd * HU
                        dst = cx[:, :, GH * hd * k:GH * hd * (k + 1)]
                        if k == 0:
                            need(dve, s("cT_ps"), u)
                    else:
                        h0 = (r % 2) * 64 + GH * hd * k
                        dst = cx[:, :, h0:h0 + GH * hd]
                    dve.tensor_tensor(dst.rearrange("p t (h m) -> p t h m", h=GH), o4[:, :, :, 0:hd],
                                      rec.unsqueeze(3).broadcast_to([P, NT, GH, hd]), ALU.mult).then_inc(s("ot_ev"), 1)

                def values(q, r, c=c, s=s):
                    if not inside(c, q, r):
                        return
                    u = RING * q + r
                    need(dve, s("v_ps"), u + 1)
                    need(dve, s("pv_ps"), 4 * (u - 2) + 4)
                    src = bank_m[:, 0:NT * c.np_].rearrange("p (k h m) -> p k h m", k=NT, h=HU)
                    dst = vaug[r % 2][:, :, :, 0:hd]
                    if c.node:
                        bias = st_v[r % 2][:, P:2 * P].rearrange("p (h m) -> p h m", h=HU).unsqueeze(1).broadcast_to([P, NT, HU, hd])
                        dve.tensor_tensor(dst, src, bias, ALU.add).then_inc(s("v_ev"), 1)
                    else:
                        dve.tensor_copy(dst, src).then_inc(s("v_ev"), 1)

                def node_out(q, r, c=c, s=s):
                    if not c.node or not inside(c, q, r):
                        return
                    u = RING * q + r
                    need(dve, s("wo_ps"), u + 1)
                    need(dve, s("store"), 16 * u)
                    dve.tensor_tensor(no_sb, bank_m[:, :], q_sb[r % RING], ALU.add).then_inc(s("wo_ev"), 1)

                def residual(q, r, c=c, s=s):
                    if c.node or r % 2 == 0 or not inside(c, q, r):
                        return
                    b = 2 * q + r // 2
                    need(dve, s("x2in"), 16 * b + 16)
                    need(dve, s("ot_ev"), 4 * b + 4)
                    dve.tensor_tensor(ctx_sb, ctx_sb, x2s, ALU.add).then_inc(s("xlink"), 1)
                    need(dve, s("xlink"), (NT + 1) * b + 1)
                    stats(ctx_sb, stt, mv, s("xlink"), (NT + 1) * b + 1, s("mv"))
                    need(dve, s("rs"), b + 1)
                    need(dve, s("x3T_ps"), b)
                    need(dve, s("x3out"), 16 * b)
                    normalise(x3s, ctx_sb, mv, rs, s("x3"))

                if not c.node:
                    dve.wait_ge(s("ones"), 3)
                values(0, 0)
                for n in range(16):
                    reduce(0, 0, 0, n)
                parts(0, 0, 0)
                for n in range(8):
                    reduce(0, 0, 1, n)

                def lead(q, r, k, i):
                    k1, r1 = (1, r) if k == 0 else (0, r + 1)
                    for j in range(2):
                        if i < 4:
                            reduce(q, r1, k1, 8 + 2 * i + j)
                        else:
                            reduce(q, r + 1, k, 2 * (i - 4) + j)
                    if i == 3:
                        parts(q, r1, k1)

                def body(q, r, c=c):
                    for i in range(8):
                        lead(q, r, 0, i)
                        if i == 4:
                            divide(q, r - 1, 1)
                        if i == 5:
                            residual(q, r - 1)
                    for i in range(8):
                        lead(q, r, 1, i)
                        if i == 0:
                            node_out(q, r - 1)
                        if i == 1:
                            values(q, r + 1)
                        if i == 4:
                            divide(q, r, 0)
                units(dve, c, body)
                qe, re = c.U // RING - 1, RING - 1
                divide(qe, re, 1)
                residual(qe, re)
                node_out(qe, re)

            g0, b0 = (lngb[:, j, :].unsqueeze(1).broadcast_to([P, NT, D]) for j in range(2))
            KF = NT + 3 + NT
            with dve.Fori(0, NB) as b:
                n = K * NB + KB * NB + KF * b + 1
                now(dve, "f_tT_ps", b)
                stats(bank_m[:, :], stt, mv, v_link, n, S["f_mv"])
                n = n + NT
                now(dve, "f_rs", b, 2, 1)
                normalise(ctx_sb, bank_m[:, :], mv, rs, v_link)
                dve.wait_ge(v_link, n + 1)
                c3 = ctx_sb.rearrange("p (t d) -> p t d", t=NT)
                dve.tensor_tensor(c3, c3, g0, ALU.mult).then_inc(v_link, 1)
                dve.wait_ge(v_link, n + 2)
                dve.tensor_tensor(c3, c3, b0, ALU.add).then_inc(v_link, 1)
                dve.wait_ge(v_link, n + 3)
                now(dve, "f_x3_in", b, 16)
                dve.tensor_tensor(ctx_sb, ctx_sb, x2s, ALU.add).then_inc(S["f_z"], 1)
                now(dve, "f_z", b)
                stats(ctx_sb, stt, mv, v_link, n + 3, S["f_mv"])
                now(dve, "f_rs", b, 2)
                before(dve, "f_out", b, 16)
                normalise(x3s, ctx_sb, mv, rs, S["f_y"])


def kernel(**inputs):
    import numpy as np
    import concourse.bacc as bacc
    from concourse.bass_utils import run_bass_kernel_spmd

    i = {k: np.asarray(v) for k, v in inputs.items()}
    rows = lambda v: np.ascontiguousarray(np.broadcast_to(v, (P,) + v.shape))
    blocks = lambda w: np.ascontiguousarray(w.reshape(NH, P, -1).transpose(1, 0, 2))

    def dims_first(w, heads):
        return w.reshape(P, heads, -1).transpose(0, 2, 1).reshape(P, -1)

    def halves(w):
        return np.ascontiguousarray(np.concatenate([dims_first(w[:, h * 64:(h + 1) * 64], HU) for h in range(2)], 1))

    col = lambda v: v.reshape(NH, P).T[:, :, None]
    zero = np.zeros((P, NH, 1), np.float32)
    conv = i["L0_attn_conv_w"].reshape(NH, P, KC).transpose(1, 0, 2)
    cv = np.concatenate([conv, col(i["L0_attn_conv_b"]), col(i["L0_attn_D_vec"]), col(i["L0_attn_bd"]), zero], 2)

    pk, first = [], 0
    We, be = i["L1_ffn_We"], i["L1_ffn_be"]
    for c in range(NODES):
        n = min(c + 1, 5)
        eq, ek, ev = first + n - 1, first, first + n // 2
        first += n
        pk.append(np.concatenate([
            We[eq], dims_first(i["L1_ffn_Wq"][c], HU), We[ek].T, dims_first(i["L1_ffn_Wk"][c], HU), We[ev].T,
            i["L1_ffn_Wv"][c], i["L1_ffn_Wo"][c], be[eq][:, None], be[ek][:, None], be[ev][:, None],
            rows(i["L1_ffn_ew"][c]), rows(i["L1_ffn_act_w"][c:c + 1])], 1))

    arrays = {
        "x": i["L0_attn_x"], "cv": cv, "gb": np.stack([i["L0_attn_ln_gamma"], i["L0_attn_ln_beta"]], 1),
        "alog": np.tile(i["L0_attn_A_log"], NB)[:, None], "w_in": i["L0_attn_W_in"], "wd": blocks(i["L0_attn_Wd"]),
        "w_out": blocks(i["L0_attn_W_out"]), "bmt": blocks(i["L0_attn_B_mat"].T), "cmt": i["L0_attn_C_mat"].T,
        "rw": i["L0_ffn_router_w"], "rb": rows(i["L0_ffn_router_b"]),
        "xw": i["L0_ffn_expert_w"].transpose(1, 0, 2).reshape(D, NE * D), "xb": i["L0_ffn_expert_b"],
        "wcq": halves(i["L1_attn_w_Q"]), "wck": halves(i["L1_attn_w_K"]), "wcv": i["L1_attn_w_V"],
        "lng": rows(i["L1_ffn_ln_g"]), "lnb": rows(i["L1_ffn_ln_b"]), "pk": np.stack(pk),
    }
    arrays = {k: np.ascontiguousarray(v) for k, v in arrays.items()}
    nc = bacc.Bacc("TRN2", target_bir_lowering=False, num_devices=1)
    a = {k: nc.dram_tensor("in_" + k, v.shape, F32, kind="ExternalInput").ap() for k, v in arrays.items()}
    a["out"] = nc.dram_tensor("out_x", (NB, L, D), F32, kind="ExternalOutput").ap()
    build(nc, a)
    r = run_bass_kernel_spmd(nc, [{"in_" + k: v for k, v in arrays.items()}], core_ids=[0])
    return r.results[0]["out_x"]
```

```python
from contextlib import ExitStack

import concourse.bass as bass
from concourse import mybir

F32 = mybir.dt.float32
BF16 = mybir.dt.bfloat16
ACT = mybir.ActivationFunctionType
ALU = mybir.AluOpType
AX = mybir.AxisListType

P = 128
NB = 8
L = 512
D = 128
NT = L // P
DI = 256
NH = DI // P
NS = 16
KC = 4
NE = 8
NODES = 6
HU = 8
GH = 4
COL = 32
RING = 4
EPS_LN = 1e-5
EPS_NODE = 1e-6

TERMS_16 = [(0, 0), (0, 1), (0, 2), (1, 0), (1, 1), (2, 0)]
TERMS_8 = [(a, b) for a in range(3) for b in range(3)]
ROWS_TOP = 128

PK = ["WeQ", "WqP", "WeKT", "WkP", "WeVT", "Wv", "Wo"]
PKC = len(PK) * P + 3 + 4
WA = 3 * P + 2
WN = WA + 2 * P + 1


def need(e, sem, value):
    if isinstance(value, int) and value <= 0:
        return
    e.wait_ge(sem, value)


def build(nc, a):
    f = lambda name, shape: nc.dram_tensor(name, shape, F32).ap()
    w_d = f("w_d", (NODES, P, WN))
    dB_d = f("dB_d", (NB, NS, 2, L))
    hs_d = f("hs_d", (NB, NS, L))
    x2T_d, x2_d, x3_d = f("x2T_d", (NB, P, L)), f("x2_d", (NB, P, NT * D)), f("x3_d", (NB, P, NT * D))
    nodes_d = f("nodes_d", ((NODES + 1) * NB, P, L))

    with ExitStack() as ctx:
        def sb(name, shape, dt=F32):
            return ctx.enter_context(nc.sbuf_tensor(name, shape, dt))

        def sem(name):
            return ctx.enter_context(nc.semaphore(name))

        bank_x = ctx.enter_context(nc.psum_tensor("bank_x", [P, 2, 1024], F32))
        bank_s = ctx.enter_context(nc.psum_tensor("bank_s", [P, 2, 512], F32))
        bank_o = ctx.enter_context(nc.psum_tensor("bank_o", [P, 512], F32))
        bank_m = ctx.enter_context(nc.psum_tensor("bank_m", [P, 512], F32))

        ident = sb("ident", [P, P])
        identb = sb("identb", [P, P], BF16)
        half = sb("half", [P, NT])
        eps_ln, eps_node = sb("eps_ln", [P, NT]), sb("eps_node", [P, NT])
        cv = sb("cv", [P, NH, KC + 4])
        cvh = sb("cvh", [P, NH, KC + 1])
        gb = sb("gb", [P, 2])
        alog = sb("alog", [P, 1])
        aneg = sb("aneg", [P, 2])
        w_in = sb("w_in", [P, 2 * DI])
        wd = sb("wd", [P, NH, DI])
        w_out = sb("w_out", [P, NH, D])
        woh = sb("woh", [P, NH, D])
        bmt = sb("bmt", [P, NH, NS])
        cmt = sb("cmt", [NS, DI])
        mean_w = sb("mean_w", [P, NS])
        rw = sb("rw", [P, NE])
        rb = sb("rb", [P, NE])
        rank = sb("rank", [P, NE])
        xw = sb("xw", [P, NE * D])
        xb = sb("xb", [NE, D])
        wc = sb("wc", [P, 3, P])
        lngb = sb("lngb", [P, 2, D])

        big = sb("big", [P, 30 * 1024])
        xs_all = big[:, 0:8192]
        sg_all = big[:, 8192:16384]
        qst = big[:, 0:8192].bitcast(BF16).rearrange("p (u h n) -> p u h n", u=RING, h=HU)
        kst = big[:, 8192:16384].bitcast(BF16).rearrange("p (u h n) -> p u h n", u=RING, h=HU)
        PT = big[:, 16384:24576].rearrange("p (k h c n) -> p k h c n", k=2, h=GH, c=2)
        wk = big[:, 16384:30720]

        at = sb("at", [P, 15 * 1024])
        o = [0]

        def cut(n):
            o[0] += n
            return at[:, o[0] - n:o[0]]

        st_qk = [cut(WA + 2 * L) for _ in range(2)]
        st_v = [cut(P + L) for _ in range(2)]
        st_o = [cut(P + 2)[:, 0:P + 1] for _ in range(2)]
        q_sb = [cut(L) for _ in range(RING)]
        qf, kf = cut(L), cut(L)
        qp = cut(3 * L // 2).bitcast(BF16).rearrange("p (t n) -> p t n", t=3)
        kp_ = cut(3 * L // 2).bitcast(BF16).rearrange("p (t n) -> p t n", t=3)
        ot_sb = cut(L)
        assert o[0] <= 15 * 1024, o
        atb = big[:, 24576:30720]
        o2 = [0]

        def cut2(n):
            o2[0] += n
            return atb[:, o2[0] - n:o2[0]]

        vaug = [cut2(NT * HU * COL).rearrange("p (c h m) -> p c h m", c=NT, h=HU) for _ in range(2)]
        ctx_sb = cut2(L)
        ctxT = cut2(L)
        no_sb = cut2(L)
        x2s = cut2(L)
        x3s = cut2(L)
        nm = cut2(32).rearrange("p (g n) -> p g n", g=2)
        mr = cut2(16)
        mp = cut2(24).bitcast(BF16)
        mT = cut2(64).bitcast(BF16)
        rec = cut2(16).rearrange("p (t h) -> p t h", t=NT)
        stt = cut2(NT * 6).rearrange("p (t s) -> p t s", t=NT)
        mv = cut2(NT * 2).rearrange("p (t s) -> p t s", t=NT)
        rs = cut2(NT)
        rs0 = cut2(NT)
        mv2 = cut2(NT * 2).rearrange("p (t s) -> p t s", t=NT)
        rs2, rs20 = cut2(NT), cut2(NT)
        stt2 = cut2(NT * 6).rearrange("p (t s) -> p t s", t=NT)
        assert o2[0] <= 6144, o2

        w0 = [0]

        def cutw(n):
            w0[0] += n
            assert w0[0] <= 14336
            return wk[:, w0[0] - n:w0[0]]

        xt = cutw(L).rearrange("p (t d) -> p t d", t=NT)
        hn = cutw(L)
        hT = cutw(L)
        cbuf = cutw(NH * (L + KC)).rearrange("p (h n) -> p h n", h=NH)
        tg = cutw(NH * L).rearrange("p (h n) -> p h n", h=NH)
        yh = cutw(NH * L).rearrange("p (h n) -> p h n", h=NH)
        ab = cutw(NH * L).rearrange("p (h n) -> p h n", h=NH)
        rl = cutw(NH * L).rearrange("p (h n) -> p h n", h=NH)
        dbx = cutw(L)[0:COL + NS, :]
        db = cutw(2 * L).rearrange("p (t n) -> p t n", t=2)
        hs = cutw(L)
        hsb = cutw(L)[0:NS, :]
        x2w, x2Tw, esum = cutw(L), cutw(L), cutw(L)
        lg = cutw(NT * NE).rearrange("p (t e) -> p t e", t=NT)
        lge = cutw(NT * NE).rearrange("p (t e) -> p t e", t=NT)
        lgm = cutw(NT * NE).rearrange("p (t e) -> p t e", t=NT)
        mx = cutw(NT)
        nmx = cutw(NT)
        sm = cutw(NT)
        fm = cutw(NT)
        mgT = cutw(L)[0:NE, :]
        sta = cutw(NT * 6).rearrange("p (t s) -> p t s", t=NT)
        mva = cutw(NT * 2).rearrange("p (t s) -> p t s", t=NT)
        mvb = cutw(NT * 2).rearrange("p (t s) -> p t s", t=NT)
        rsa, rsa0, rsb, rsb0 = cutw(NT), cutw(NT), cutw(NT), cutw(NT)
        scaled = [x.rearrange("p h n -> p (h n)").rearrange("p (e d) -> p e d", e=NE) for x in (ab, rl)]
        pk_sb = at[:, 0:NODES * PKC].rearrange("p (c n) -> p c n", c=NODES)
        po_sb = at[:, NODES * PKC:NODES * (PKC + WN)].rearrange("p (c n) -> p c n", c=NODES)
        bv_sb = at[:, NODES * (PKC + WN):NODES * (PKC + WN + 1)]
        wv = lambda c, n: pk_sb[:, c, PK.index(n) * P:(PK.index(n) + 1) * P]
        vec = lambda c, i: pk_sb[:, c, len(PK) * P + i:len(PK) * P + i + 1]

        bx0, bx1 = bank_x[:, 0, :], bank_x[:, 1, :]
        sec = lambda t, h: t[:, h * 512:(h + 1) * 512]

        s_w = sem("weights_in")
        s_id = sem("identity_ready")
        s_c = sem("constants_ready")
        N_W = 16

        block = ctx.enter_context(nc.Block())
        S = {}
        credit = []

        def now(e, name, b, n=1, k=None):
            e.wait_ge(S[name], n * b + (n if k is None else k) + 1)

        def before(e, name, b, n=1):
            e.wait_ge(S[name], n * b + 1)

        def names(prefix, *ns):
            for n in ns:
                S[prefix + n] = sem(prefix + n)
                if prefix in ("a_", "b_", "f_"):
                    credit.append(S[prefix + n])

        passed = sem("wait_passed")
        names("p_", "ev", "in", "mm", "out")
        names("a_", "x", "mv", "rs", "rs_link", "hn", "hT_ps", "hT_ev", "win_ps", "xs_ev", "tg", "g_ev", "yh", "th", "xs", "z_ps", "z_ev",
              "ab", "ln", "sp", "mb_ps", "mb_ev", "dB_out", "link", "link2")
        names("r_", "A", "bx", "dA", "hs", "in", "out")
        names("b_", "x", "hs", "c_ps", "y", "yo_ps", "mv", "rs", "rs_link", "x1", "xT_ps", "xT_ev", "lg_ps", "lg", "ex", "mg", "mgT_ps",
              "mgT_ev", "yb_ps", "acc", "e_ps", "sc", "red", "mv2", "rs2", "rs2_link", "x2", "x2T_ps", "x2T_ev", "out", "outT",
              "link", "link2")
        names("f_", "n_in", "x3_in", "tT_ps", "tT_ev", "mv", "rs", "rs_link", "nm", "z", "mv2", "rs2", "rs2_link", "y", "out", "link", "link2")
        names("c_", "qk0", "qk1", "v0", "v1", "o0", "o1", "kh_ps", "qh_ps", "qT_ps", "v_ps", "ot_ps", "mT_ps", "wo_ps", "cT_ps", "x3T_ps",
              "kf_ev", "qf_ev", "q_ev", "v_ev", "ot_ev", "mT_ev", "pv_ev", "cT_ev", "wo_ev", "x3T_ev", "sp", "stk0", "stk1", "stk2",
              "stk3", "m_dma", "s_ps", "red", "nm_ok", "st_ps", "ex", "pv_ps", "store", "link", "pool", "sum", "xlink", "plink",
              "x2in", "x3", "x3out", "mv", "rs", "ones")

        class Kind:
            pass

        UC, U = 2 * NB, 2 * NB + NODES * NB
        QC, QU = UC // RING, U // RING
        kc, kn = Kind(), Kind()
        kc.node, kc.hd, kc.terms, kc.loads_qk, kc.loads_v = False, 8, TERMS_8, 1, 1
        kn.node, kn.hd, kn.terms, kn.loads_qk, kn.loads_v = True, 16, TERMS_16, 3, 2
        for c in (kc, kn):
            c.R = len(c.terms) * c.hd
            c.R3 = c.R + 3
            c.np_ = HU * c.hd
            c.scale = float(c.hd) ** -0.5

        def at_(c, q, r):
            x = Kind()
            x.q, x.r = q + r // RING, r % RING
            x.u = RING * x.q + x.r
            if isinstance(q, int):
                if not 0 <= x.u < U:
                    return None
                c = kc if x.u < UC else kn
            x.c, x.un = c, x.u - UC
            x.b = 2 * x.q + x.r // 2
            x.half = x.r % 2
            x.turn = x.q - QC * c.node
            return x

        def only(x, node):
            return x if x is not None and x.c.node == node else None

        def units(e, body):
            for r in range(RING):
                body(kc, 0, r)
            with e.Fori(1, QC - 1) as it:
                for r in range(RING):
                    body(kc, it, r)
            for q in (QC - 1, QC):
                for r in range(RING):
                    body(None, q, r)
            with e.Fori(QC + 1, QU - 1) as it:
                for r in range(RING):
                    body(kn, it, r)
            for r in range(RING):
                body(kn, QU - 1, r)

        def stacked(x):
            n = 16 * 2 * len(x.c.terms) * (x.turn + 1)
            return n + 16 * 2 * len(kc.terms) * QC if x.c.node else n

        def loaded(x, n_node, n_first=1):
            n = 2 * x.turn + x.r // 2 + 1
            return 16 * (n_node * n + n_first * 2 * QC) if x.c.node else 16 * n_first * n

        def led(c, q, r, k, i):
            for j in range(2):
                if i < 2:
                    yield (at_(c, q, r), 1, 12 + 2 * i + j) if k == 0 else (at_(c, q, r + 1), 0, 12 + 2 * i + j)
                else:
                    yield at_(c, q, r + 1), k, 2 * (i - 2) + j

        def led_group(c, q, r, k):
            return (at_(c, q, r), 1) if k == 0 else (at_(c, q, r + 1), 0)

        def staged(e, body, depth):
            for b in range(depth - 1):
                body(b)
            with e.Fori(depth - 1, NB) as it:
                body(it)
            for b in range(NB, NB + depth - 1):
                body(b)

        def batch(b):
            return not isinstance(b, int) or 0 <= b < NB

        @block.sync
        def _(sp):
            for dst, src in ((cv[:, :, :], a["cv"]), (gb[:, :], a["gb"]), (alog[:, :], a["alog"]),
                             (w_in[:, :], a["w_in"]), (wd[:, :, :], a["wd"]), (w_out[:, :, :], a["w_out"]),
                             (bmt[:, :, :], a["bmt"]), (cmt[:, :], a["cmt"]), (rw[:, :], a["rw"]),
                             (rb[:, :], a["rb"]), (xw[:, :], a["xw"]), (xb[:, :], a["xb"]),
                             (wc[:, 0:2, :], a["wckq"]), (wc[:, 2, :], a["wcv"]),
                             (lngb[:, 0, :], a["lng"]), (lngb[:, 1, :], a["lnb"])):
                sp.dma_start(dst, src).then_inc(s_w, 16)

            def row(t, i):
                return t[bass.ds(i, 1)].rearrange("o p n -> (o p) n")

            def when(*waits):
                for x, v in waits:
                    need(sp, x, v)
                    if not isinstance(v, int):
                        sp.sem_inc(passed, 1)

            sp.dma_start(pk_sb, a["pk"].rearrange("c p n -> p c n")).then_inc(S["p_in"], 16)

            def tokens(t, i):
                return t[bass.ds(i, 1)].rearrange("o (t p) d -> p (o t) d", p=P)

            def body(b):
                if batch(b):
                    when((S["a_hn"], b + 1))
                    sp.dma_start(xt, tokens(a["x"], b)).then_inc(S["a_x"], 16)
                b = b - 1
                if batch(b):
                    when((S["a_mb_ev"], b + 2))
                    for t, first in ((0, COL), (1, 0)):
                        sp.dma_start(dB_d[bass.ds(b, 1)][:, :, t, :].rearrange("o n l -> (o n) l"),
                                     dbx[first:first + NS, :]).then_inc(S["a_dB_out"], 16)
            staged(sp, body, 2)
            sp.wait_ge(S["a_dB_out"], 32 * NB + 1)
            sp.dma_start(db, dB_d.rearrange("b n t l -> (b n) t l")).then_inc(S["r_in"], 16)
            sp.wait_ge(S["p_ev"], 2)
            sp.dma_start(w_d.rearrange("c p n -> p c n"), po_sb).then_inc(S["p_out"], 16)
            sp.wait_ge(S["r_hs"], 1)
            sp.dma_start(hs_d.rearrange("b n l -> (b n) l"), hs).then_inc(S["r_out"], 16)
            sp.wait_ge(S["r_out"], 16)
            def body(b):
                if batch(b):
                    when((S["b_mv"], b + 1), (S["b_c_ps"], 2 * b + 1))
                    sp.dma_start(xt, tokens(a["x"], b)).then_inc(S["b_x"], 16)
                    sp.dma_start(hsb, row(hs_d, b)).then_inc(S["b_hs"], 16)
                b = b - 2
                if batch(b):
                    when((S["b_x2"], b + 2))
                    sp.dma_start(row(x2_d, b), x2w).then_inc(S["b_out"], 16)
                    when((S["b_x2T_ev"], b + 2))
                    sp.dma_start(row(x2T_d, b), x2Tw).then_inc(S["b_outT"], 16)
            staged(sp, body, 3)
            sp.wait_ge(S["b_out"], 16 * NB + 1)
            sp.wait_ge(S["b_outT"], 16 * NB + 1)
            sp.wait_ge(S["p_out"], 16)
            sp.wait_ge(S["c_ones"], 3)

            def load_qk(x):
                if x is None:
                    return
                t, done = st_qk[x.half], S[f"c_qk{x.half}"]
                when((S["c_kh_ps"], x.u - 1), *[(S["c_qh_ps"], x.un - 1)] * x.c.node)
                if x.c.node:
                    when((S["c_store"], 16 * (x.un + 1)))
                    sp.dma_start(t[:, 0:WA], row(w_d, x.un // NB)[:, 0:WA]).then_inc(done, 16)
                    sp.dma_start(t[:, WA:WA + L], row(nodes_d, x.un)).then_inc(done, 16)
                    sp.dma_start(t[:, WA + L:WA + 2 * L], row(nodes_d, (x.un // 40) * NB + x.un % NB)).then_inc(done, 16)
                else:
                    sp.dma_start(t[:, WA:WA + L], row(x2T_d, x.u // 2)).then_inc(done, 16)

            def load_v(x):
                if x is None:
                    return
                t, done = st_v[x.half], S[f"c_v{x.half}"]
                when((S["c_v_ev"], x.u - 1))
                if x.c.node:
                    when((S["c_store"], 16 * (x.un + 1)))
                    sp.dma_start(t[:, 0:P], row(w_d, x.un // NB)[:, WA:WA + P]).then_inc(done, 16)
                    sp.dma_start(t[:, P:P + L], row(nodes_d, ((x.un // NB + 1) // 2) * NB + x.un % NB)).then_inc(done, 16)
                else:
                    sp.dma_start(t[:, P:P + L], row(x2T_d, x.u // 2)).then_inc(done, 16)

            def load_o(x):
                x = only(x, True)
                if x is None:
                    return
                when((S["c_wo_ev"], x.un - 1))
                sp.dma_start(st_o[x.half], row(w_d, x.un // NB)[:, WA + P:WN]).then_inc(S[f"c_o{x.half}"], 16)

            def stack(x):
                if x is None:
                    return
                n = x.c.np_
                done = S[f"c_stk{x.r}"]
                k_parts, q_parts = (kp_, qp) if x.c.node else (kp_[0:n], kp_[n:2 * n])
                when((S["c_ex"], 16 * (x.u - RING + 1)), (S["c_sp"], 2 * x.u + 1))
                for i, (_, part) in enumerate(x.c.terms):
                    sp.dma_start(kst[i * x.c.hd:(i + 1) * x.c.hd, x.r, :, :], k_parts[0:n, part, :]).then_inc(done, 16)
                when((S["c_sp"], 2 * x.u + 2))
                for i, (part, _) in enumerate(x.c.terms):
                    sp.dma_start(qst[i * x.c.hd:(i + 1) * x.c.hd, x.r, :, :], q_parts[0:n, part, :]).then_inc(done, 16)

            def store(x):
                x = only(x, True)
                if x is None:
                    return
                when((S["c_store"], 16 * (NB + x.un)), (S["c_wo_ev"], x.un + 1))
                sp.dma_start(row(nodes_d, x.un + NB), no_sb).then_inc(S["c_store"], 16)

            def store_x3(x):
                x = only(x, False)
                if x is None or not x.half:
                    return
                when((S["c_store"], 16 * x.b), (S["c_x3T_ev"], x.b + 1))
                sp.dma_start(row(nodes_d, x.b), no_sb).then_inc(S["c_store"], 16)
                sp.dma_start(row(x3_d, x.b), x3s).then_inc(S["c_x3out"], 16)

            def load_x2(x):
                x = only(x, False)
                if x is None or not x.half:
                    return
                when((S["c_x3"], x.b))
                sp.dma_start(x2s, row(x2_d, x.b)).then_inc(S["c_x2in"], 16)

            load_qk(at_(kc, 0, 0))
            load_qk(at_(kc, 0, 1))
            load_v(at_(kc, 0, 0))
            stack(at_(kc, 0, 0))
            load_v(at_(kc, 0, 1))
            load_qk(at_(kc, 0, 2))
            stack(at_(kc, 0, 1))
            load_qk(at_(kc, 0, 3))
            stack(at_(kc, 0, 2))

            def body(c, q, r):
                load_qk(at_(c, q, r + 4))
                load_v(at_(c, q, r + 2))
                load_x2(at_(c, q, r))
                store(at_(c, q, r - 1))
                load_o(at_(c, q, r + 1))
                stack(at_(c, q, r + 3))
                store_x3(at_(c, q, r - 1))
            units(sp, body)
            store(at_(kn, QU - 1, RING - 1))
            sp.wait_ge(S["c_store"], 16 * (NB + NODES * NB))
            sp.wait_ge(S["c_x3out"], 16 * NB)

            def body(b):
                if batch(b):
                    when((S["f_tT_ps"], b + 1))
                    sp.dma_start(no_sb, row(nodes_d, b + NODES * NB)).then_inc(S["f_n_in"], 16)
                b = b - 1
                if batch(b):
                    when((S["f_z"], b + 1))
                    sp.dma_start(x2s, row(x3_d, b)).then_inc(S["f_x3_in"], 16)
                b = b - 1
                if batch(b):
                    when((S["f_y"], b + 2))
                    sp.dma_start(tokens(a["out"], b), x3s.rearrange("p (t d) -> p t d", t=NT)).then_inc(S["f_out"], 16)
            staged(sp, body, 3)
            sp.wait_ge(S["f_out"], 16 * NB + 1)

        @block.gpsimd
        def _(pool):
            for x in credit:
                pool.sem_inc(x, 1)
            pool.memset(ident[:, :], 0.0).then_inc(s_id, 1)
            pool.memset(identb[:, :], 0.0).then_inc(s_id, 1)
            pool.memset(half[:, :], -0.5).then_inc(s_c, 1)
            pool.memset(eps_ln[:, :], EPS_LN).then_inc(s_c, 1)
            pool.memset(eps_node[:, :], EPS_NODE).then_inc(s_c, 1)
            pool.memset(mean_w[:, :], 1.0 / DI).then_inc(s_c, 1)
            pool.memset(cbuf[:, :, 0:KC], 0.0).then_inc(s_c, 1)
            for e_ in range(NE):
                pool.memset(rank[:, e_:e_ + 1], float(NE - e_)).then_inc(s_c, 1)
            pool.wait_ge(s_id, 2)
            for m in (ident, identb):
                pool.affine_select(out=m[:, :], in_=m[:, :], compare_op=ALU.not_equal, fill=1.0, base=0,
                                   pattern=[[-1, P]], channel_multiplier=1).then_inc(s_id, 1)
            pool.wait_ge(s_c, 5 + NE)

            def rstd(mv_, t0, t1, eps, ready, link, done):
                pool.wait_ge(*ready)
                pool.tensor_tensor(t0, mv_[:, :, 1], eps, ALU.add).then_inc(link[0], 1)
                pool.wait_ge(*link)
                pool.tensor_tensor(t1, t0, half[:, :], ALU.pow).then_inc(done, 1)

            with pool.Fori(0, NB) as b:
                rstd(mva, rsa0, rsa, eps_ln[:, :], (S["a_mv"], b + 2), (S["a_rs_link"], b + 2), S["a_rs"])

            def body(b):
                if batch(b):
                    rstd(mva, rsa0, rsa, eps_ln[:, :], (S["b_mv"], b + 2), (S["b_rs_link"], b + 2), S["b_rs"])
                b = b - 1
                if batch(b):
                    rstd(mvb, rsb0, rsb, eps_ln[:, :], (S["b_mv2"], b + 2), (S["b_rs2_link"], b + 2), S["b_rs2"])
            staged(pool, body, 2)

            pool.wait_ge(S["b_x2T_ev"], NB + 1)
            pool.wait_ge(S["b_out"], 16 * NB + 1)
            pool.wait_ge(S["b_outT"], 16 * NB + 1)
            pool.memset(kst[64:P, :, :, :], 1.0).then_inc(S["c_ones"], 1)
            for j in range(2):
                pool.wait_ge(S["c_ones"], j + 1)
                pool.memset(vaug[j], 1.0).then_inc(S["c_ones"], 1)
            pool.wait_ge(S["c_ones"], 3)

            def in_parts(src, dst, base, done, n):
                pool.tensor_copy(dst[:, 0, :], src).then_inc(S["c_pool"], 1)
                need(pool, S["c_pool"], base + 1)
                pool.tensor_tensor(src, src, dst[:, 0, :], ALU.subtract).then_inc(S["c_pool"], 1)
                need(pool, S["c_pool"], base + 2)
                pool.sem_inc(passed, 1)
                pool.tensor_copy(dst[:, 1, :], src).then_inc(S["c_pool"], 1)
                need(pool, S["c_pool"], base + 3)
                pool.tensor_tensor(dst[:, 2, :], src, dst[:, 1, :], ALU.subtract).then_inc(done, n)

            def split(x):
                if x is None:
                    return
                base = 3 * UC + 6 * x.un if x.c.node else 3 * x.u
                before_ = at_(x.c, x.q, x.r - 1)
                if before_ is not None:
                    need(pool, S[f"c_stk{before_.r}"], stacked(before_))
                need(pool, S["c_kf_ev"], x.u + 1)
                pool.sem_inc(passed, 1)
                in_parts(kf, kp_, base, S["c_sp"], 1 if x.c.node else 2)
                if x.c.node:
                    need(pool, S["c_qf_ev"], x.un + 1)
                    pool.sem_inc(passed, 1)
                    in_parts(qf, qp, base + 3, S["c_sp"], 1)

            def residual_rstd(x):
                x = only(x, False)
                if x is None or not x.half:
                    return
                rstd(mv, rs0, rs, eps_ln[:, :], (S["c_mv"], x.b + 1), (S["c_plink"], x.b + 1), S["c_rs"])

            split(at_(kc, 0, 0))
            split(at_(kc, 0, 1))
            split(at_(kc, 0, 2))

            def body(c, q, r):
                residual_rstd(at_(c, q, r - 1))
                split(at_(c, q, r + 3))
            units(pool, body)

            def body(b):
                if batch(b - 1):
                    rstd(mv2, rs20, rs2, eps_ln[:, :], (S["f_mv2"], b + 1), (S["f_rs2_link"], b + 1), S["f_rs2"])
                if batch(b):
                    rstd(mv, rs0, rs, eps_node[:, :], (S["f_mv"], b + 2), (S["f_rs_link"], b + 2), S["f_rs"])
            staged(pool, body, 2)

        @block.scalar
        def _(act):
            act.wait_ge(s_w, 16 * N_W)
            act.activation(aneg[:, 0:1], alog[:, :], ACT.Exp).then_inc(S["r_A"], 1)
            act.wait_ge(S["r_A"], 1)
            act.activation(aneg[:, 1:2], aneg[:, 0:1], ACT.Copy, scale=-1.0).then_inc(S["r_A"], 1)

            def body(b):
                b0, b1 = b, b - 1
                if batch(b1):
                    now(act, "a_yh", b1)
                    before(act, "a_sp", b1)
                    act.activation(ab, yh, ACT.Tanh).then_inc(S["a_th"], 1)
                if batch(b0):
                    now(act, "a_hT_ps", b0)
                    before(act, "a_win_ps", b0)
                    act.activation(hT, bank_m[:, :], ACT.Identity, bias=gb[:, 1:2], scale=gb[:, 0:1]).then_inc(S["a_hT_ev"], 1)
                if batch(b1):
                    now(act, "a_z_ev", b1, NH)
                    now(act, "a_xs", b1)
                    act.activation(ab, rl, ACT.Abs).then_inc(S["a_ab"], 1)
                    now(act, "a_ab", b1, 2, 1)
                    act.activation(ab, ab, ACT.Exp, scale=-1.0).then_inc(S["a_ab"], 1)
                    now(act, "a_ab", b1, 2)
                    act.activation(ab, ab, ACT.Ln, bias=1.0).then_inc(S["a_ln"], 1)
                if batch(b0):
                    now(act, "a_win_ps", b0)
                    before(act, "a_yh", b0)
                    act.activation(cbuf[:, :, KC:KC + L], bx0.rearrange("p (h n) -> p h n", h=NH), ACT.Copy).then_inc(S["a_xs_ev"], 1)
                    before(act, "a_g_ev", b0)
                    act.activation(tg, bx1.rearrange("p (h n) -> p h n", h=NH), ACT.Tanh, scale=0.5).then_inc(S["a_tg"], 1)
                if batch(b1):
                    now(act, "a_mb_ps", b1)
                    before(act, "a_dB_out", b1, 32)
                    act.activation(dbx[0:NS, :], bank_o[0:NS, :], ACT.Copy)
                    act.activation(dbx[COL:COL + NS, :], bank_o[COL:COL + NS, :], ACT.Copy).then_inc(S["a_mb_ev"], 1)
            staged(act, body, 2)
            act.wait_ge(S["r_in"], 16)
            act.wait_ge(S["r_A"], 2)
            act.activation(hn, db[:, 0, :], ACT.Exp, scale=aneg[:, 1:2]).then_inc(S["r_dA"], 1)

            def scale(b, t):
                now(act, "b_e_ps", b, NT, t + 1)
                need(act, S["b_red"], NT * b + t)
                for e_ in range(NE):
                    i = act.activation(scaled[t % 2][:, e_, :], bank_x[:, t % 2, e_ * D:(e_ + 1) * D], ACT.Identity, scale=lgm[:, t, e_:e_ + 1])
                i.then_inc(S["b_sc"], 1)

            def body(b):
                b1, b2 = b - 1, b - 2
                if batch(b1):
                    now(act, "b_xT_ps", b1)
                    before(act, "b_e_ps", b1, NT)
                    act.activation(hT, bank_m[:, :], ACT.Copy).then_inc(S["b_xT_ev"], 1)
                    now(act, "b_lg", b1)
                    before(act, "b_mg", b1)
                    for t in range(NT):
                        act.activation(lge[:, t, :], lg[:, t, :], ACT.Exp, bias=nmx[:, t:t + 1],
                                       accum_out=sm[:, t:t + 1]).then_inc(S["b_ex"], 1)
                    now(act, "b_mg", b1)
                    scale(b1, 0)
                    now(act, "b_mgT_ps", b1)
                    before(act, "b_yb_ps", b1)
                    act.activation(mgT, bank_m[0:NE, :], ACT.Copy).then_inc(S["b_mgT_ev"], 1)
                    for t in range(1, NT):
                        scale(b1, t)
                if batch(b2):
                    now(act, "b_x2T_ps", b2)
                    before(act, "b_outT", b2, 16)
                    act.activation(x2Tw, bank_m[:, :], ACT.Copy).then_inc(S["b_x2T_ev"], 1)
            staged(act, body, 3)

            def ev_qT(x):
                x = only(x, True)
                if x is None:
                    return
                need(act, S["c_qT_ps"], x.un + 1)
                need(act, S["c_wo_ev"], x.un - RING + 1)
                act.activation(q_sb[x.r], bank_m[:, :], ACT.Identity, bias=st_qk[x.half][:, 3 * P:3 * P + 1]).then_inc(S["c_q_ev"], 1)

            def ev_kh(x):
                if x is None:
                    return
                need(act, S["c_kh_ps"], x.u + 1)
                if x.c.node:
                    need(act, S["c_sp"], 2 * x.u - 1)
                    act.activation(kf, bank_m[:, :], ACT.Identity, bias=st_qk[x.half][:, 3 * P + 1:WA]).then_inc(S["c_kf_ev"], 1)
                else:
                    need(act, S["c_sp"], 2 * x.u)
                    act.activation(kf, bank_m[:, :], ACT.Copy).then_inc(S["c_kf_ev"], 1)

            def ev_qh(x):
                x = only(x, True)
                if x is None:
                    return
                need(act, S["c_qh_ps"], x.un + 1)
                need(act, S["c_sp"], 2 * x.u)
                act.activation(qf, bank_m[:, :], ACT.Copy).then_inc(S["c_qf_ev"], 1)

            def ev_v(x):
                if x is None:
                    return
                need(act, S["c_v_ps"], x.u + 1)
                need(act, S["c_pv_ps"], 4 * (x.u - 2) + 4)
                act.activation(vaug[x.half][:, :, :, 0:x.c.hd],
                               bank_m[:, 0:NT * x.c.np_].rearrange("p (k h m) -> p k h m", k=NT, h=HU), ACT.Copy).then_inc(S["c_v_ev"], 1)

            def ev_m(x, k):
                if x is None:
                    return
                G = 2 * x.u + k
                need(act, S["c_mT_ps"], G + 1)
                need(act, S["c_m_dma"], 16 * G)
                act.activation(mT[0:48, :], bank_m[0:48, 0:P], ACT.Copy).then_inc(S["c_mT_ev"], 1)
                need(act, S["c_mT_ev"], G + 1)
                act.dma_start(qst[x.c.R:x.c.R3, x.r, GH * k:GH * k + GH, :], mT[0:48, :]).then_inc(S["c_m_dma"], 16)

            def ev_pv(x, k):
                if x is None:
                    return
                G = 2 * x.u + k
                need(act, S["c_pv_ps"], 2 * G + 2)
                need(act, S["c_ot_ps"], G)
                act.activation(ot_sb, bank_o[:, :], ACT.Copy).then_inc(S["c_pv_ev"], 1)

            def ev_cT(x):
                x = only(x, True)
                if x is None:
                    return
                need(act, S["c_cT_ps"], x.un + 1)
                need(act, S["c_wo_ps"], x.un)
                act.activation(ctxT, bank_m[:, :], ACT.Copy).then_inc(S["c_cT_ev"], 1)

            def ev_x3T(x):
                x = only(x, False)
                if x is None or not x.half:
                    return
                need(act, S["c_x3T_ps"], x.b + 1)
                need(act, S["c_store"], 16 * x.b)
                act.activation(no_sb, bank_m[:, :], ACT.Copy).then_inc(S["c_x3T_ev"], 1)

            def exp(x, k, i):
                G = 2 * x.u + k
                kp, h = i // GH, i % GH
                need(act, S["c_st_ps"], 8 * G + i + 1)
                if h == 0:
                    need(act, S["c_pv_ps"], 2 * (G - 1) + kp + 1)
                act.activation(PT[:, kp, h, :, :], bank_x[:, i % 2, :].rearrange("p (c n) -> p c n", c=2),
                               ACT.Exp, scale=x.c.scale).then_inc(S["c_ex"], 1)

            ev_kh(at_(kc, 0, 0))
            ev_v(at_(kc, 0, 0))
            ev_kh(at_(kc, 0, 1))
            ev_m(at_(kc, 0, 0), 0)
            ev_kh(at_(kc, 0, 2))

            def body(c, q, r):
                x, last, ahead = at_(c, q, r), at_(c, q, r - 1), at_(c, q, r + 3)
                for i in range(8):
                    exp(x, 0, i)
                    if i == 1:
                        ev_pv(last, 1)
                    if i == 2:
                        ev_v(at_(c, q, r + 1))
                    if i == 5:
                        ev_m(*led_group(c, q, r, 0))
                    if i == 6:
                        ev_cT(last)
                for i in range(8):
                    exp(x, 1, i)
                    if i == 1:
                        ev_pv(x, 0)
                    if i == 2:
                        ev_qT(ahead)
                    if i == 5:
                        ev_m(*led_group(c, q, r, 1))
                    if i == 6:
                        ev_kh(ahead)
                    if i == 7:
                        ev_qh(ahead)
                        ev_x3T(last)
            units(act, body)
            end = at_(kn, QU - 1, RING - 1)
            ev_pv(end, 1)
            ev_cT(end)

            with act.Fori(0, NB) as b:
                now(act, "f_tT_ps", b)
                before(act, "f_nm", b)
                act.activation(ctxT, bank_m[:, :], ACT.Copy).then_inc(S["f_tT_ev"], 1)

        @block.tensor
        def _(pe):
            pe.wait_ge(s_id, 4)
            pe.wait_ge(s_w, 16 * N_W)
            xs_at = lambda b, h: xs_all[:, bass.ds((b * NH + h) * L, L)]

            def body(b):
                b0, b1 = b, b - 1
                if batch(b0):
                    now(pe, "a_hn", b0)
                    before(pe, "a_hT_ev", b0)
                    for t in range(NT):
                        mm = pe.transpose(bank_m[:, t * P:(t + 1) * P], hn[:, t * P:(t + 1) * P], ident[:, :])
                    mm.then_inc(S["a_hT_ps"], 1)
                if batch(b1):
                    now(pe, "a_xs", b1)
                    before(pe, "a_z_ev", b1, NH)
                    for h in range(NH):
                        for k in range(NH):
                            mm = pe.matmul(bank_s[:, h, :], wd[:, k, h * P:(h + 1) * P], xs_at(b1, k),
                                           start=(k == 0), stop=(k == NH - 1))
                    mm.then_inc(S["a_z_ps"], 1)
                if batch(b0):
                    now(pe, "a_hT_ev", b0)
                    before(pe, "a_xs_ev", b0)
                    before(pe, "a_g_ev", b0)
                    for j in range(2 * NH):
                        mm = pe.matmul(sec(bank_x[:, j // NH, :], j % NH), w_in[:, j * P:(j + 1) * P], hT, start=True, stop=True)
                    mm.then_inc(S["a_win_ps"], 1)
                if batch(b1):
                    now(pe, "a_sp", b1)
                    before(pe, "a_mb_ev", b1)
                    for k in range(NH):
                        pe.matmul(bank_o[COL:COL + NS, :], mean_w[:, :], rl[:, k, :], start=(k == 0), stop=(k == NH - 1))
                        mm = pe.matmul(bank_o[0:NS, :], bmt[:, k, :], xs_at(b1, k), start=(k == 0), stop=(k == NH - 1))
                    mm.then_inc(S["a_mb_ps"], 1)
            staged(pe, body, 2)

            pe.wait_ge(S["p_in"], 16)
            pe.wait_ge(S["a_g_ev"], NB + 1)
            pe.wait_ge(S["a_z_ev"], NH * NB + 1)
            for c in range(NODES):
                pe.matmul(bx0[:, c * P:(c + 1) * P], wv(c, "WeKT"), wv(c, "WkP"), start=True, stop=True)
                pe.matmul(bx1[:, c * P:(c + 1) * P], wv(c, "WeVT"), wv(c, "Wv"), start=True, stop=True)
                pe.matmul(bank_s[:, 0, c:c + 1], wv(c, "WkP"), vec(c, 1), start=True, stop=True)
                mm = pe.matmul(bank_s[:, 0, NODES + c:NODES + c + 1], wv(c, "Wv"), vec(c, 2), start=True, stop=True)
            mm.then_inc(S["p_mm"], 1)
            pe.wait_ge(S["p_ev"], 1)
            for c in range(NODES):
                mm = pe.matmul(bank_s[:, 1, c:c + 1], po_sb[:, c, WA + P:WA + 2 * P], bv_sb[:, c:c + 1], start=True, stop=True)
            mm.then_inc(S["p_mm"], 1)

            def experts(b, t):
                need(pe, S["b_sc"], NT * b + t)
                for j in range(2):
                    mm = pe.matmul(sec(bank_x[:, t % 2, :], j), hT[:, t * P:(t + 1) * P], xw[:, j * 512:(j + 1) * 512],
                                   start=True, stop=True)
                mm.then_inc(S["b_e_ps"], 1)

            def states(b, h):
                pe.matmul(bank_s[:, h, :], cmt[:, h * P:(h + 1) * P], hsb, start=True, stop=True).then_inc(S["b_c_ps"], 1)

            def body(b):
                b0, b1, b2 = b, b - 1, b - 2
                if batch(b1):
                    now(pe, "b_x1", b1)
                    need(pe, S["b_x2T_ev"], b1)
                    for t in range(NT):
                        mm = pe.transpose(bank_m[:, t * P:(t + 1) * P], hn[:, t * P:(t + 1) * P], ident[:, :])
                    mm.then_inc(S["b_xT_ps"], 1)
                if batch(b0):
                    now(pe, "b_hs", b0, 16)
                    before(pe, "b_y", b0)
                    need(pe, S["b_acc"], b0)
                    states(b0, 0)
                if batch(b1):
                    now(pe, "b_xT_ev", b1)
                    for t in range(NT):
                        mm = pe.matmul(bank_m[:, t * NE:(t + 1) * NE], hT[:, t * P:(t + 1) * P], rw[:, :], start=True, stop=True)
                    mm.then_inc(S["b_lg_ps"], 1)
                if batch(b0):
                    states(b0, 1)
                if batch(b1):
                    experts(b1, 0)
                    experts(b1, 1)
                if batch(b0):
                    now(pe, "b_y", b0)
                    before(pe, "b_mv", b0)
                    for t in range(NT):
                        for k in range(NH):
                            mm = pe.matmul(bank_o[:, t * P:(t + 1) * P], yh[:, k, t * P:(t + 1) * P], woh[:, k, :],
                                           start=(k == 0), stop=(k == NH - 1))
                    mm.then_inc(S["b_yo_ps"], 1)
                if batch(b1):
                    now(pe, "b_mg", b1)
                    for t in range(NT):
                        mm = pe.transpose(bank_m[0:NE, t * P:(t + 1) * P], lgm[:, t, :], ident[:, :])
                    mm.then_inc(S["b_mgT_ps"], 1)
                    experts(b1, 2)
                    now(pe, "b_mgT_ev", b1)
                    for t in range(NT):
                        mm = pe.matmul(bank_s[:, 0, t * P:(t + 1) * P], mgT[:, t * P:(t + 1) * P], xb[:, :], start=True, stop=True)
                    mm.then_inc(S["b_yb_ps"], 1)
                    experts(b1, 3)
                if batch(b2):
                    now(pe, "b_x2", b2)
                    before(pe, "b_x2T_ev", b2)
                    for t in range(NT):
                        mm = pe.transpose(bank_m[:, t * P:(t + 1) * P], x2w[:, t * P:(t + 1) * P], ident[:, :])
                    mm.then_inc(S["b_x2T_ps"], 1)
            staged(pe, body, 3)

            reader = [None]

            def misc(sem_, value):
                if reader[0] is not None:
                    need(pe, *reader[0])
                reader[0] = (sem_, value)

            def proj_q(x):
                x = only(x, True)
                if x is None:
                    return
                t = st_qk[x.half]
                need(pe, S[f"c_qk{x.half}"], loaded(x, kn.loads_qk))
                misc(S["c_q_ev"], x.un + 1)
                pe.matmul(bank_m[:, :], t[:, 0:P], t[:, WA:WA + L], start=True, stop=True).then_inc(S["c_qT_ps"], 1)

            def proj_kh(x):
                if x is None:
                    return
                t = st_qk[x.half]
                need(pe, S[f"c_qk{x.half}"], loaded(x, kn.loads_qk))
                misc(S["c_kf_ev"], x.u + 1)
                w, src = (t[:, 2 * P:3 * P], t[:, WA + L:WA + 2 * L]) if x.c.node else (wc[:, x.half, :], t[:, WA:WA + L])
                pe.matmul(bank_m[:, :], w, src, start=True, stop=True).then_inc(S["c_kh_ps"], 1)

            def proj_qh(x):
                x = only(x, True)
                if x is None:
                    return
                need(pe, S["c_q_ev"], x.un + 1)
                misc(S["c_qf_ev"], x.un + 1)
                pe.matmul(bank_m[:, :], st_qk[x.half][:, P:2 * P], q_sb[x.r], start=True, stop=True).then_inc(S["c_qh_ps"], 1)

            def value(x):
                if x is None:
                    return
                t, n = st_v[x.half], x.c.np_
                need(pe, S[f"c_v{x.half}"], loaded(x, kn.loads_v))
                misc(S["c_v_ev"], x.u + 1)
                w = t[:, 0:P] if x.c.node else wc[:, 2, x.half * n:(x.half + 1) * n]
                for k in range(NT):
                    mm = pe.matmul(bank_m[:, k * n:(k + 1) * n], t[:, P + k * P:P + (k + 1) * P], w, start=True, stop=True)
                mm.then_inc(S["c_v_ps"], 1)

            def scores(x, k, n):
                if x is None:
                    return
                N = 16 * (2 * x.u + k) + n
                if k == 0 and n == 0:
                    need(pe, S[f"c_stk{x.r}"], stacked(x))
                need(pe, S["c_red"], N - 1)
                h, t = GH * k + n // NT, n % NT
                pe.matmul(bank_s[:, n % 2, :], qst[0:x.c.R, x.r, h, t * P:(t + 1) * P], kst[0:x.c.R, x.r, h, :],
                          start=True, stop=True).then_inc(S["c_s_ps"], 1)

            def maxima(x, k):
                if x is None:
                    return
                G = 2 * x.u + k
                need(pe, S["c_nm_ok"], G + 1)
                misc(S["c_mT_ev"], G + 1)
                pe.matmul(bank_m[0:48, 0:P], mp[:, 0:48], identb[:, :], start=True, stop=True).then_inc(S["c_mT_ps"], 1)

            def scoresT(x, k, i):
                G = 2 * x.u + k
                kp, h = i // GH, GH * k + i % GH
                if i == 0:
                    need(pe, S["c_m_dma"], 16 * (G + 1))
                need(pe, S["c_ex"], 8 * G + i - 1)
                for j in range(2):
                    kc_ = 2 * kp + j
                    mm = pe.matmul(sec(bank_x[:, i % 2, :], j), kst[0:x.c.R3, x.r, h, kc_ * P:(kc_ + 1) * P],
                                   qst[0:x.c.R3, x.r, h, :], start=True, stop=True)
                mm.then_inc(S["c_st_ps"], 1)

            def output(x, k, kp, j):
                if x is None:
                    return
                G = 2 * x.u + k
                if j == 0:
                    need(pe, S["c_ex"], 8 * G + 4 * kp + 4)
                    if kp == 0:
                        need(pe, S["c_pv_ev"], G)
                        need(pe, S["c_v_ev"], x.u + 1)
                for h in range(GH):
                    mm = pe.matmul(bank_o[COL * h:COL * (h + 1), :], vaug[x.half][:, 2 * kp + j, GH * k + h, :],
                                   PT[:, kp, h, j, :], start=(kp == 0 and j == 0), stop=(kp == 1 and j == 1))
                if j == 1:
                    mm.then_inc(S["c_pv_ps"], 1)

            def turn(x, k):
                if x is None:
                    return
                G = 2 * x.u + k
                need(pe, S["c_pv_ev"], G + 1)
                misc(S["c_ot_ev"], G + 1)
                for t in range(NT):
                    mm = pe.transpose(bank_m[:, t * P:(t + 1) * P], ot_sb[:, t * P:(t + 1) * P], ident[:, :])
                mm.then_inc(S["c_ot_ps"], 1)

            def turn_ctx(x):
                x = only(x, True)
                if x is None:
                    return
                need(pe, S["c_ot_ev"], 2 * x.u + 2)
                misc(S["c_cT_ev"], x.un + 1)
                for t in range(NT):
                    mm = pe.transpose(bank_m[:, t * P:(t + 1) * P], ctx_sb[:, t * P:(t + 1) * P], ident[:, :])
                mm.then_inc(S["c_cT_ps"], 1)

            def out_proj(x):
                x = only(x, True)
                if x is None:
                    return
                need(pe, S[f"c_o{x.half}"], loaded(x, 1, 0))
                need(pe, S["c_cT_ev"], x.un + 1)
                misc(S["c_wo_ev"], x.un + 1)
                pe.matmul(bank_m[:, :], st_o[x.half][:, 0:P], ctxT, start=True, stop=True).then_inc(S["c_wo_ps"], 1)

            def turn_x3(x):
                x = only(x, False)
                if x is None or not x.half:
                    return
                need(pe, S["c_x3"], x.b + 1)
                misc(S["c_x3T_ev"], x.b + 1)
                for t in range(NT):
                    mm = pe.transpose(bank_m[:, t * P:(t + 1) * P], x3s[:, t * P:(t + 1) * P], ident[:, :])
                mm.then_inc(S["c_x3T_ps"], 1)

            pe.wait_ge(S["c_ones"], 3)
            pe.wait_ge(S["b_x2T_ev"], NB + 1)
            proj_kh(at_(kc, 0, 0))
            value(at_(kc, 0, 0))
            proj_kh(at_(kc, 0, 1))
            for n in range(16):
                scores(at_(kc, 0, 0), 0, n)
            maxima(at_(kc, 0, 0), 0)
            for n in range(12):
                scores(at_(kc, 0, 0), 1, n)
            proj_kh(at_(kc, 0, 2))

            def ring_reader(c, q):
                return (S["c_qf_ev"], RING * q + 3 - UC) if c.node else (S["c_kf_ev"], RING * q + 3)

            def body(c, q, r):
                x, last, ahead = at_(c, q, r), at_(c, q, r - 1), at_(c, q, r + 3)
                in_loop = not isinstance(q, int)
                if in_loop and r == 0:
                    reader[0] = ring_reader(c, q)
                for i in range(8):
                    scoresT(x, 0, i)
                    for group in led(c, q, r, 0, i):
                        scores(*group)
                    if i == 0:
                        output(last, 1, 1, 0)
                    if i == 1:
                        output(last, 1, 1, 1)
                    if i == 2:
                        value(at_(c, q, r + 1))
                    if i == 3:
                        turn(last, 1)
                    if i == 4:
                        output(x, 0, 0, 0)
                    if i == 5:
                        maxima(*led_group(c, q, r, 0))
                        output(x, 0, 0, 1)
                    if i == 6:
                        turn_ctx(last)
                    if i == 7:
                        out_proj(last)
                for i in range(8):
                    scoresT(x, 1, i)
                    for group in led(c, q, r, 1, i):
                        scores(*group)
                    if i == 0:
                        output(x, 0, 1, 0)
                    if i == 1:
                        output(x, 0, 1, 1)
                    if i == 2:
                        proj_q(ahead)
                    if i == 3:
                        turn(x, 0)
                    if i == 4:
                        output(x, 1, 0, 0)
                    if i == 5:
                        maxima(*led_group(c, q, r, 1))
                        output(x, 1, 0, 1)
                    if i == 6:
                        proj_kh(ahead)
                    if i == 7:
                        proj_qh(ahead)
                        turn_x3(last)
                if in_loop and r == RING - 1:
                    reader[0] = ring_reader(c, QU - 1 if c.node else QC - 1)
            units(pe, body)
            end = at_(kn, QU - 1, RING - 1)
            output(end, 1, 1, 0)
            output(end, 1, 1, 1)
            turn(end, 1)
            turn_ctx(end)
            out_proj(end)

            with pe.Fori(0, NB) as b:
                now(pe, "f_n_in", b, 16)
                before(pe, "f_tT_ev", b)
                for t in range(NT):
                    mm = pe.transpose(bank_m[:, t * P:(t + 1) * P], no_sb[:, t * P:(t + 1) * P], ident[:, :])
                mm.then_inc(S["f_tT_ps"], 1)

        @block.vector
        def _(dve):
            dve.wait_ge(s_w, 16 * N_W)
            dve.wait_ge(s_c, 5 + NE)
            dve.tensor_scalar(cvh[:, :, :], cv[:, :, 0:KC + 1], 0.5, None, ALU.mult).then_inc(s_c, 1)
            dve.tensor_scalar(woh[:, :, :], w_out[:, :, :], 0.5, None, ALU.mult).then_inc(s_c, 1)

            def stats(src, st_, mv_, link, base, done):
                for t in range(NT):
                    dve.bn_stats(st_[:, t, :], src[:, t * D:(t + 1) * D]).then_inc(link, 1)
                need(dve, link, base + NT)
                dve.sem_inc(passed, 1)
                for t in range(NT):
                    i = dve.bn_aggr(mv_[:, t, :], st_[:, t, :])
                i.then_inc(done, 1)

            def normalise(dst, src, mv_, rs_, done):
                for t in range(NT):
                    i = dve.tensor_scalar(dst[:, t * D:(t + 1) * D], src[:, t * D:(t + 1) * D], mv_[:, t, 0:1], rs_[:, t:t + 1],
                                          ALU.subtract, ALU.mult)
                i.then_inc(done, 1)

            class Links:

                def __init__(self, name, per, b):
                    self.sem, self.per, self.b, self.n = S[name], per, b, 0

                def count(self, ins):
                    self.n += 1
                    assert self.n <= self.per
                    return ins.then_inc(self.sem, 1)

                def base(self):
                    return self.per * self.b + 1 + self.n

                def wait(self, back=0):
                    dve.wait_ge(self.sem, self.base() - back)

            xtf = xt.rearrange("p t d -> p (t d)")
            halves = lambda t, b: t[:, bass.ds(b * NH * L, NH * L)]
            flat = lambda t: t.rearrange("p h n -> p (h n)")
            dve.wait_ge(s_c, 5 + NE + 2)

            def body(b):
                b0, b1 = b, b - 1
                if batch(b0):
                    now(dve, "a_x", b0, 16)
                    stats(xtf, sta, mva, S["a_link"], NT * b0 + 1, S["a_mv"])
                if batch(b1):
                    now(dve, "a_xs_ev", b1)
                    taps(Links("a_link2", NH * KC - 1, b1))
                if batch(b0):
                    now(dve, "a_rs", b0)
                    before(dve, "a_hT_ps", b0)
                    normalise(hn, xtf, mva, rsa, S["a_hn"])
                if batch(b1):
                    now(dve, "a_th", b1)
                    now(dve, "a_yh", b1)
                    dve.scalar_tensor_tensor(halves(xs_all, b1), flat(ab), 1.0, flat(yh), ALU.add, ALU.mult).then_inc(S["a_xs"], 1)
                    now(dve, "a_z_ps", b1)
                    before(dve, "a_mb_ps", b1)
                    for h in range(NH):
                        dve.tensor_scalar(rl[:, h, :], bank_s[:, h, :], cv[:, h, KC + 2:KC + 3], None, ALU.add).then_inc(S["a_z_ev"], 1)
                    now(dve, "a_ln", b1)
                    dve.scalar_tensor_tensor(rl, rl, 0.0, ab, ALU.max, ALU.add).then_inc(S["a_sp"], 1)
                if batch(b0):
                    now(dve, "a_tg", b0)
                    dve.scalar_tensor_tensor(halves(sg_all, b0), flat(tg), 1.0, bx1, ALU.add, ALU.mult).then_inc(S["a_g_ev"], 1)

            def taps(v):
                for j in range(KC):
                    for h in range(NH):
                        if j == 0:
                            i = dve.tensor_scalar(yh[:, h, :], cbuf[:, h, KC:KC + L], cvh[:, h, KC - 1:KC], cvh[:, h, KC:KC + 1],
                                                  ALU.mult, ALU.add)
                        else:
                            v.wait(1)
                            i = dve.scalar_tensor_tensor(yh[:, h, :], cbuf[:, h, KC - j:KC - j + L],
                                                         cvh[:, h, KC - 1 - j:KC - j], yh[:, h, :], ALU.mult, ALU.add)
                        if (j, h) == (KC - 1, NH - 1):
                            i.then_inc(S["a_yh"], 1)
                        else:
                            v.count(i)
            staged(dve, body, 2)

            dve.wait_ge(S["p_mm"], 1)
            for c in range(NODES):
                po = po_sb[:, c, :]
                dve.tensor_scalar(po[:, 0:P], wv(c, "WeQ"), vec(c, 3), None, ALU.mult)
                dve.tensor_copy(po[:, P:2 * P], wv(c, "WqP"))
                dve.tensor_scalar(po[:, 2 * P:3 * P], bx0[:, c * P:(c + 1) * P], vec(c, 4), None, ALU.mult)
                dve.tensor_scalar(po[:, 3 * P:3 * P + 1], vec(c, 0), vec(c, 3), None, ALU.mult)
                dve.tensor_scalar(po[:, 3 * P + 1:WA], bank_s[:, 0, c:c + 1], vec(c, 4), None, ALU.mult)
                dve.tensor_scalar(po[:, WA:WA + P], bx1[:, c * P:(c + 1) * P], vec(c, 5), None, ALU.mult)
                dve.tensor_scalar(bv_sb[:, c:c + 1], bank_s[:, 0, NODES + c:NODES + c + 1], vec(c, 5), None, ALU.mult)
                i = dve.tensor_scalar(po[:, WA + P:WA + 2 * P], wv(c, "Wo"), vec(c, 6), None, ALU.mult)
            i.then_inc(S["p_ev"], 1)

            dve.wait_ge(S["r_in"], 16)
            dve.tensor_tensor(hT, db[:, 1, :], db[:, 0, :], ALU.mult).then_inc(S["r_bx"], 1)
            dve.wait_ge(S["p_mm"], 2)
            dve.tensor_copy(po_sb[:, :, WN - 1], bank_s[:, 1, 0:NODES]).then_inc(S["p_ev"], 1)
            dve.wait_ge(S["r_dA"], 1)
            dve.wait_ge(S["r_bx"], 1)
            dve.tensor_tensor_scan(hs, hn, hT, 0.0, ALU.mult, ALU.add).then_inc(S["r_hs"], 1)

            def body(b):
                b0, b1, b2 = b, b - 1, b - 2
                A, B = Links("b_link", 2 + 1 + NT, b0), Links("b_link2", 7 + 1 + NT, b1)
                if batch(b1):
                    now(dve, "b_lg_ps", b1)
                    B.count(dve.tensor_tensor(lg, bank_m[:, 0:NT * NE].rearrange("p (t e) -> p t e", t=NT),
                                              rb[:, :].unsqueeze(1).broadcast_to([P, NT, NE]), ALU.add))
                    B.wait()
                    B.count(dve.tensor_reduce(mx, lg, AX.X, ALU.max))
                    B.wait()
                    dve.tensor_scalar(nmx, mx, -1.0, None, ALU.mult).then_inc(S["b_lg"], 1)
                    before(dve, "b_mgT_ps", b1)
                    before(dve, "b_sc", b1, NT)
                    B.count(dve.tensor_tensor(lgm, lg, mx.unsqueeze(2).broadcast_to([P, NT, NE]), ALU.is_equal))
                if batch(b0):
                    for h in range(NH):
                        now(dve, "b_c_ps", b0, 2, h + 1)
                        A.count(dve.scalar_tensor_tensor(yh[:, h, :], xs_all[:, bass.ds((b0 * NH + h) * L, L)], cv[:, h, KC + 1:KC + 2],
                                                         bank_s[:, h, :], ALU.mult, ALU.add))
                if batch(b1):
                    B.wait()
                    B.count(dve.tensor_tensor(lgm, lgm, rank[:, :].unsqueeze(1).broadcast_to([P, NT, NE]), ALU.mult))
                if batch(b0):
                    A.wait()
                    dve.tensor_tensor(flat(yh), flat(yh), halves(sg_all, b0), ALU.mult).then_inc(S["b_y"], 1)
                if batch(b1):
                    B.wait()
                    B.count(dve.tensor_reduce(fm, lgm, AX.X, ALU.max))
                    B.wait()
                    B.count(dve.tensor_tensor(lgm, lgm, fm.unsqueeze(2).broadcast_to([P, NT, NE]), ALU.is_equal))
                    now(dve, "b_ex", b1, NT)
                    B.count(dve.reciprocal(mx, sm))
                    B.wait()
                    dve.tensor_tensor(lgm, lgm, mx.unsqueeze(2).broadcast_to([P, NT, NE]), ALU.mult).then_inc(S["b_mg"], 1)
                if batch(b2):
                    now(dve, "b_rs2", b2)
                    before(dve, "b_x2T_ps", b2)
                    before(dve, "b_out", b2, 16)
                    normalise(x2w, tg[:, 1, :], mvb, rsb, S["b_x2"])
                if batch(b0):
                    now(dve, "b_x", b0, 16)
                    now(dve, "b_yo_ps", b0)
                    before(dve, "b_x1", b0)
                    A.count(dve.scalar_tensor_tensor(tg[:, 0, :], xtf, 2.0, bank_o[:, :], ALU.mult, ALU.add))
                    A.wait()
                    stats(tg[:, 0, :], sta, mva, A.sem, A.base(), S["b_mv"])
                if batch(b1):
                    for t in range(2):
                        expert_sum(b1, t)
                    now(dve, "b_yb_ps", b1)
                    before(dve, "b_x2", b1)
                    dve.tensor_tensor(tg[:, 1, :], bank_s[:, 0, :], hn, ALU.add).then_inc(S["b_acc"], 1)
                if batch(b0):
                    now(dve, "b_rs", b0)
                    before(dve, "b_xT_ps", b0)
                    before(dve, "b_acc", b0)
                    normalise(hn, tg[:, 0, :], mva, rsa, S["b_x1"])
                if batch(b1):
                    for t in range(2, NT):
                        expert_sum(b1, t)
                    now(dve, "b_red", b1, NT)
                    now(dve, "b_acc", b1)
                    B.count(dve.tensor_tensor(tg[:, 1, :], tg[:, 1, :], esum, ALU.add))
                    B.wait()
                    stats(tg[:, 1, :], sta, mvb, B.sem, B.base(), S["b_mv2"])

            def expert_sum(b, t):
                now(dve, "b_sc", b, NT, t + 1)
                dve.tensor_reduce(esum[:, t * D:(t + 1) * D], scaled[t % 2].rearrange("p e d -> p d e"), AX.X, ALU.add).then_inc(S["b_red"], 1)
            staged(dve, body, 3)

            def reduce(x, k, n):
                if x is None:
                    return
                need(dve, S["c_s_ps"], 16 * (2 * x.u + k) + n + 1)
                dve.tensor_reduce(nm[:, k, n:n + 1], bank_s[:, n % 2, :], AX.X, ALU.max, negate=True).then_inc(S["c_red"], 1)

            def parts(x, k, step):
                if x is None:
                    return
                G = 2 * x.u + k
                if step == 0:
                    need(dve, S["c_red"], 16 * G + 16)
                    need(dve, S["c_mT_ps"], G)
                    dve.tensor_copy(mp[:, 0:16], nm[:, k, :]).then_inc(S["c_link"], 1)
                else:
                    need(dve, S["c_link"], 3 * G + step)
                if step == 1:
                    dve.tensor_tensor(mr, nm[:, k, :], mp[:, 0:16], ALU.subtract).then_inc(S["c_link"], 1)
                if step == 2:
                    dve.tensor_copy(mp[:, 16:32], mr).then_inc(S["c_link"], 1)
                if step == 3:
                    dve.tensor_tensor(mp[:, 32:48], mr, mp[:, 16:32], ALU.subtract).then_inc(S["c_nm_ok"], 1)

            o4 = bank_m[:, :].rearrange("p (t h m) -> p t h m", t=NT, h=GH)

            def divide(x, k, step):
                if x is None:
                    return
                G = 2 * x.u + k
                w = GH * x.c.hd
                if step == 0:
                    need(dve, S["c_ot_ps"], G + 1)
                    dve.reciprocal(rec, o4[:, :, :, x.c.hd]).then_inc(S["c_sum"], 1)
                    return
                if x.c.node and k == 0:
                    need(dve, S["c_cT_ps"], x.un)
                first = k * w if x.c.node else x.half * 2 * w + k * w
                dst = ctx_sb.rearrange("p (t m) -> p t m", t=NT)[:, :, first:first + w]
                need(dve, S["c_sum"], G + 1)
                dve.tensor_tensor(dst.rearrange("p t (h m) -> p t h m", h=GH), o4[:, :, :, 0:x.c.hd],
                                  rec.unsqueeze(3).broadcast_to([P, NT, GH, x.c.hd]), ALU.mult).then_inc(S["c_ot_ev"], 1)

            def node_out(x):
                x = only(x, True)
                if x is None:
                    return
                need(dve, S["c_wo_ps"], x.un + 1)
                need(dve, S["c_store"], 16 * (NB + x.un))
                dve.scalar_tensor_tensor(no_sb, bank_m[:, :], st_o[x.half][:, P:P + 1], q_sb[x.r], ALU.add, ALU.add).then_inc(S["c_wo_ev"], 1)

            def residual(x, step):
                x = only(x, False)
                if x is None or not x.half:
                    return
                if step == 0:
                    need(dve, S["c_x2in"], 16 * x.b + 16)
                    need(dve, S["c_ot_ev"], 4 * x.b + 4)
                    dve.tensor_tensor(ctx_sb, ctx_sb, x2s, ALU.add).then_inc(S["c_xlink"], 1)
                if step == 1:
                    need(dve, S["c_xlink"], (NT + 1) * x.b + 1)
                    stats(ctx_sb, stt, mv, S["c_xlink"], (NT + 1) * x.b + 1, S["c_mv"])
                if step == 2:
                    need(dve, S["c_rs"], x.b + 1)
                    need(dve, S["c_x3T_ps"], x.b)
                    need(dve, S["c_x3out"], 16 * x.b)
                    normalise(x3s, ctx_sb, mv, rs, S["c_x3"])

            dve.wait_ge(S["c_ones"], 3)
            for n in range(16):
                reduce(at_(kc, 0, 0), 0, n)
            for step in range(4):
                parts(at_(kc, 0, 0), 0, step)
            for n in range(12):
                reduce(at_(kc, 0, 0), 1, n)

            def body(c, q, r):
                x, last = at_(c, q, r), at_(c, q, r - 1)
                for k in range(2):
                    for i in range(8):
                        for j, group in enumerate(led(c, q, r, k, i)):
                            if i == 4:
                                divide(*((last, 1) if k == 0 else (x, 0)), j)
                            reduce(*group)
                            if i in (2, 3):
                                parts(*led_group(c, q, r, k), 2 * (i - 2) + j)
                        if (k, i) == (0, 5):
                            residual(last, 0)
                        if (k, i) == (0, 7):
                            residual(last, 1)
                        if (k, i) == (1, 0):
                            node_out(last)
                        if (k, i) == (1, 3):
                            residual(last, 2)
            units(dve, body)
            end = at_(kn, QU - 1, RING - 1)
            for step in range(2):
                divide(end, 1, step)
            node_out(end)

            g0, b0_ = (lngb[:, j, :].unsqueeze(1).broadcast_to([P, NT, D]) for j in range(2))
            c3 = ctx_sb.rearrange("p (t d) -> p t d", t=NT)

            def body(b):
                b0, b1, b2 = b, b - 1, b - 2
                if batch(b2):
                    now(dve, "f_rs2", b2)
                    before(dve, "f_out", b2, 16)
                    normalise(x3s, ctx_sb, mv2, rs2, S["f_y"])
                if batch(b1):
                    v = Links("f_link", 2 + NT, b1)
                    now(dve, "f_rs", b1)
                    before(dve, "f_y", b1)
                    normalise(ctx_sb, ctxT, mv, rs, S["f_nm"])
                    now(dve, "f_nm", b1)
                    v.count(dve.tensor_tensor(c3, c3, g0, ALU.mult))
                    v.wait()
                    v.count(dve.tensor_tensor(c3, c3, b0_, ALU.add))
                    v.wait()
                    now(dve, "f_x3_in", b1, 16)
                    dve.tensor_tensor(ctx_sb, ctx_sb, x2s, ALU.add).then_inc(S["f_z"], 1)
                    now(dve, "f_z", b1)
                    stats(ctx_sb, stt2, mv2, v.sem, v.base(), S["f_mv2"])
                if batch(b0):
                    now(dve, "f_tT_ev", b0)
                    stats(ctxT, stt, mv, S["f_link2"], NT * b0 + 1, S["f_mv"])
            staged(dve, body, 3)


def kernel(**inputs):
    import numpy as np
    import concourse.bacc as bacc
    from concourse.bass_utils import run_bass_kernel_spmd

    i = {k: np.asarray(v) for k, v in inputs.items()}
    rows = lambda v: np.ascontiguousarray(np.broadcast_to(v, (P,) + v.shape))
    blocks = lambda w: np.ascontiguousarray(w.reshape(NH, P, -1).transpose(1, 0, 2))

    def dims_first(w, heads):
        return w.reshape(P, heads, -1).transpose(0, 2, 1).reshape(P, -1)

    wckq = np.stack([np.concatenate([dims_first(i["L1_attn_w_" + w][:, h * 64:(h + 1) * 64], HU) for w in "KQ"], 1)
                     for h in range(2)], 1)

    col = lambda v: v.reshape(NH, P).T[:, :, None]
    zero = np.zeros((P, NH, 1), np.float32)
    conv = i["L0_attn_conv_w"].reshape(NH, P, KC).transpose(1, 0, 2)
    cv = np.concatenate([conv, col(i["L0_attn_conv_b"]), col(i["L0_attn_D_vec"]), col(i["L0_attn_bd"]), zero], 2)

    pk, first = [], 0
    We, be = i["L1_ffn_We"], i["L1_ffn_be"]
    for c in range(NODES):
        n = min(c + 1, 5)
        eq, ek, ev = first + n - 1, first, first + n // 2
        first += n
        pk.append(np.concatenate([
            We[eq], dims_first(i["L1_ffn_Wq"][c], HU), We[ek].T, dims_first(i["L1_ffn_Wk"][c], HU), We[ev].T,
            i["L1_ffn_Wv"][c], i["L1_ffn_Wo"][c], be[eq][:, None], be[ek][:, None], be[ev][:, None],
            rows(i["L1_ffn_ew"][c]), rows(i["L1_ffn_act_w"][c:c + 1])], 1))

    arrays = {
        "x": i["L0_attn_x"], "cv": cv, "gb": np.stack([i["L0_attn_ln_gamma"], i["L0_attn_ln_beta"]], 1),
        "alog": np.tile(i["L0_attn_A_log"], NB)[:, None], "w_in": i["L0_attn_W_in"], "wd": blocks(i["L0_attn_Wd"]),
        "w_out": blocks(i["L0_attn_W_out"]), "bmt": blocks(i["L0_attn_B_mat"].T), "cmt": i["L0_attn_C_mat"].T,
        "rw": i["L0_ffn_router_w"], "rb": rows(i["L0_ffn_router_b"]),
        "xw": i["L0_ffn_expert_w"].transpose(1, 0, 2).reshape(D, NE * D), "xb": i["L0_ffn_expert_b"],
        "wckq": wckq, "wcv": i["L1_attn_w_V"],
        "lng": rows(i["L1_ffn_ln_g"]), "lnb": rows(i["L1_ffn_ln_b"]), "pk": np.stack(pk),
    }
    arrays = {k: np.ascontiguousarray(v) for k, v in arrays.items()}
    nc = bacc.Bacc("TRN2", target_bir_lowering=False, num_devices=1)
    a = {k: nc.dram_tensor("in_" + k, v.shape, F32, kind="ExternalInput").ap() for k, v in arrays.items()}
    a["out"] = nc.dram_tensor("out_x", (NB, L, D), F32, kind="ExternalOutput").ap()
    build(nc, a)
    r = run_bass_kernel_spmd(nc, [{"in_" + k: v for k, v in arrays.items()}], core_ids=[0])
    return r.results[0]["out_x"]
```

```python
from contextlib import ExitStack

import concourse.bass as bass
from concourse import mybir

F32 = mybir.dt.float32
BF16 = mybir.dt.bfloat16
ACT = mybir.ActivationFunctionType
ALU = mybir.AluOpType
AX = mybir.AxisListType

P = 128
NB = 8
L = 512
D = 128
NT = L // P
DI = 256
NH = DI // P
NS = 16
KC = 4
NE = 8
NODES = 6
HU = 8
GH = 4
COL = 32
RING = 4
EPS_LN = 1e-5
EPS_NODE = 1e-6

TERMS_16 = [(0, 0), (0, 1), (0, 2), (1, 0), (1, 1), (2, 0)]
TERMS_8 = [(a, b) for a in range(3) for b in range(3)]
TWO_ONES = 1.00193786621093750

PK = ["WeQ", "WqP", "WeKT", "WkP", "WeVT", "Wv", "Wo"]
PKC = len(PK) * P + 3 + 4
WA = 3 * P + 2
WN = WA + 2 * P + 1


def need(e, sem, value):
    if isinstance(value, int) and value <= 0:
        return
    e.wait_ge(sem, value)


def build(nc, a):
    f = lambda name, shape: nc.dram_tensor(name, shape, F32).ap()
    w_d = f("w_d", (NODES, P, WN))
    dB_d = f("dB_d", (NB, NS, 2, L))
    hs_d = f("hs_d", (NB, NS, L))
    x2T_d, x2_d, x3_d = f("x2T_d", (NB, P, L)), f("x2_d", (NB, P, NT * D)), f("x3_d", (NB, P, NT * D))
    nodes_d = f("nodes_d", (NODES * NB, P, L))

    with ExitStack() as ctx:
        def sb(name, shape, dt=F32):
            return ctx.enter_context(nc.sbuf_tensor(name, shape, dt))

        def sem(name):
            return ctx.enter_context(nc.semaphore(name))

        bank_x = ctx.enter_context(nc.psum_tensor("bank_x", [P, 2, 1024], F32))
        bank_s = ctx.enter_context(nc.psum_tensor("bank_s", [P, 2, 512], F32))
        bank_o = ctx.enter_context(nc.psum_tensor("bank_o", [P, 512], F32))
        bank_m = ctx.enter_context(nc.psum_tensor("bank_m", [P, 512], F32))

        ident = sb("ident", [P, P])
        identb = sb("identb", [P, P], BF16)
        half = sb("half", [P, NT])
        eps_ln, eps_node = sb("eps_ln", [P, NT]), sb("eps_node", [P, NT])
        cv = sb("cv", [P, NH, KC + 4])
        cvh = sb("cvh", [P, NH, KC + 1])
        gb = sb("gb", [P, 2])
        alog = sb("alog", [P, 1])
        aneg = sb("aneg", [P, 2])
        w_in = sb("w_in", [P, 2 * DI])
        wd = sb("wd", [P, NH, DI])
        w_out = sb("w_out", [P, NH, D])
        woh = sb("woh", [P, NH, D])
        bmt = sb("bmt", [P, NH, NS])
        cmt = sb("cmt", [NS, DI])
        mean_w = sb("mean_w", [P, NS])
        rw = sb("rw", [P, NE])
        rb = sb("rb", [P, NE])
        rank = sb("rank", [P, NE])
        xw = sb("xw", [P, NE * D])
        xb = sb("xb", [NE, D])
        wc = sb("wc", [P, 3, P])
        lngb = sb("lngb", [P, 2, D])

        big = sb("big", [P, 30 * 1024])
        xs_all = big[:, 0:8192]
        sg_all = big[:, 8192:16384]
        qst = big[:, 0:8192].bitcast(BF16).rearrange("p (u h n) -> p u h n", u=RING, h=HU)
        kst = big[:, 8192:16384].bitcast(BF16).rearrange("p (u h n) -> p u h n", u=RING, h=HU)
        kst_f = big[:, 8192:16384].rearrange("p (u n) -> p u n", u=RING)
        PT = big[:, 16384:24576].rearrange("p (k h c n) -> p k h c n", k=2, h=GH, c=2)
        wk = big[:, 16384:30720]

        at = sb("at", [P, 15 * 1024])
        o = [0]

        def cut(n):
            o[0] += n
            return at[:, o[0] - n:o[0]]

        st_qk = [cut(WA + 2 * L) for _ in range(2)]
        st_v = [cut(P + L) for _ in range(2)]
        st_o = [cut(P + 2)[:, 0:P + 1] for _ in range(2)]
        q_sb = [cut(L) for _ in range(RING)]
        qf, kf = cut(L), cut(L)
        qp = cut(3 * L // 2).bitcast(BF16).rearrange("p (t n) -> p t n", t=3)
        kp_ = cut(3 * L // 2).bitcast(BF16).rearrange("p (t n) -> p t n", t=3)
        ot_sb = cut(L)
        assert o[0] <= 15 * 1024, o
        atb = big[:, 24576:30720]
        o2 = [0]

        def cut2(n):
            o2[0] += n
            return atb[:, o2[0] - n:o2[0]]

        vaug = [at[:, o_ * 1024:(o_ + 1) * 1024].rearrange("p (c h m) -> p c h m", c=NT, h=HU) for o_ in (10, 11)]
        assert NT * HU * COL == 1024 and max(o[0], NODES * (PKC + WN + 1)) <= 10 * 1024
        ctx_sb = cut2(L)
        ctxT = cut2(L)
        no_sb = cut2(L)
        x2s = cut2(L)
        x3s = cut2(L)
        nm = cut2(32).rearrange("p (g n) -> p g n", g=2)
        mr = cut2(16)
        mp = cut2(24).bitcast(BF16)
        mT = cut2(64).bitcast(BF16)
        rec = cut2(16).rearrange("p (t h) -> p t h", t=NT)
        stt = cut2(NT * 6).rearrange("p (t s) -> p t s", t=NT)
        mv = cut2(NT * 2).rearrange("p (t s) -> p t s", t=NT)
        rs = cut2(NT)
        rs0 = cut2(NT)
        mv2 = cut2(NT * 2).rearrange("p (t s) -> p t s", t=NT)
        rs2, rs20 = cut2(NT), cut2(NT)
        stt2 = cut2(NT * 6).rearrange("p (t s) -> p t s", t=NT)
        nT, zn = cut2(L), cut2(L)
        assert o2[0] <= 6144, o2

        w0 = [0]

        def cutw(n):
            w0[0] += n
            assert w0[0] <= 14336
            return wk[:, w0[0] - n:w0[0]]

        xt = cutw(L).rearrange("p (t d) -> p t d", t=NT)
        hn = cutw(L)
        hT = cutw(L)
        cbuf = cutw(NH * (L + KC)).rearrange("p (h n) -> p h n", h=NH)
        tg = cutw(NH * L).rearrange("p (h n) -> p h n", h=NH)
        yh = cutw(NH * L).rearrange("p (h n) -> p h n", h=NH)
        ab = cutw(NH * L).rearrange("p (h n) -> p h n", h=NH)
        rl = cutw(NH * L).rearrange("p (h n) -> p h n", h=NH)
        dbx = cutw(L)[0:COL + NS, :]
        db = cutw(2 * L).rearrange("p (t n) -> p t n", t=2)
        hs = cutw(L)
        hsb = cutw(L)[0:NS, :]
        x2w, x2Tw, esum = cutw(L), cutw(L), cutw(L)
        lg = cutw(NT * NE).rearrange("p (t e) -> p t e", t=NT)
        lge = cutw(NT * NE).rearrange("p (t e) -> p t e", t=NT)
        lgm = cutw(NT * NE).rearrange("p (t e) -> p t e", t=NT)
        mx = cutw(NT)
        nmx = cutw(NT)
        sm = cutw(NT)
        fm = cutw(NT)
        mgT = cutw(L)[0:NE, :]
        sta = cutw(NT * 6).rearrange("p (t s) -> p t s", t=NT)
        mva = cutw(NT * 2).rearrange("p (t s) -> p t s", t=NT)
        mvb = cutw(NT * 2).rearrange("p (t s) -> p t s", t=NT)
        rsa, rsa0, rsb, rsb0 = cutw(NT), cutw(NT), cutw(NT), cutw(NT)
        scaled = [x.rearrange("p h n -> p (h n)").rearrange("p (e d) -> p e d", e=NE) for x in (ab, rl)]
        pk_sb = at[:, 0:NODES * PKC].rearrange("p (c n) -> p c n", c=NODES)
        po_sb = at[:, NODES * PKC:NODES * (PKC + WN)].rearrange("p (c n) -> p c n", c=NODES)
        bv_sb = at[:, NODES * (PKC + WN):NODES * (PKC + WN + 1)]
        wv = lambda c, n: pk_sb[:, c, PK.index(n) * P:(PK.index(n) + 1) * P]
        vec = lambda c, i: pk_sb[:, c, len(PK) * P + i:len(PK) * P + i + 1]

        bx0, bx1 = bank_x[:, 0, :], bank_x[:, 1, :]
        sec = lambda t, h: t[:, h * 512:(h + 1) * 512]

        s_w = sem("weights_in")
        s_id = sem("identity_ready")
        s_c = sem("constants_ready")
        s_w2 = sem("other_weights_in")
        N_W, N_W2 = 7, 9

        block = ctx.enter_context(nc.Block())
        S = {}
        credit = []

        def now(e, name, b, n=1, k=None):
            e.wait_ge(S[name], n * b + (n if k is None else k) + 1)

        def before(e, name, b, n=1):
            e.wait_ge(S[name], n * b + 1)

        def names(prefix, *ns):
            for n in ns:
                S[prefix + n] = sem(prefix + n)
                if prefix in ("a_", "b_"):
                    credit.append(S[prefix + n])

        passed = sem("wait_passed")
        names("p_", "ev", "in", "mm", "out")
        names("a_", "x", "mv", "rs", "rs_link", "hn", "hT_ps", "hT_ev", "win_ps", "xs_ev", "tg", "g_ev", "yh", "th", "xs", "z_ps", "z_ev",
              "ab", "ln", "sp", "mb_ps", "mb_ev", "dB_out", "link", "link2")
        names("r_", "A", "bx", "dA", "hs", "in", "out")
        names("b_", "x", "hs", "c_ps", "y", "yo_ps", "mv", "rs", "rs_link", "x1", "xT_ps", "xT_ev", "lg_ps", "lg", "ex", "mg", "mgT_ps",
              "mgT_ev", "yb_ps", "acc", "e_ps", "sc", "red", "mv2", "rs2", "rs2_link", "x2", "x2T_ps", "x2T_ev", "out", "outT",
              "link", "link2")
        names("f_", "x3_in", "tT_ps", "tT_ev", "mv", "rs", "rs_link", "nm", "z", "mv2", "rs2", "rs2_link", "y", "out", "link", "link2", "plink")
        names("c_", "qk0", "qk1", "v0", "v1", "o0", "o1", "kh_ps", "qh_ps", "qT_ps", "v_ps", "ot_ps", "mT_ps", "wo_ps", "cT_ps", "x3T_ps",
              "kf_ev", "qf_ev", "q_ev", "v_ev", "ot_ev", "mT_ev", "pv_ev", "cT_ev", "wo_ev", "x3T_ev", "sp", "stk0", "stk1", "stk2",
              "stk3", "m_dma", "s_ps", "red", "nm_ok", "st_ps", "ex", "pv_ps", "store", "link", "pool", "sum", "xlink", "plink",
              "x2in", "x3", "x3out", "mv", "rs", "ones")

        class Kind:
            pass

        UC, U = 2 * NB, 2 * NB + NODES * NB
        QC, QU = UC // RING, U // RING
        U_LAST = (NODES - 1) * NB
        kc, kn = Kind(), Kind()
        kc.node, kc.hd, kc.terms, kc.loads_qk, kc.loads_v = False, 8, TERMS_8, 1, 1
        kn.node, kn.hd, kn.terms, kn.loads_qk, kn.loads_v = True, 16, TERMS_16, 3, 2
        for c in (kc, kn):
            c.R = len(c.terms) * c.hd
            c.R3 = c.R + 3
            c.np_ = HU * c.hd
            c.scale = float(c.hd) ** -0.5

        def at_(c, q, r):
            x = Kind()
            x.q, x.r = q + r // RING, r % RING
            x.u = RING * x.q + x.r
            if isinstance(q, int):
                if not 0 <= x.u < U:
                    return None
                c = kc if x.u < UC else kn
            x.c, x.un = c, x.u - UC
            x.b = 2 * x.q + x.r // 2
            x.half = x.r % 2
            x.turn = x.q - QC * c.node
            return x

        def only(x, node):
            return x if x is not None and x.c.node == node else None

        def units(e, body):
            for r in range(RING):
                body(kc, 0, r)
            with e.Fori(1, QC - 1) as it:
                for r in range(RING):
                    body(kc, it, r)
            for q in (QC - 1, QC):
                for r in range(RING):
                    body(None, q, r)
            with e.Fori(QC + 1, QU - 2) as it:
                for r in range(RING):
                    body(kn, it, r)
            for q in (QU - 2, QU - 1):
                for r in range(RING):
                    body(kn, q, r)

        def final(x):
            if x is None or not isinstance(x.un, int) or x.un < U_LAST:
                return None
            return x.un - U_LAST

        def stacked(x):
            n = 16 * 2 * len(x.c.terms) * (x.turn + 1)
            return n + 16 * 2 * len(kc.terms) * QC if x.c.node else n

        def loaded(x, n_node, n_first=1):
            n = 2 * x.turn + x.r // 2 + 1
            return 16 * (n_node * n + n_first * 2 * QC) if x.c.node else 16 * n_first * n

        def led(c, q, r, k, i):
            for j in range(2):
                if i < 2:
                    yield (at_(c, q, r), 1, 12 + 2 * i + j) if k == 0 else (at_(c, q, r + 1), 0, 12 + 2 * i + j)
                else:
                    yield at_(c, q, r + 1), k, 2 * (i - 2) + j

        def paced(x, node, first):
            return node if x.c.node else first

        def led_group(c, q, r, k):
            return (at_(c, q, r), 1) if k == 0 else (at_(c, q, r + 1), 0)

        def staged(e, body, depth):
            for b in range(depth - 1):
                body(b)
            with e.Fori(depth - 1, NB) as it:
                body(it)
            for b in range(NB, NB + depth - 1):
                body(b)

        def batch(b):
            return not isinstance(b, int) or 0 <= b < NB

        @block.sync
        def _(sp):
            first_weights = ((cv[:, :, :], a["cv"]), (gb[:, :], a["gb"]), (w_in[:, :], a["w_in"]), (wd[:, :, :], a["wd"]),
                             (bmt[:, :, :], a["bmt"]), (w_out[:, :, :], a["w_out"]), (alog[:, :], a["alog"]))
            other_weights = ((cmt[:, :], a["cmt"]), (rw[:, :], a["rw"]), (rb[:, :], a["rb"]), (xw[:, :], a["xw"]), (xb[:, :], a["xb"]),
                             (wc[:, 0:2, :], a["wckq"]), (wc[:, 2, :], a["wcv"]), (lngb[:, 0, :], a["lng"]), (lngb[:, 1, :], a["lnb"]))
            assert (len(first_weights), len(other_weights)) == (N_W, N_W2)

            def weights(group, done):
                for dst, src in group:
                    sp.dma_start(dst, src).then_inc(done, 16)

            def row(t, i):
                return t[bass.ds(i, 1)].rearrange("o p n -> (o p) n")

            def when(*waits):
                for x, v in waits:
                    need(sp, x, v)
                    if not isinstance(v, int):
                        sp.sem_inc(passed, 1)

            def tokens(t, i):
                return t[bass.ds(i, 1)].rearrange("o (t p) d -> p (o t) d", p=P)

            def body(b):
                if batch(b):
                    when((S["a_hn"], b + 1))
                    sp.dma_start(xt, tokens(a["x"], b)).then_inc(S["a_x"], 16)
                if isinstance(b, int) and b == 0:
                    weights(first_weights, s_w)
                if isinstance(b, int) and b == 1:
                    weights(other_weights, s_w2)
                    sp.dma_start(pk_sb, a["pk"].rearrange("c p n -> p c n")).then_inc(S["p_in"], 16)
                b = b - 3
                if batch(b):
                    when((S["a_mb_ev"], b + 2))
                    for t, first in ((0, COL), (1, 0)):
                        sp.dma_start(dB_d[bass.ds(b, 1)][:, :, t, :].rearrange("o n l -> (o n) l"),
                                     dbx[first:first + NS, :]).then_inc(S["a_dB_out"], 16)
            staged(sp, body, 4)
            sp.wait_ge(S["a_dB_out"], 32 * NB + 1)
            sp.dma_start(db, dB_d.rearrange("b n t l -> (b n) t l")).then_inc(S["r_in"], 16)
            sp.wait_ge(S["r_hs"], 1)
            sp.dma_start(hs_d.rearrange("b n l -> (b n) l"), hs).then_inc(S["r_out"], 16)
            sp.wait_ge(S["r_out"], 16)
            def load_qk(x):
                if x is None:
                    return
                t, done = st_qk[x.half], S[f"c_qk{x.half}"]
                when((S["c_kh_ps"], x.u - 1), *[(S["c_qh_ps"], x.un - 1)] * x.c.node)
                if x.c.node:
                    when((S["c_store"], 16 * (x.un + 1)))
                    sp.dma_start(t[:, 0:WA], row(w_d, x.un // NB)[:, 0:WA]).then_inc(done, 16)
                    sp.dma_start(t[:, WA:WA + L], row(nodes_d, x.un)).then_inc(done, 16)
                    sp.dma_start(t[:, WA + L:WA + 2 * L], row(nodes_d, (x.un // 40) * NB + x.un % NB)).then_inc(done, 16)
                else:
                    sp.dma_start(t[:, WA:WA + L], row(x2T_d, x.u // 2)).then_inc(done, 16)

            def load_v(x):
                if x is None:
                    return
                t, done = st_v[x.half], S[f"c_v{x.half}"]
                when((S["c_v_ev"], x.u - 1))
                if x.c.node:
                    when((S["c_store"], 16 * (x.un + 1)))
                    sp.dma_start(t[:, 0:P], row(w_d, x.un // NB)[:, WA:WA + P]).then_inc(done, 16)
                    sp.dma_start(t[:, P:P + L], row(nodes_d, ((x.un // NB + 1) // 2) * NB + x.un % NB)).then_inc(done, 16)
                else:
                    sp.dma_start(t[:, P:P + L], row(x2T_d, x.u // 2)).then_inc(done, 16)

            def load_o(x):
                x = only(x, True)
                if x is None:
                    return
                when((S["c_wo_ev"], x.un - 1))
                sp.dma_start(st_o[x.half], row(w_d, x.un // NB)[:, WA + P:WN]).then_inc(S[f"c_o{x.half}"], 16)

            def stack(x):
                if x is None:
                    return
                n = x.c.np_
                done = S[f"c_stk{x.r}"]
                k_parts, q_parts = (kp_, qp) if x.c.node else (kp_[0:n], kp_[n:2 * n])
                when((S["c_ex"], 16 * (x.u - RING + 1)), (S["c_sp"], 2 * x.u + 1))
                for i, (_, part) in enumerate(x.c.terms):
                    sp.dma_start(kst[i * x.c.hd:(i + 1) * x.c.hd, x.r, :, :], k_parts[0:n, part, :]).then_inc(done, 16)
                when((S["c_sp"], 2 * x.u + 2))
                for i, (part, _) in enumerate(x.c.terms):
                    sp.dma_start(qst[i * x.c.hd:(i + 1) * x.c.hd, x.r, :, :], q_parts[0:n, part, :]).then_inc(done, 16)

            def store(x):
                x = only(x, True)
                if x is None or final(x) is not None:
                    return
                when((S["c_store"], 16 * (NB + x.un)), (S["c_wo_ev"], x.un + 1))
                sp.dma_start(row(nodes_d, x.un + NB), no_sb).then_inc(S["c_store"], 16)

            def store_x3(x):
                x = only(x, False)
                if x is None or not x.half:
                    return
                when((S["c_store"], 16 * x.b), (S["c_x3T_ev"], x.b + 1))
                sp.dma_start(row(nodes_d, x.b), no_sb).then_inc(S["c_store"], 16)
                sp.dma_start(row(x3_d, x.b), x3s).then_inc(S["c_x3out"], 16)

            def load_x2(x):
                x = only(x, False)
                if x is None or not x.half:
                    return
                when((S["c_x3"], x.b))
                sp.dma_start(x2s, row(x2_d, x.b)).then_inc(S["c_x2in"], 16)

            def load_x3(x):
                j = final(x)
                if j is None:
                    return
                when((S["f_z"], j))
                sp.dma_start(x2s, row(x3_d, j)).then_inc(S["f_x3_in"], 16)

            def store_out(x):
                j = final(x)
                if j is None:
                    return
                when((S["f_y"], j + 1))
                sp.dma_start(tokens(a["out"], j), x3s.rearrange("p (t d) -> p t d", t=NT)).then_inc(S["f_out"], 16)

            def body(b):
                if batch(b):
                    when((S["b_mv"], b + 1), (S["b_c_ps"], 2 * b + 1))
                    sp.dma_start(xt, tokens(a["x"], b)).then_inc(S["b_x"], 16)
                    sp.dma_start(hsb, row(hs_d, b)).then_inc(S["b_hs"], 16)
                if isinstance(b, int) and b == 0:
                    sp.wait_ge(S["p_ev"], 2)
                    sp.dma_start(w_d.rearrange("c p n -> p c n"), po_sb).then_inc(S["p_out"], 16)
                if isinstance(b, int) and b == NB:
                    sp.wait_ge(S["b_outT"], 16 * (NB - 2) + 1)
                    sp.wait_ge(S["p_out"], 16)
                    load_qk(at_(kc, 0, 0))
                    load_qk(at_(kc, 0, 1))
                    load_v(at_(kc, 0, 0))
                if isinstance(b, int) and b == NB + 1:
                    sp.wait_ge(S["c_ones"], RING)
                    stack(at_(kc, 0, 0))
                b = b - 2
                if batch(b):
                    when((S["b_x2"], b + 2))
                    sp.dma_start(row(x2_d, b), x2w).then_inc(S["b_out"], 16)
                    when((S["b_x2T_ev"], b + 2))
                    sp.dma_start(row(x2T_d, b), x2Tw).then_inc(S["b_outT"], 16)
            staged(sp, body, 3)
            sp.wait_ge(S["b_out"], 16 * NB + 1)
            sp.wait_ge(S["b_outT"], 16 * NB + 1)

            load_v(at_(kc, 0, 1))
            load_qk(at_(kc, 0, 2))
            stack(at_(kc, 0, 1))
            load_qk(at_(kc, 0, 3))
            stack(at_(kc, 0, 2))

            def body(c, q, r):
                load_qk(at_(c, q, r + 4))
                load_v(at_(c, q, r + 2))
                load_x2(at_(c, q, r))
                store(at_(c, q, r - 1))
                load_o(at_(c, q, r + 1))
                load_x3(at_(c, q, r - 1))
                store_out(at_(c, q, r - 2))
                stack(at_(c, q, r + 3))
                store_x3(at_(c, q, r - 1))
            units(sp, body)
            load_x3(at_(kn, QU - 1, RING - 1))
            for r in (RING - 2, RING - 1):
                store_out(at_(kn, QU - 1, r))
            sp.wait_ge(S["c_store"], 16 * NODES * NB)
            sp.wait_ge(S["c_x3out"], 16 * NB)
            sp.wait_ge(S["f_out"], 16 * NB)

        @block.gpsimd
        def _(pool):
            for x in credit:
                pool.sem_inc(x, 1)
            pool.memset(ident[:, :], 0.0).then_inc(s_id, 1)
            pool.memset(identb[:, :], 0.0).then_inc(s_id, 1)
            pool.memset(half[:, :], -0.5).then_inc(s_c, 1)
            pool.memset(eps_ln[:, :], EPS_LN).then_inc(s_c, 1)
            pool.memset(eps_node[:, :], EPS_NODE).then_inc(s_c, 1)
            pool.memset(mean_w[:, :], 1.0 / DI).then_inc(s_c, 1)
            pool.memset(cbuf[:, :, 0:KC], 0.0).then_inc(s_c, 1)
            for e_ in range(NE):
                pool.memset(rank[:, e_:e_ + 1], float(NE - e_)).then_inc(s_c, 1)
            for j in range(2):
                pool.memset(vaug[j], 1.0).then_inc(s_c, 1)
            pool.wait_ge(s_id, 2)
            for m in (ident, identb):
                pool.affine_select(out=m[:, :], in_=m[:, :], compare_op=ALU.not_equal, fill=1.0, base=0,
                                   pattern=[[-1, P]], channel_multiplier=1).then_inc(s_id, 1)
            pool.wait_ge(s_c, 7 + NE)

            def rstd(mv_, t0, t1, eps, ready, link, done):
                pool.wait_ge(*ready)
                pool.tensor_tensor(t0, mv_[:, :, 1], eps, ALU.add).then_inc(link[0], 1)
                pool.wait_ge(*link)
                pool.tensor_tensor(t1, t0, half[:, :], ALU.pow).then_inc(done, 1)

            with pool.Fori(0, NB) as b:
                rstd(mva, rsa0, rsa, eps_ln[:, :], (S["a_mv"], b + 2), (S["a_rs_link"], b + 2), S["a_rs"])

            def in_parts(src, dst, base, done, n):
                pool.tensor_copy(dst[:, 0, :], src).then_inc(S["c_pool"], 1)
                need(pool, S["c_pool"], base + 1)
                pool.tensor_tensor(src, src, dst[:, 0, :], ALU.subtract).then_inc(S["c_pool"], 1)
                need(pool, S["c_pool"], base + 2)
                pool.sem_inc(passed, 1)
                pool.tensor_copy(dst[:, 1, :], src).then_inc(S["c_pool"], 1)
                need(pool, S["c_pool"], base + 3)
                pool.tensor_tensor(dst[:, 2, :], src, dst[:, 1, :], ALU.subtract).then_inc(done, n)

            def split(x):
                if x is None:
                    return
                base = 3 * UC + 6 * x.un if x.c.node else 3 * x.u
                before_ = at_(x.c, x.q, x.r - 1)
                if before_ is not None:
                    need(pool, S[f"c_stk{before_.r}"], stacked(before_))
                need(pool, S["c_kf_ev"], x.u + 1)
                pool.sem_inc(passed, 1)
                in_parts(kf, kp_, base, S["c_sp"], 1 if x.c.node else 2)
                if x.c.node:
                    need(pool, S["c_qf_ev"], x.un + 1)
                    pool.sem_inc(passed, 1)
                    in_parts(qf, qp, base + 3, S["c_sp"], 1)

            def residual_rstd(x):
                x = only(x, False)
                if x is None or not x.half:
                    return
                rstd(mv, rs0, rs, eps_ln[:, :], (S["c_mv"], x.b + 1), (S["c_plink"], x.b + 1), S["c_rs"])

            def body(b):
                if batch(b):
                    rstd(mva, rsa0, rsa, eps_ln[:, :], (S["b_mv"], b + 2), (S["b_rs_link"], b + 2), S["b_rs"])
                if isinstance(b, int) and b == NB:
                    pool.wait_ge(S["b_y"], NB + 1)
                    pool.wait_ge(S["b_rs2"], NB)
                    for r in range(RING):
                        pool.memset(kst_f[64:P, r, :], TWO_ONES).then_inc(S["c_ones"], 1)
                        pool.wait_ge(S["c_ones"], r + 1)
                    split(at_(kc, 0, 0))
                b = b - 1
                if batch(b):
                    rstd(mvb, rsb0, rsb, eps_ln[:, :], (S["b_mv2"], b + 2), (S["b_rs2_link"], b + 2), S["b_rs2"])
            staged(pool, body, 2)

            split(at_(kc, 0, 1))
            split(at_(kc, 0, 2))

            g3, b3 = (lngb[:, j, :].unsqueeze(1).broadcast_to([P, NT, D]) for j in range(2))
            z3, x33 = (t.rearrange("p (t d) -> p t d", t=NT) for t in (zn, x2s))

            def final_sum(x):
                j = final(x)
                if j is None:
                    return
                rstd(mv, rs0, rs, eps_node[:, :], (S["f_mv"], j + 1), (S["f_rs_link"], j + 1), S["f_rs"])
                need(pool, S["f_x3_in"], 16 * (j + 1))
                pool.tensor_tensor(x33, x33, b3, ALU.add).then_inc(S["f_plink"], 1)
                need(pool, S["f_nm"], j + 1)
                pool.tensor_tensor(z3, z3, g3, ALU.mult).then_inc(S["f_plink"], 1)
                need(pool, S["f_plink"], 2 * j + 2)
                pool.tensor_tensor(zn, zn, x2s, ALU.add).then_inc(S["f_z"], 1)

            def final_rstd(x):
                j = final(x)
                if j is None:
                    return
                rstd(mv2, rs20, rs2, eps_ln[:, :], (S["f_mv2"], j + 1), (S["f_rs2_link"], j + 1), S["f_rs2"])

            def body(c, q, r):
                residual_rstd(at_(c, q, r - 1))
                final_sum(at_(c, q, r - 1))
                split(at_(c, q, r + 3))
                final_rstd(at_(c, q, r - 1))
            units(pool, body)
            end = at_(kn, QU - 1, RING - 1)
            final_sum(end)
            final_rstd(end)

        @block.scalar
        def _(act):
            act.wait_ge(s_w, 16 * N_W)
            act.wait_ge(s_c, 7 + NE)
            act.activation(aneg[:, 0:1], alog[:, :], ACT.Exp).then_inc(S["r_A"], 1)
            act.wait_ge(S["r_A"], 1)
            act.activation(aneg[:, 1:2], aneg[:, 0:1], ACT.Copy, scale=-1.0).then_inc(S["r_A"], 1)

            def body(b):
                b0, b1, b2 = b, b - 1, b - 2
                if batch(b2):
                    now(act, "a_z_ev", b2, NH)
                    before(act, "a_sp", b2)
                    act.activation(ab, rl, ACT.Abs).then_inc(S["a_ab"], 1)
                    now(act, "a_ab", b2, 2, 1)
                    act.activation(ab, ab, ACT.Exp, scale=-1.0).then_inc(S["a_ab"], 1)
                    now(act, "a_ab", b2, 2)
                    act.activation(ab, ab, ACT.Ln, bias=1.0).then_inc(S["a_ln"], 1)
                if batch(b0):
                    now(act, "a_hT_ps", b0)
                    before(act, "a_win_ps", b0)
                    act.activation(hT, bank_m[:, :], ACT.Identity, bias=gb[:, 1:2], scale=gb[:, 0:1]).then_inc(S["a_hT_ev"], 1)
                if batch(b1):
                    now(act, "a_yh", b1)
                    now(act, "a_g_ev", b1)
                    act.activation(tg, yh, ACT.Tanh).then_inc(S["a_th"], 1)
                if batch(b0):
                    now(act, "a_win_ps", b0)
                    before(act, "a_yh", b0)
                    act.activation(cbuf[:, :, KC:KC + L], bx0.rearrange("p (h n) -> p h n", h=NH), ACT.Copy).then_inc(S["a_xs_ev"], 1)
                    before(act, "a_xs", b0)
                    act.activation(tg, bx1.rearrange("p (h n) -> p h n", h=NH), ACT.Tanh, scale=0.5).then_inc(S["a_tg"], 1)
                if batch(b2):
                    now(act, "a_mb_ps", b2)
                    before(act, "a_dB_out", b2, 32)
                    act.activation(dbx[0:NS, :], bank_o[0:NS, :], ACT.Copy)
                    act.activation(dbx[COL:COL + NS, :], bank_o[COL:COL + NS, :], ACT.Copy).then_inc(S["a_mb_ev"], 1)
            staged(act, body, 3)
            act.wait_ge(S["r_in"], 16)
            act.wait_ge(S["r_A"], 2)
            act.activation(hn, db[:, 0, :], ACT.Exp, scale=aneg[:, 1:2]).then_inc(S["r_dA"], 1)

            def ev_qT(x):
                x = only(x, True)
                if x is None:
                    return
                need(act, S["c_qT_ps"], x.un + 1)
                need(act, S["c_wo_ev"], x.un - RING + 1)
                act.activation(q_sb[x.r], bank_m[:, :], ACT.Identity, bias=st_qk[x.half][:, 3 * P:3 * P + 1]).then_inc(S["c_q_ev"], 1)

            def ev_kh(x):
                if x is None:
                    return
                need(act, S["c_kh_ps"], x.u + 1)
                if x.c.node:
                    need(act, S["c_sp"], 2 * x.u - 1)
                    act.activation(kf, bank_m[:, :], ACT.Identity, bias=st_qk[x.half][:, 3 * P + 1:WA]).then_inc(S["c_kf_ev"], 1)
                else:
                    need(act, S["c_sp"], 2 * x.u)
                    act.activation(kf, bank_m[:, :], ACT.Copy).then_inc(S["c_kf_ev"], 1)

            def ev_qh(x):
                x = only(x, True)
                if x is None:
                    return
                need(act, S["c_qh_ps"], x.un + 1)
                need(act, S["c_sp"], 2 * x.u)
                act.activation(qf, bank_m[:, :], ACT.Copy).then_inc(S["c_qf_ev"], 1)

            def ev_v(x):
                if x is None:
                    return
                need(act, S["c_v_ps"], x.u + 1)
                need(act, S["c_pv_ps"], 4 * (x.u - 2) + 4)
                act.activation(vaug[x.half][:, :, :, 0:x.c.hd],
                               bank_m[:, 0:NT * x.c.np_].rearrange("p (k h m) -> p k h m", k=NT, h=HU), ACT.Copy).then_inc(S["c_v_ev"], 1)

            def ev_m(x, k):
                if x is None:
                    return
                G = 2 * x.u + k
                need(act, S["c_mT_ps"], G + 1)
                need(act, S["c_m_dma"], 16 * G)
                act.activation(mT[0:48, :], bank_m[0:48, 0:P], ACT.Copy).then_inc(S["c_mT_ev"], 1)
                need(act, S["c_mT_ev"], G + 1)
                act.dma_start(qst[x.c.R:x.c.R3, x.r, GH * k:GH * k + GH, :], mT[0:48, :]).then_inc(S["c_m_dma"], 16)

            def ev_pv(x, k):
                if x is None:
                    return
                G = 2 * x.u + k
                need(act, S["c_pv_ps"], 2 * G + 2)
                need(act, S["c_ot_ps"], G)
                act.activation(ot_sb, bank_o[:, :], ACT.Copy).then_inc(S["c_pv_ev"], 1)

            def ev_cT(x):
                x = only(x, True)
                if x is None:
                    return
                need(act, S["c_cT_ps"], x.un + 1)
                need(act, S["c_wo_ps"], x.un)
                act.activation(ctxT, bank_m[:, :], ACT.Copy).then_inc(S["c_cT_ev"], 1)

            def ev_x3T(x):
                x = only(x, False)
                if x is None or not x.half:
                    return
                need(act, S["c_x3T_ps"], x.b + 1)
                need(act, S["c_store"], 16 * x.b)
                act.activation(no_sb, bank_m[:, :], ACT.Copy).then_inc(S["c_x3T_ev"], 1)

            def ev_final(x):
                j = final(x)
                if j is None:
                    return
                need(act, S["f_tT_ps"], j + 1)
                need(act, S["f_nm"], j)
                act.activation(nT, bank_m[:, :], ACT.Copy).then_inc(S["f_tT_ev"], 1)

            def exp(x, k, i):
                G = 2 * x.u + k
                kp, h = i // GH, i % GH
                need(act, S["c_st_ps"], 8 * G + i + 1)
                if h == 0:
                    need(act, S["c_pv_ps"], 2 * (G - 1) + kp + 1)
                act.activation(PT[:, kp, h, :, :], bank_x[:, i % 2, :].rearrange("p (c n) -> p c n", c=2),
                               ACT.Exp, scale=x.c.scale).then_inc(S["c_ex"], 1)

            def scale(b, t):
                now(act, "b_e_ps", b, NT, t + 1)
                need(act, S["b_red"], NT * b + t)
                for e_ in range(NE):
                    i = act.activation(scaled[t % 2][:, e_, :], bank_x[:, t % 2, e_ * D:(e_ + 1) * D], ACT.Identity, scale=lgm[:, t, e_:e_ + 1])
                i.then_inc(S["b_sc"], 1)

            def body(b):
                b1, b2 = b - 1, b - 2
                if batch(b1):
                    now(act, "b_xT_ps", b1)
                    before(act, "b_e_ps", b1, NT)
                    act.activation(hT, bank_m[:, :], ACT.Copy).then_inc(S["b_xT_ev"], 1)
                    now(act, "b_lg", b1)
                    before(act, "b_mg", b1)
                    for t in range(NT):
                        act.activation(lge[:, t, :], lg[:, t, :], ACT.Exp, bias=nmx[:, t:t + 1],
                                       accum_out=sm[:, t:t + 1]).then_inc(S["b_ex"], 1)
                    now(act, "b_mg", b1)
                    scale(b1, 0)
                    now(act, "b_mgT_ps", b1)
                    before(act, "b_yb_ps", b1)
                    act.activation(mgT, bank_m[0:NE, :], ACT.Copy).then_inc(S["b_mgT_ev"], 1)
                    for t in range(1, NT):
                        scale(b1, t)
                if batch(b2):
                    now(act, "b_x2T_ps", b2)
                    before(act, "b_outT", b2, 16)
                    act.activation(x2Tw, bank_m[:, :], ACT.Copy).then_inc(S["b_x2T_ev"], 1)
                if isinstance(b, int) and b == NB:
                    ev_kh(at_(kc, 0, 0))
            staged(act, body, 3)

            ev_v(at_(kc, 0, 0))
            ev_kh(at_(kc, 0, 1))
            ev_m(at_(kc, 0, 0), 0)
            ev_kh(at_(kc, 0, 2))

            def body(c, q, r):
                x, last, ahead = at_(c, q, r), at_(c, q, r - 1), at_(c, q, r + 3)
                for k in range(2):
                    for i in range(8):
                        exp(x, k, i)
                        if i == paced(x, 1, 3):
                            ev_pv(*((last, 1) if k == 0 else (x, 0)))
                        if i == paced(x, 5, 4):
                            ev_m(*led_group(c, q, r, k))
                        if k == 0:
                            if i == paced(x, 2, 7):
                                ev_v(at_(c, q, r + 1))
                            if i == 6:
                                ev_cT(last)
                        else:
                            if i == 1:
                                ev_final(last)
                            if i == 2:
                                ev_qT(ahead)
                                ev_kh(only(ahead, False))
                            if i == 6:
                                ev_kh(only(ahead, True))
                            if i == 7:
                                ev_qh(ahead)
                                ev_x3T(last)
            units(act, body)
            end = at_(kn, QU - 1, RING - 1)
            ev_pv(end, 1)
            ev_cT(end)
            ev_final(end)

        @block.tensor
        def _(pe):
            pe.wait_ge(s_id, 4)
            pe.wait_ge(s_w, 16 * N_W)
            xs_at = lambda b, h: xs_all[:, bass.ds((b * NH + h) * L, L)]

            def body(b):
                b0, b1, b2 = b, b - 1, b - 2
                if batch(b0):
                    now(pe, "a_hn", b0)
                    before(pe, "a_hT_ev", b0)
                    for t in range(NT):
                        mm = pe.transpose(bank_m[:, t * P:(t + 1) * P], hn[:, t * P:(t + 1) * P], ident[:, :])
                    mm.then_inc(S["a_hT_ps"], 1)
                    now(pe, "a_hT_ev", b0)
                    before(pe, "a_xs_ev", b0)
                    before(pe, "a_g_ev", b0)
                    for j in range(2 * NH):
                        mm = pe.matmul(sec(bank_x[:, j // NH, :], j % NH), w_in[:, j * P:(j + 1) * P], hT, start=True, stop=True)
                    mm.then_inc(S["a_win_ps"], 1)
                if batch(b2):
                    now(pe, "a_sp", b2)
                    before(pe, "a_mb_ev", b2)
                    for k in range(NH):
                        pe.matmul(bank_o[COL:COL + NS, :], mean_w[:, :], rl[:, k, :], start=(k == 0), stop=(k == NH - 1))
                        mm = pe.matmul(bank_o[0:NS, :], bmt[:, k, :], xs_at(b2, k), start=(k == 0), stop=(k == NH - 1))
                    mm.then_inc(S["a_mb_ps"], 1)
                if batch(b1):
                    now(pe, "a_xs", b1)
                    before(pe, "a_z_ev", b1, NH)
                    for h in range(NH):
                        for k in range(NH):
                            mm = pe.matmul(bank_s[:, h, :], wd[:, k, h * P:(h + 1) * P], xs_at(b1, k),
                                           start=(k == 0), stop=(k == NH - 1))
                    mm.then_inc(S["a_z_ps"], 1)
            staged(pe, body, 3)

            pe.wait_ge(S["p_in"], 16)
            pe.wait_ge(s_w2, 16 * N_W2)
            pe.wait_ge(S["a_g_ev"], NB + 1)
            pe.wait_ge(S["a_z_ev"], NH * NB + 1)
            for c in range(NODES):
                pe.matmul(bx0[:, c * P:(c + 1) * P], wv(c, "WeKT"), wv(c, "WkP"), start=True, stop=True)
                pe.matmul(bx1[:, c * P:(c + 1) * P], wv(c, "WeVT"), wv(c, "Wv"), start=True, stop=True)
                pe.matmul(bank_s[:, 0, c:c + 1], wv(c, "WkP"), vec(c, 1), start=True, stop=True)
                mm = pe.matmul(bank_s[:, 0, NODES + c:NODES + c + 1], wv(c, "Wv"), vec(c, 2), start=True, stop=True)
            mm.then_inc(S["p_mm"], 1)
            pe.wait_ge(S["p_ev"], 1)
            pe.wait_ge(S["a_mb_ev"], NB + 1)
            for c in range(NODES):
                mm = pe.matmul(bank_o[:, c:c + 1], po_sb[:, c, WA + P:WA + 2 * P], bv_sb[:, c:c + 1], start=True, stop=True)
            mm.then_inc(S["p_mm"], 1)

            reader = [None]

            def misc(sem_, value):
                if reader[0] is not None:
                    need(pe, *reader[0])
                reader[0] = (sem_, value)

            def proj_q(x):
                x = only(x, True)
                if x is None:
                    return
                t = st_qk[x.half]
                need(pe, S[f"c_qk{x.half}"], loaded(x, kn.loads_qk))
                misc(S["c_q_ev"], x.un + 1)
                pe.matmul(bank_m[:, :], t[:, 0:P], t[:, WA:WA + L], start=True, stop=True).then_inc(S["c_qT_ps"], 1)

            def proj_kh(x):
                if x is None:
                    return
                t = st_qk[x.half]
                need(pe, S[f"c_qk{x.half}"], loaded(x, kn.loads_qk))
                misc(S["c_kf_ev"], x.u + 1)
                w, src = (t[:, 2 * P:3 * P], t[:, WA + L:WA + 2 * L]) if x.c.node else (wc[:, x.half, :], t[:, WA:WA + L])
                pe.matmul(bank_m[:, :], w, src, start=True, stop=True).then_inc(S["c_kh_ps"], 1)

            def proj_qh(x):
                x = only(x, True)
                if x is None:
                    return
                need(pe, S["c_q_ev"], x.un + 1)
                misc(S["c_qf_ev"], x.un + 1)
                pe.matmul(bank_m[:, :], st_qk[x.half][:, P:2 * P], q_sb[x.r], start=True, stop=True).then_inc(S["c_qh_ps"], 1)

            def value(x):
                if x is None:
                    return
                t, n = st_v[x.half], x.c.np_
                need(pe, S[f"c_v{x.half}"], loaded(x, kn.loads_v))
                misc(S["c_v_ev"], x.u + 1)
                w = t[:, 0:P] if x.c.node else wc[:, 2, x.half * n:(x.half + 1) * n]
                for k in range(NT):
                    mm = pe.matmul(bank_m[:, k * n:(k + 1) * n], t[:, P + k * P:P + (k + 1) * P], w, start=True, stop=True)
                mm.then_inc(S["c_v_ps"], 1)

            def scores(x, k, n):
                if x is None:
                    return
                N = 16 * (2 * x.u + k) + n
                if k == 0 and n == 0:
                    need(pe, S[f"c_stk{x.r}"], stacked(x))
                need(pe, S["c_red"], N - 1)
                h, t = GH * k + n // NT, n % NT
                pe.matmul(bank_s[:, n % 2, :], qst[0:x.c.R, x.r, h, t * P:(t + 1) * P], kst[0:x.c.R, x.r, h, :],
                          start=True, stop=True).then_inc(S["c_s_ps"], 1)

            def maxima(x, k):
                if x is None:
                    return
                G = 2 * x.u + k
                need(pe, S["c_nm_ok"], G + 1)
                misc(S["c_mT_ev"], G + 1)
                pe.matmul(bank_m[0:48, 0:P], mp[:, 0:48], identb[:, :], start=True, stop=True).then_inc(S["c_mT_ps"], 1)

            def scoresT(x, k, i):
                G = 2 * x.u + k
                kp, h = i // GH, GH * k + i % GH
                if i == 0:
                    need(pe, S["c_m_dma"], 16 * (G + 1))
                need(pe, S["c_ex"], 8 * G + i - 1)
                for j in range(2):
                    kc_ = 2 * kp + j
                    mm = pe.matmul(sec(bank_x[:, i % 2, :], j), kst[0:x.c.R3, x.r, h, kc_ * P:(kc_ + 1) * P],
                                   qst[0:x.c.R3, x.r, h, :], start=True, stop=True)
                mm.then_inc(S["c_st_ps"], 1)

            def output(x, k, kp, step, steps):
                if x is None or not 0 <= step < steps:
                    return
                G = 2 * x.u + k
                j, cols = 2 * step // steps, slice(0, L) if steps == 2 else slice(step % 2 * L // 2, (step % 2 + 1) * L // 2)
                if step == 0:
                    need(pe, S["c_ex"], 8 * G + 4 * kp + 4)
                    if kp == 0:
                        need(pe, S["c_pv_ev"], G)
                        need(pe, S["c_v_ev"], x.u + 1)
                for h in range(GH):
                    mm = pe.matmul(bank_o[COL * h:COL * (h + 1), cols], vaug[x.half][:, 2 * kp + j, GH * k + h, :],
                                   PT[:, kp, h, j, cols], start=(kp == 0 and step == 0),
                                   stop=(kp == 1 and step == steps - 1))
                if step == steps - 1:
                    mm.then_inc(S["c_pv_ps"], 1)

            def turn(x, k):
                if x is None:
                    return
                G = 2 * x.u + k
                need(pe, S["c_pv_ev"], G + 1)
                misc(S["c_ot_ev"], G + 1)
                for t in range(NT):
                    mm = pe.transpose(bank_m[:, t * P:(t + 1) * P], ot_sb[:, t * P:(t + 1) * P], ident[:, :])
                mm.then_inc(S["c_ot_ps"], 1)

            def turn_ctx(x):
                x = only(x, True)
                if x is None:
                    return
                need(pe, S["c_ot_ev"], 2 * x.u + 2)
                misc(S["c_cT_ev"], x.un + 1)
                for t in range(NT):
                    mm = pe.transpose(bank_m[:, t * P:(t + 1) * P], ctx_sb[:, t * P:(t + 1) * P], ident[:, :])
                mm.then_inc(S["c_cT_ps"], 1)

            def out_proj(x):
                x = only(x, True)
                if x is None:
                    return
                need(pe, S[f"c_o{x.half}"], loaded(x, 1, 0))
                need(pe, S["c_cT_ev"], x.un + 1)
                misc(S["c_wo_ev"], x.un + 1)
                pe.matmul(bank_m[:, :], st_o[x.half][:, 0:P], ctxT, start=True, stop=True).then_inc(S["c_wo_ps"], 1)

            def turn_x3(x):
                x = only(x, False)
                if x is None or not x.half:
                    return
                need(pe, S["c_x3"], x.b + 1)
                misc(S["c_x3T_ev"], x.b + 1)
                for t in range(NT):
                    mm = pe.transpose(bank_m[:, t * P:(t + 1) * P], x3s[:, t * P:(t + 1) * P], ident[:, :])
                mm.then_inc(S["c_x3T_ps"], 1)

            def turn_final(x):
                j = final(x)
                if j is None:
                    return
                need(pe, S["c_wo_ev"], x.un + 1)
                misc(S["f_tT_ev"], j + 1)
                for t in range(NT):
                    mm = pe.transpose(bank_m[:, t * P:(t + 1) * P], no_sb[:, t * P:(t + 1) * P], ident[:, :])
                mm.then_inc(S["f_tT_ps"], 1)

            def experts(b, t):
                need(pe, S["b_sc"], NT * b + t)
                for j in range(2):
                    mm = pe.matmul(sec(bank_x[:, t % 2, :], j), hT[:, t * P:(t + 1) * P], xw[:, j * 512:(j + 1) * 512],
                                   start=True, stop=True)
                mm.then_inc(S["b_e_ps"], 1)

            def states(b, h):
                pe.matmul(bank_s[:, h, :], cmt[:, h * P:(h + 1) * P], hsb, start=True, stop=True).then_inc(S["b_c_ps"], 1)

            def body(b):
                b0, b1, b2 = b, b - 1, b - 2
                if batch(b1):
                    now(pe, "b_x1", b1)
                    need(pe, S["b_x2T_ev"], b1)
                    for t in range(NT):
                        mm = pe.transpose(bank_m[:, t * P:(t + 1) * P], hn[:, t * P:(t + 1) * P], ident[:, :])
                    mm.then_inc(S["b_xT_ps"], 1)
                if batch(b0):
                    now(pe, "b_hs", b0, 16)
                    before(pe, "b_y", b0)
                    need(pe, S["b_acc"], b0)
                    states(b0, 0)
                if batch(b1):
                    now(pe, "b_xT_ev", b1)
                    for t in range(NT):
                        mm = pe.matmul(bank_m[:, t * NE:(t + 1) * NE], hT[:, t * P:(t + 1) * P], rw[:, :], start=True, stop=True)
                    mm.then_inc(S["b_lg_ps"], 1)
                if batch(b0):
                    states(b0, 1)
                if batch(b1):
                    experts(b1, 0)
                    experts(b1, 1)
                if batch(b0):
                    now(pe, "b_y", b0)
                    before(pe, "b_mv", b0)
                    for t in range(NT):
                        for k in range(NH):
                            mm = pe.matmul(bank_o[:, t * P:(t + 1) * P], yh[:, k, t * P:(t + 1) * P], woh[:, k, :],
                                           start=(k == 0), stop=(k == NH - 1))
                    mm.then_inc(S["b_yo_ps"], 1)
                if batch(b1):
                    now(pe, "b_mg", b1)
                    for t in range(NT):
                        mm = pe.transpose(bank_m[0:NE, t * P:(t + 1) * P], lgm[:, t, :], ident[:, :])
                    mm.then_inc(S["b_mgT_ps"], 1)
                    experts(b1, 2)
                    now(pe, "b_mgT_ev", b1)
                    for t in range(NT):
                        mm = pe.matmul(bank_s[:, 0, t * P:(t + 1) * P], mgT[:, t * P:(t + 1) * P], xb[:, :], start=True, stop=True)
                    mm.then_inc(S["b_yb_ps"], 1)
                    experts(b1, 3)
                if batch(b2):
                    now(pe, "b_x2", b2)
                    if isinstance(b, int) and b == NB + 1:
                        misc(S["b_x2T_ev"], NB + 1)
                    else:
                        before(pe, "b_x2T_ev", b2)
                    for t in range(NT):
                        mm = pe.transpose(bank_m[:, t * P:(t + 1) * P], x2w[:, t * P:(t + 1) * P], ident[:, :])
                    mm.then_inc(S["b_x2T_ps"], 1)
                if isinstance(b, int) and b == NB:
                    reader[0] = (S["b_x2T_ev"], NB)
                    proj_kh(at_(kc, 0, 0))
            staged(pe, body, 3)

            pe.wait_ge(S["c_ones"], RING)
            value(at_(kc, 0, 0))
            proj_kh(at_(kc, 0, 1))
            for n in range(16):
                scores(at_(kc, 0, 0), 0, n)
            maxima(at_(kc, 0, 0), 0)
            for n in range(12):
                scores(at_(kc, 0, 0), 1, n)
            proj_kh(at_(kc, 0, 2))

            def ring_reader(c, q):
                return (S["c_qf_ev"], RING * q + 3 - UC) if c.node else (S["c_ot_ev"], 2 * RING * q - 1)

            def body(c, q, r):
                x, last, ahead = at_(c, q, r), at_(c, q, r - 1), at_(c, q, r + 3)
                in_loop = not isinstance(q, int)
                if in_loop and r == 0:
                    reader[0] = ring_reader(c, q)
                steps = paced(x, 2, 4)
                for k in range(2):
                    for i in range(8):
                        one, two = led(c, q, r, k, i)
                        scores(*one)
                        scoresT(x, k, i)
                        scores(*two)
                        if i == paced(x, 5, 4):
                            maxima(*led_group(c, q, r, k))
                        output(*((last, 1) if k == 0 else (x, 0)), 1, i, steps)
                        output(x, k, 0, i - 4, steps)
                        if i == paced(x, 3, 5):
                            turn(*((last, 1) if k == 0 else (x, 0)))
                        if k == 0:
                            if i == paced(x, 2, 7):
                                value(at_(c, q, r + 1))
                            if i == 6:
                                turn_ctx(last)
                            if i == 7:
                                out_proj(last)
                        else:
                            if i == 1:
                                turn_final(last)
                            if i == 2:
                                proj_q(ahead)
                                proj_kh(only(ahead, False))
                            if i == 6:
                                proj_kh(only(ahead, True))
                            if i == 7:
                                proj_qh(ahead)
                                turn_x3(last)
                if in_loop and r == RING - 1:
                    reader[0] = ring_reader(c, QU - 2 if c.node else QC - 1)
            units(pe, body)
            end = at_(kn, QU - 1, RING - 1)
            for step in range(2):
                output(end, 1, 1, step, 2)
            turn(end, 1)
            turn_ctx(end)
            out_proj(end)
            turn_final(end)

        @block.vector
        def _(dve):
            dve.wait_ge(s_w, 16 * N_W)
            dve.wait_ge(s_c, 7 + NE)
            dve.tensor_scalar(cvh[:, :, :], cv[:, :, 0:KC + 1], 0.5, None, ALU.mult).then_inc(s_c, 1)
            dve.tensor_scalar(woh[:, :, :], w_out[:, :, :], 0.5, None, ALU.mult).then_inc(s_c, 1)

            def stats(src, st_, mv_, link, base, done):
                for t in range(NT):
                    dve.bn_stats(st_[:, t, :], src[:, t * D:(t + 1) * D]).then_inc(link, 1)
                need(dve, link, base + NT)
                dve.sem_inc(passed, 1)
                for t in range(NT):
                    i = dve.bn_aggr(mv_[:, t, :], st_[:, t, :])
                i.then_inc(done, 1)

            def normalise(dst, src, mv_, rs_, done):
                for t in range(NT):
                    i = dve.tensor_scalar(dst[:, t * D:(t + 1) * D], src[:, t * D:(t + 1) * D], mv_[:, t, 0:1], rs_[:, t:t + 1],
                                          ALU.subtract, ALU.mult)
                i.then_inc(done, 1)

            class Links:

                def __init__(self, name, per, b):
                    self.sem, self.per, self.b, self.n = S[name], per, b, 0

                def count(self, ins):
                    self.n += 1
                    assert self.n <= self.per
                    return ins.then_inc(self.sem, 1)

                def base(self):
                    return self.per * self.b + 1 + self.n

                def wait(self, back=0):
                    dve.wait_ge(self.sem, self.base() - back)

            xtf = xt.rearrange("p t d -> p (t d)")
            halves = lambda t, b: t[:, bass.ds(b * NH * L, NH * L)]
            flat = lambda t: t.rearrange("p h n -> p (h n)")
            dve.wait_ge(s_c, 7 + NE + 2)

            def body(b):
                b0, b1, b2 = b, b - 1, b - 2
                if batch(b0):
                    now(dve, "a_x", b0, 16)
                    before(dve, "a_hn", b0)
                    stats(xtf, sta, mva, S["a_link"], NT * b0 + 1, S["a_mv"])
                if batch(b1):
                    now(dve, "a_xs_ev", b1)
                    before(dve, "a_xs", b1)
                    v = Links("a_link2", NH * KC - 1, b1)
                    taps(v, range(0, 2))
                if batch(b0):
                    now(dve, "a_rs", b0)
                    before(dve, "a_hT_ps", b0)
                    normalise(hn, xtf, mva, rsa, S["a_hn"])
                if batch(b1):
                    taps(v, range(2, KC))
                if batch(b2):
                    now(dve, "a_ln", b2)
                    dve.scalar_tensor_tensor(rl, rl, 0.0, ab, ALU.max, ALU.add).then_inc(S["a_sp"], 1)
                if batch(b1):
                    now(dve, "a_th", b1)
                    now(dve, "a_yh", b1)
                    dve.scalar_tensor_tensor(halves(xs_all, b1), flat(tg), 1.0, flat(yh), ALU.add, ALU.mult).then_inc(S["a_xs"], 1)
                if batch(b0):
                    now(dve, "a_tg", b0)
                    dve.scalar_tensor_tensor(halves(sg_all, b0), flat(tg), 1.0, bx1, ALU.add, ALU.mult).then_inc(S["a_g_ev"], 1)
                if batch(b1):
                    now(dve, "a_z_ps", b1)
                    before(dve, "a_mb_ps", b1)
                    for h in range(NH):
                        dve.tensor_scalar(rl[:, h, :], bank_s[:, h, :], cv[:, h, KC + 2:KC + 3], None, ALU.add).then_inc(S["a_z_ev"], 1)

            def taps(v, js):
                for j in js:
                    for h in range(NH):
                        if j == 0:
                            i = dve.tensor_scalar(yh[:, h, :], cbuf[:, h, KC:KC + L], cvh[:, h, KC - 1:KC], cvh[:, h, KC:KC + 1],
                                                  ALU.mult, ALU.add)
                        else:
                            v.wait(1)
                            i = dve.scalar_tensor_tensor(yh[:, h, :], cbuf[:, h, KC - j:KC - j + L],
                                                         cvh[:, h, KC - 1 - j:KC - j], yh[:, h, :], ALU.mult, ALU.add)
                        if (j, h) == (KC - 1, NH - 1):
                            i.then_inc(S["a_yh"], 1)
                        else:
                            v.count(i)
            staged(dve, body, 3)

            dve.wait_ge(S["r_in"], 16)
            dve.tensor_tensor(hT, db[:, 1, :], db[:, 0, :], ALU.mult).then_inc(S["r_bx"], 1)
            dve.wait_ge(S["r_dA"], 1)
            dve.wait_ge(S["r_bx"], 1)
            dve.tensor_tensor_scan(hs, hn, hT, 0.0, ALU.mult, ALU.add).then_inc(S["r_hs"], 1)

            dve.wait_ge(S["p_mm"], 1)
            dve.wait_ge(s_w2, 16 * N_W2)
            for c in range(NODES):
                po = po_sb[:, c, :]
                dve.tensor_scalar(po[:, 0:P], wv(c, "WeQ"), vec(c, 3), None, ALU.mult)
                dve.tensor_copy(po[:, P:2 * P], wv(c, "WqP"))
                dve.tensor_scalar(po[:, 2 * P:3 * P], bx0[:, c * P:(c + 1) * P], vec(c, 4), None, ALU.mult)
                dve.tensor_scalar(po[:, 3 * P:3 * P + 1], vec(c, 0), vec(c, 3), None, ALU.mult)
                dve.tensor_scalar(po[:, 3 * P + 1:WA], bank_s[:, 0, c:c + 1], vec(c, 4), None, ALU.mult)
                dve.tensor_scalar(po[:, WA:WA + P], bx1[:, c * P:(c + 1) * P], vec(c, 5), None, ALU.mult)
                dve.tensor_scalar(bv_sb[:, c:c + 1], bank_s[:, 0, NODES + c:NODES + c + 1], vec(c, 5), None, ALU.mult)
                i = dve.tensor_scalar(po[:, WA + P:WA + 2 * P], wv(c, "Wo"), vec(c, 6), None, ALU.mult)
            i.then_inc(S["p_ev"], 1)
            dve.wait_ge(S["p_mm"], 2)
            dve.tensor_copy(po_sb[:, :, WN - 1], bank_o[:, 0:NODES]).then_inc(S["p_ev"], 1)

            def body(b):
                b0, b1, b2 = b, b - 1, b - 2
                A, B = Links("b_link", 2 + 1 + NT, b0), Links("b_link2", 7 + 1 + NT, b1)
                if batch(b1):
                    now(dve, "b_lg_ps", b1)
                    B.count(dve.tensor_tensor(lg, bank_m[:, 0:NT * NE].rearrange("p (t e) -> p t e", t=NT),
                                              rb[:, :].unsqueeze(1).broadcast_to([P, NT, NE]), ALU.add))
                    B.wait()
                    B.count(dve.tensor_reduce(mx, lg, AX.X, ALU.max))
                    B.wait()
                    dve.tensor_scalar(nmx, mx, -1.0, None, ALU.mult).then_inc(S["b_lg"], 1)
                    before(dve, "b_mgT_ps", b1)
                    before(dve, "b_sc", b1, NT)
                    B.count(dve.tensor_tensor(lgm, lg, mx.unsqueeze(2).broadcast_to([P, NT, NE]), ALU.is_equal))
                if batch(b0):
                    for h in range(NH):
                        now(dve, "b_c_ps", b0, 2, h + 1)
                        A.count(dve.scalar_tensor_tensor(yh[:, h, :], xs_all[:, bass.ds((b0 * NH + h) * L, L)], cv[:, h, KC + 1:KC + 2],
                                                         bank_s[:, h, :], ALU.mult, ALU.add))
                if batch(b1):
                    B.wait()
                    B.count(dve.tensor_tensor(lgm, lgm, rank[:, :].unsqueeze(1).broadcast_to([P, NT, NE]), ALU.mult))
                if batch(b0):
                    A.wait()
                    dve.tensor_tensor(flat(yh), flat(yh), halves(sg_all, b0), ALU.mult).then_inc(S["b_y"], 1)
                if batch(b1):
                    B.wait()
                    B.count(dve.tensor_reduce(fm, lgm, AX.X, ALU.max))
                    B.wait()
                    B.count(dve.tensor_tensor(lgm, lgm, fm.unsqueeze(2).broadcast_to([P, NT, NE]), ALU.is_equal))
                    now(dve, "b_ex", b1, NT)
                    B.count(dve.reciprocal(mx, sm))
                    B.wait()
                    dve.tensor_tensor(lgm, lgm, mx.unsqueeze(2).broadcast_to([P, NT, NE]), ALU.mult).then_inc(S["b_mg"], 1)
                if batch(b2):
                    now(dve, "b_rs2", b2)
                    before(dve, "b_x2T_ps", b2)
                    before(dve, "b_out", b2, 16)
                    normalise(x2w, tg[:, 1, :], mvb, rsb, S["b_x2"])
                if batch(b0):
                    now(dve, "b_x", b0, 16)
                    now(dve, "b_yo_ps", b0)
                    before(dve, "b_x1", b0)
                    A.count(dve.scalar_tensor_tensor(tg[:, 0, :], xtf, 2.0, bank_o[:, :], ALU.mult, ALU.add))
                    A.wait()
                    stats(tg[:, 0, :], sta, mva, A.sem, A.base(), S["b_mv"])
                if batch(b1):
                    for t in range(2):
                        expert_sum(b1, t)
                    now(dve, "b_yb_ps", b1)
                    before(dve, "b_x2", b1)
                    dve.tensor_tensor(tg[:, 1, :], bank_s[:, 0, :], hn, ALU.add).then_inc(S["b_acc"], 1)
                if batch(b0):
                    now(dve, "b_rs", b0)
                    before(dve, "b_xT_ps", b0)
                    before(dve, "b_acc", b0)
                    normalise(hn, tg[:, 0, :], mva, rsa, S["b_x1"])
                if batch(b1):
                    for t in range(2, NT):
                        expert_sum(b1, t)
                    now(dve, "b_red", b1, NT)
                    now(dve, "b_acc", b1)
                    B.count(dve.tensor_tensor(tg[:, 1, :], tg[:, 1, :], esum, ALU.add))
                    B.wait()
                    stats(tg[:, 1, :], sta, mvb, B.sem, B.base(), S["b_mv2"])

            def expert_sum(b, t):
                now(dve, "b_sc", b, NT, t + 1)
                dve.tensor_reduce(esum[:, t * D:(t + 1) * D], scaled[t % 2].rearrange("p e d -> p d e"), AX.X, ALU.add).then_inc(S["b_red"], 1)
            staged(dve, body, 3)

            def reduce(x, k, n):
                if x is None:
                    return
                need(dve, S["c_s_ps"], 16 * (2 * x.u + k) + n + 1)
                dve.tensor_reduce(nm[:, k, n:n + 1], bank_s[:, n % 2, :], AX.X, ALU.max, negate=True).then_inc(S["c_red"], 1)

            def parts(x, k, step):
                if x is None:
                    return
                G = 2 * x.u + k
                if step == 0:
                    need(dve, S["c_red"], 16 * G + 16)
                    need(dve, S["c_mT_ps"], G)
                    dve.tensor_copy(mp[:, 0:16], nm[:, k, :]).then_inc(S["c_link"], 1)
                else:
                    need(dve, S["c_link"], 3 * G + step)
                if step == 1:
                    dve.tensor_tensor(mr, nm[:, k, :], mp[:, 0:16], ALU.subtract).then_inc(S["c_link"], 1)
                if step == 2:
                    dve.tensor_copy(mp[:, 16:32], mr).then_inc(S["c_link"], 1)
                if step == 3:
                    dve.tensor_tensor(mp[:, 32:48], mr, mp[:, 16:32], ALU.subtract).then_inc(S["c_nm_ok"], 1)

            o4 = bank_m[:, :].rearrange("p (t h m) -> p t h m", t=NT, h=GH)

            def divide(x, k, step):
                if x is None:
                    return
                G = 2 * x.u + k
                w = GH * x.c.hd
                if step == 0:
                    need(dve, S["c_ot_ps"], G + 1)
                    dve.reciprocal(rec, o4[:, :, :, x.c.hd]).then_inc(S["c_sum"], 1)
                    return
                if x.c.node and k == 0:
                    need(dve, S["c_cT_ps"], x.un)
                first = k * w if x.c.node else x.half * 2 * w + k * w
                dst = ctx_sb.rearrange("p (t m) -> p t m", t=NT)[:, :, first:first + w]
                need(dve, S["c_sum"], G + 1)
                dve.tensor_tensor(dst.rearrange("p t (h m) -> p t h m", h=GH), o4[:, :, :, 0:x.c.hd],
                                  rec.unsqueeze(3).broadcast_to([P, NT, GH, x.c.hd]), ALU.mult).then_inc(S["c_ot_ev"], 1)

            def node_out(x):
                x = only(x, True)
                if x is None:
                    return
                need(dve, S["c_wo_ps"], x.un + 1)
                if final(x):
                    need(dve, S["f_tT_ps"], final(x))
                else:
                    need(dve, S["c_store"], 16 * (NB + x.un))
                dve.scalar_tensor_tensor(no_sb, bank_m[:, :], st_o[x.half][:, P:P + 1], q_sb[x.r], ALU.add, ALU.add).then_inc(S["c_wo_ev"], 1)

            def residual(x, step):
                x = only(x, False)
                if x is None or not x.half:
                    return
                if step == 0:
                    need(dve, S["c_x2in"], 16 * x.b + 16)
                    need(dve, S["c_ot_ev"], 4 * x.b + 4)
                    dve.tensor_tensor(ctx_sb, ctx_sb, x2s, ALU.add).then_inc(S["c_xlink"], 1)
                if step == 1:
                    need(dve, S["c_xlink"], (NT + 1) * x.b + 1)
                    stats(ctx_sb, stt, mv, S["c_xlink"], (NT + 1) * x.b + 1, S["c_mv"])
                if step == 2:
                    need(dve, S["c_rs"], x.b + 1)
                    need(dve, S["c_x3T_ps"], x.b)
                    need(dve, S["c_x3out"], 16 * x.b)
                    normalise(x3s, ctx_sb, mv, rs, S["c_x3"])

            def final_norm(x, step):
                j = final(x)
                if j is None:
                    return
                if step == 0:
                    need(dve, S["f_tT_ev"], j + 1)
                    stats(nT, stt, mv, S["f_link"], NT * j, S["f_mv"])
                if step == 1:
                    need(dve, S["f_rs"], j + 1)
                    need(dve, S["f_y"], j)
                    normalise(zn, nT, mv, rs, S["f_nm"])
                if step == 2:
                    need(dve, S["f_z"], j + 1)
                    stats(zn, stt2, mv2, S["f_link2"], NT * j, S["f_mv2"])
                if step == 3:
                    need(dve, S["f_rs2"], j + 1)
                    need(dve, S["f_out"], 16 * j)
                    normalise(x3s, zn, mv2, rs2, S["f_y"])

            for n in range(16):
                reduce(at_(kc, 0, 0), 0, n)
            for step in range(4):
                parts(at_(kc, 0, 0), 0, step)
            for n in range(12):
                reduce(at_(kc, 0, 0), 1, n)

            def body(c, q, r):
                x, last = at_(c, q, r), at_(c, q, r - 1)
                for k in range(2):
                    for i in range(8):
                        for j, group in enumerate(led(c, q, r, k, i)):
                            if i == paced(x, 4, 6):
                                divide(*((last, 1) if k == 0 else (x, 0)), j)
                            reduce(*group)
                            if i in (2, 3):
                                parts(*led_group(c, q, r, k), 2 * (i - 2) + j)
                        if (k, i) == (0, paced(x, 5, 7)):
                            residual(last, 0)
                        if (k, i) == (1, 0):
                            residual(last, 1)
                            node_out(last)
                        if (k, i) == (1, 3):
                            residual(last, 2)
                            final_norm(last, 0)
                        if (k, i) == (1, 5):
                            final_norm(last, 1)
                        if (k, i) == (0, 1):
                            final_norm(at_(c, q, r - 2), 2)
                        if (k, i) == (0, 7):
                            final_norm(at_(c, q, r - 2), 3)
            units(dve, body)
            end, last = at_(kn, QU - 1, RING - 1), at_(kn, QU - 1, RING - 2)
            final_norm(last, 2)
            for step in range(2):
                divide(end, 1, step)
            final_norm(last, 3)
            node_out(end)
            for step in range(4):
                final_norm(end, step)


def kernel(**inputs):
    import numpy as np
    import concourse.bacc as bacc
    from concourse.bass_utils import run_bass_kernel_spmd

    i = {k: np.asarray(v) for k, v in inputs.items()}
    rows = lambda v: np.ascontiguousarray(np.broadcast_to(v, (P,) + v.shape))
    blocks = lambda w: np.ascontiguousarray(w.reshape(NH, P, -1).transpose(1, 0, 2))

    def dims_first(w, heads):
        return w.reshape(P, heads, -1).transpose(0, 2, 1).reshape(P, -1)

    wckq = np.stack([np.concatenate([dims_first(i["L1_attn_w_" + w][:, h * 64:(h + 1) * 64], HU) for w in "KQ"], 1)
                     for h in range(2)], 1)

    col = lambda v: v.reshape(NH, P).T[:, :, None]
    zero = np.zeros((P, NH, 1), np.float32)
    conv = i["L0_attn_conv_w"].reshape(NH, P, KC).transpose(1, 0, 2)
    cv = np.concatenate([conv, col(i["L0_attn_conv_b"]), col(i["L0_attn_D_vec"]), col(i["L0_attn_bd"]), zero], 2)

    pk, first = [], 0
    We, be = i["L1_ffn_We"], i["L1_ffn_be"]
    for c in range(NODES):
        n = min(c + 1, 5)
        eq, ek, ev = first + n - 1, first, first + n // 2
        first += n
        pk.append(np.concatenate([
            We[eq], dims_first(i["L1_ffn_Wq"][c], HU), We[ek].T, dims_first(i["L1_ffn_Wk"][c], HU), We[ev].T,
            i["L1_ffn_Wv"][c], i["L1_ffn_Wo"][c], be[eq][:, None], be[ek][:, None], be[ev][:, None],
            rows(i["L1_ffn_ew"][c]), rows(i["L1_ffn_act_w"][c:c + 1])], 1))

    arrays = {
        "x": i["L0_attn_x"], "cv": cv, "gb": np.stack([i["L0_attn_ln_gamma"], i["L0_attn_ln_beta"]], 1),
        "alog": np.tile(i["L0_attn_A_log"], NB)[:, None], "w_in": i["L0_attn_W_in"], "wd": blocks(i["L0_attn_Wd"]),
        "w_out": blocks(i["L0_attn_W_out"]), "bmt": blocks(i["L0_attn_B_mat"].T), "cmt": i["L0_attn_C_mat"].T,
        "rw": i["L0_ffn_router_w"], "rb": rows(i["L0_ffn_router_b"]),
        "xw": i["L0_ffn_expert_w"].transpose(1, 0, 2).reshape(D, NE * D), "xb": i["L0_ffn_expert_b"],
        "wckq": wckq, "wcv": i["L1_attn_w_V"],
        "lng": rows(i["L1_ffn_ln_g"]), "lnb": rows(i["L1_ffn_ln_b"]), "pk": np.stack(pk),
    }
    arrays = {k: np.ascontiguousarray(v) for k, v in arrays.items()}
    nc = bacc.Bacc("TRN2", target_bir_lowering=False, num_devices=1)
    a = {k: nc.dram_tensor("in_" + k, v.shape, F32, kind="ExternalInput").ap() for k, v in arrays.items()}
    a["out"] = nc.dram_tensor("out_x", (NB, L, D), F32, kind="ExternalOutput").ap()
    build(nc, a)
    r = run_bass_kernel_spmd(nc, [{"in_" + k: v for k, v in arrays.items()}], core_ids=[0])
    return r.results[0]["out_x"]
```
